# Optimizing a Trainium2 kernel written in Bass

```python
import numpy as np
import jax
import jax.numpy as jnp

def _softmax(x, axis=-1):
    return jax.nn.softmax(x, axis=axis)

def _gelu(x):
    return jax.nn.gelu(x, approximate=True)

def _silu(x):
    return jax.nn.silu(x)

def _sigmoid(x):
    return jax.nn.sigmoid(x)

def _layernorm(x, axis=-1, eps=1e-05):
    m = jnp.mean(x, axis=axis, keepdims=True)
    v = jnp.var(x, axis=axis, keepdims=True)
    return (x - m) / jnp.sqrt(v + eps)

def _scatter_add(tgt, idx, src, axis=0):
    return tgt.at[idx].add(src)

def _segment_sum(src, seg, n):
    return jax.ops.segment_sum(src, seg, n)
kernel_name = 'mk_xattn_seq_d2_seqx_r4_2b42ea'

def setup_inputs(seed: int=0):
    np.random.seed(seed)
    _w = jnp.asarray

    def _rec_inputs():
        import jax
        import jax.numpy as jnp
        _rk = jax.random.key(seed)
        x = -0.0002928 + 1 * jax.random.normal(jax.random.fold_in(_rk, 1), (16, 256, 512), jnp.float32)
        _lenS = 256 - jax.random.randint(jax.random.fold_in(_rk, 7), (16,), 0, max(1, 256 // 4) + 1, jnp.int32)
        _lenS2 = 256 - jax.random.randint(jax.random.fold_in(_rk, 8), (16,), 0, max(1, 256 // 4) + 1, jnp.int32)
        _ctx_2048P = jax.random.normal(jax.random.fold_in(_rk, 11), (16, 16, 512), jnp.float32)
        _ctx_2048c = jax.random.dirichlet(jax.random.fold_in(_rk, 511), 0.3 * jnp.ones((16,), jnp.float32), (16, 256))
        _ctx_2048t = jnp.einsum('bsk,bkd->bsd', _ctx_2048c, _ctx_2048P)
        _ctx_2048t = _ctx_2048t * jax.lax.rsqrt(jnp.mean(jnp.square(_ctx_2048t)) + 1e-12) * 0.953939
        ctx_2048 = 0.000189249 + 0.0999589 * (_ctx_2048t + 0.3 * jax.random.normal(jax.random.fold_in(_rk, 611), (16, 256, 512), jnp.float32))
        _validS = jnp.arange(256)[None, :] < _lenS[:, None]
        _validS2 = jnp.arange(256)[None, :] < _lenS2[:, None]
        _causal = jnp.tril(jnp.ones((256, 256), dtype=bool))
        mask_BxS2_bf1 = jnp.ones((16, 256), dtype=bool)
        return (x, ctx_2048, mask_BxS2_bf1)
    x, ctx_2048, mask_BxS2_bf1 = _rec_inputs()

    def _L0_xattn_setup():
        import jax, jax.numpy as jnp
        import numpy as np
        B, L, E, H = (4, 128, 512, 32)
        S = E // H
        EXTRA_MAA, EXTRA_DECAY = (32, 64)
        EPS = 1e-05

        def _ln(x, w, b):
            m = jnp.mean(x, axis=-1, keepdims=True)
            v = jnp.mean((x - m) ** 2, axis=-1, keepdims=True)
            return (x - m) * jax.lax.rsqrt(v + EPS) * w + b

        def _token_shift(xn, prev_row):
            first = (prev_row - xn[:, 0])[:, None]
            rest = xn[:, :-1] - xn[:, 1:]
            return jnp.concatenate([first, rest], axis=1)
        key = jax.random.key(seed)
        ks = jax.random.split(key, 24)
        rn = lambda k, shp, s=1.0: jax.random.normal(k, shp, dtype=jnp.float32) * s
        return dict(x=rn(ks[0], (B, L, E)), state=rn(ks[1], (B, 2 + S, E), 0.1), ln1_w=jnp.ones((E,), jnp.float32), ln1_b=jnp.zeros((E,), jnp.float32), ln2_w=jnp.ones((E,), jnp.float32), ln2_b=jnp.zeros((E,), jnp.float32), maa_x=rn(ks[2], (E,), 0.02), maa_w1=rn(ks[3], (E, 5 * EXTRA_MAA), 0.02), maa_w2=rn(ks[4], (5, EXTRA_MAA, E), 0.02), maa_stack=rn(ks[5], (5, E), 0.02), time_decay=rn(ks[6], (E,), 0.5), decay_w1=rn(ks[7], (E, EXTRA_DECAY), 0.02), decay_w2=rn(ks[8], (EXTRA_DECAY, E), 0.02), faaaa=rn(ks[9], (H, S), 0.1), Wr=rn(ks[10], (E, E), 0.02), Wk=rn(ks[11], (E, E), 0.02), Wv=rn(ks[12], (E, E), 0.02), Wg=rn(ks[13], (E, E), 0.02), Wo=rn(ks[14], (E, E), 0.02), gn_w=jnp.ones((E,), jnp.float32), gn_b=jnp.zeros((E,), jnp.float32), ffn_maa_k=rn(ks[15], (E,), 0.02), ffn_maa_r=rn(ks[16], (E,), 0.02), ffn_Wk=rn(ks[17], (E, E), 0.02), ffn_Wr=rn(ks[18], (E, E), 0.02), ffn_Wv=rn(ks[19], (E, E), 0.02), i=0)
    _L0_xattn_all = _L0_xattn_setup()
    _L0_xattn_in = {k: v for k, v in _L0_xattn_all.items() if k in ('ln1_w', 'ln1_b', 'ln2_w', 'ln2_b', 'maa_x', 'maa_w1', 'maa_w2', 'maa_stack', 'time_decay', 'decay_w1', 'decay_w2', 'faaaa', 'Wr', 'Wk', 'Wv', 'Wg', 'Wo', 'gn_w', 'gn_b', 'ffn_maa_k', 'ffn_maa_r', 'ffn_Wk', 'ffn_Wr', 'ffn_Wv')}
    del _L0_xattn_all

    def _L1_xattn_setup():
        import jax, jax.numpy as jnp
        import numpy as np
        D = 512
        H = 16
        HD = D // H
        INNER = 4 * D
        EPS = 1e-05

        def layer_norm(x, w, b):
            mu = jnp.mean(x, axis=-1, keepdims=True)
            var = jnp.mean(jnp.square(x - mu), axis=-1, keepdims=True)
            return (x - mu) * jax.lax.rsqrt(var + EPS) * w + b
        key = jax.random.key(seed)
        ks = jax.random.split(key, 12)
        B, LQ, LK = (4, 256, 512)
        std = 0.02
        inp = {'hidden_states': jax.random.normal(ks[0], (B, LQ, D), jnp.float32), 'encoder_hidden_states': jax.random.normal(ks[1], (B, LK, D), jnp.float32), 'encoder_attention_mask': jnp.ones((B, LK), dtype=bool), 'ln1_w': jnp.ones((D,), jnp.float32), 'ln1_b': jnp.zeros((D,), jnp.float32), 'q_w': jax.random.normal(ks[2], (D, D), jnp.float32) * std, 'q_b': jnp.zeros((D,), jnp.float32), 'k_w': jax.random.normal(ks[3], (D, D), jnp.float32) * std, 'k_b': jnp.zeros((D,), jnp.float32), 'v_w': jax.random.normal(ks[4], (D, D), jnp.float32) * std, 'v_b': jnp.zeros((D,), jnp.float32), 'cproj_w': jax.random.normal(ks[5], (D, D), jnp.float32) * std, 'cproj_b': jnp.zeros((D,), jnp.float32), 'ln2_w': jnp.ones((D,), jnp.float32), 'ln2_b': jnp.zeros((D,), jnp.float32), 'fc_w': jax.random.normal(ks[6], (D, INNER), jnp.float32) * std, 'fc_b': jnp.zeros((INNER,), jnp.float32), 'proj_w': jax.random.normal(ks[7], (INNER, D), jnp.float32) * std, 'proj_b': jnp.zeros((D,), jnp.float32)}
        return inp
    _L1_xattn_all = _L1_xattn_setup()
    _L1_xattn_in = {k: v for k, v in _L1_xattn_all.items() if k in ('ln1_w', 'ln1_b', 'q_w', 'q_b', 'k_w', 'k_b', 'v_w', 'v_b', 'cproj_w', 'cproj_b', 'ln2_w', 'ln2_b', 'fc_w', 'fc_b', 'proj_w', 'proj_b')}
    del _L1_xattn_all
    return {'x': x, 'ctx_2048': ctx_2048, 'mask_BxS2_bf1': mask_BxS2_bf1, 'L0_xattn_ln1_w': _L0_xattn_in['ln1_w'], 'L0_xattn_ln1_b': _L0_xattn_in['ln1_b'], 'L0_xattn_ln2_w': _L0_xattn_in['ln2_w'], 'L0_xattn_ln2_b': _L0_xattn_in['ln2_b'], 'L0_xattn_maa_x': _L0_xattn_in['maa_x'], 'L0_xattn_maa_w1': _L0_xattn_in['maa_w1'], 'L0_xattn_maa_w2': _L0_xattn_in['maa_w2'], 'L0_xattn_maa_stack': _L0_xattn_in['maa_stack'], 'L0_xattn_time_decay': _L0_xattn_in['time_decay'], 'L0_xattn_decay_w1': _L0_xattn_in['decay_w1'], 'L0_xattn_decay_w2': _L0_xattn_in['decay_w2'], 'L0_xattn_faaaa': _L0_xattn_in['faaaa'], 'L0_xattn_Wr': _L0_xattn_in['Wr'], 'L0_xattn_Wk': _L0_xattn_in['Wk'], 'L0_xattn_Wv': _L0_xattn_in['Wv'], 'L0_xattn_Wg': _L0_xattn_in['Wg'], 'L0_xattn_Wo': _L0_xattn_in['Wo'], 'L0_xattn_gn_w': _L0_xattn_in['gn_w'], 'L0_xattn_gn_b': _L0_xattn_in['gn_b'], 'L0_xattn_ffn_maa_k': _L0_xattn_in['ffn_maa_k'], 'L0_xattn_ffn_maa_r': _L0_xattn_in['ffn_maa_r'], 'L0_xattn_ffn_Wk': _L0_xattn_in['ffn_Wk'], 'L0_xattn_ffn_Wr': _L0_xattn_in['ffn_Wr'], 'L0_xattn_ffn_Wv': _L0_xattn_in['ffn_Wv'], 'L1_xattn_ln1_w': _L1_xattn_in['ln1_w'], 'L1_xattn_ln1_b': _L1_xattn_in['ln1_b'], 'L1_xattn_q_w': _L1_xattn_in['q_w'], 'L1_xattn_q_b': _L1_xattn_in['q_b'], 'L1_xattn_k_w': _L1_xattn_in['k_w'], 'L1_xattn_k_b': _L1_xattn_in['k_b'], 'L1_xattn_v_w': _L1_xattn_in['v_w'], 'L1_xattn_v_b': _L1_xattn_in['v_b'], 'L1_xattn_cproj_w': _L1_xattn_in['cproj_w'], 'L1_xattn_cproj_b': _L1_xattn_in['cproj_b'], 'L1_xattn_ln2_w': _L1_xattn_in['ln2_w'], 'L1_xattn_ln2_b': _L1_xattn_in['ln2_b'], 'L1_xattn_fc_w': _L1_xattn_in['fc_w'], 'L1_xattn_fc_b': _L1_xattn_in['fc_b'], 'L1_xattn_proj_w': _L1_xattn_in['proj_w'], 'L1_xattn_proj_b': _L1_xattn_in['proj_b']}

def reference(x, ctx_2048, mask_BxS2_bf1, L0_xattn_ln1_w, L0_xattn_ln1_b, L0_xattn_ln2_w, L0_xattn_ln2_b, L0_xattn_maa_x, L0_xattn_maa_w1, L0_xattn_maa_w2, L0_xattn_maa_stack, L0_xattn_time_decay, L0_xattn_decay_w1, L0_xattn_decay_w2, L0_xattn_faaaa, L0_xattn_Wr, L0_xattn_Wk, L0_xattn_Wv, L0_xattn_Wg, L0_xattn_Wo, L0_xattn_gn_w, L0_xattn_gn_b, L0_xattn_ffn_maa_k, L0_xattn_ffn_maa_r, L0_xattn_ffn_Wk, L0_xattn_ffn_Wr, L0_xattn_ffn_Wv, L1_xattn_ln1_w, L1_xattn_ln1_b, L1_xattn_q_w, L1_xattn_q_b, L1_xattn_k_w, L1_xattn_k_b, L1_xattn_v_w, L1_xattn_v_b, L1_xattn_cproj_w, L1_xattn_cproj_b, L1_xattn_ln2_w, L1_xattn_ln2_b, L1_xattn_fc_w, L1_xattn_fc_b, L1_xattn_proj_w, L1_xattn_proj_b):
    import jax
    import jax.numpy as jnp

    def _L0_xattn_ref(x, state, ln1_w, ln1_b, ln2_w, ln2_b, maa_x, maa_w1, maa_w2, maa_stack, time_decay, decay_w1, decay_w2, faaaa, Wr, Wk, Wv, Wg, Wo, gn_w, gn_b, ffn_maa_k, ffn_maa_r, ffn_Wk, ffn_Wr, ffn_Wv, i):
        import jax, jax.numpy as jnp
        import numpy as np
        B, L, E, H = (4, 128, 512, 32)
        S = E // H
        EXTRA_MAA, EXTRA_DECAY = (32, 64)
        EPS = 1e-05

        def _ln(x, w, b):
            m = jnp.mean(x, axis=-1, keepdims=True)
            v = jnp.mean((x - m) ** 2, axis=-1, keepdims=True)
            return (x - m) * jax.lax.rsqrt(v + EPS) * w + b

        def _token_shift(xn, prev_row):
            first = (prev_row - xn[:, 0])[:, None]
            rest = xn[:, :-1] - xn[:, 1:]
            return jnp.concatenate([first, rest], axis=1)
        b, l = (x.shape[0], x.shape[1])
        i0 = (2 + S) * i + 0
        i1 = (2 + S) * i + 1
        xn = _ln(x, ln1_w, ln1_b)
        sx = _token_shift(xn, state[:, i1])
        xxx = jnp.tanh((xn + sx * maa_x) @ maa_w1).reshape(b, l, 5, 1, EXTRA_MAA)
        xxx = jnp.matmul(xxx, maa_w2).reshape(b, l, 5, E)
        x5 = xn[:, :, None] + sx[:, :, None] * (maa_stack + xxx)
        w = jnp.exp(-jnp.exp(time_decay + jnp.tanh(x5[:, :, 1] @ decay_w1) @ decay_w2))
        w = w.reshape(b, l, H, S)
        r = (x5[:, :, 3] @ Wr.T).reshape(b, l, H, S)
        k = (x5[:, :, 0] @ Wk.T).reshape(b, l, H, S)
        v = (x5[:, :, 2] @ Wv.T).reshape(b, l, H, S)
        g = jax.nn.silu(x5[:, :, 4] @ Wg.T)
        s0 = state[:, (2 + S) * i + 2:(2 + S) * (i + 1)].reshape(b, H, S, S)
        u = faaaa[None, :, :, None]

        def step(s, rkvw):
            r_t, k_t, v_t, w_t = rkvw
            a = k_t[:, :, :, None] * v_t[:, :, None, :]
            out = jnp.einsum('bhk,bhkd->bhd', r_t, u * a + s)
            return (a + w_t[:, :, :, None] * s, out)
        xs = tuple((jnp.moveaxis(t, 1, 0) for t in (r, k, v, w)))
        _, outs = jax.lax.scan(step, s0, xs)
        att = jnp.moveaxis(outs, 0, 1).reshape(b, l, E)
        a4 = att.reshape(b, l, H, S)
        m = jnp.mean(a4, axis=-1, keepdims=True)
        var = jnp.mean((a4 - m) ** 2, axis=-1, keepdims=True)
        att = ((a4 - m) * jax.lax.rsqrt(var + EPS)).reshape(b, l, E) * gn_w + gn_b
        x = x + att * g @ Wo.T
        xn2 = _ln(x, ln2_w, ln2_b)
        sx2 = _token_shift(xn2, state[:, i0])
        xk = xn2 + sx2 * ffn_maa_k
        xr = xn2 + sx2 * ffn_maa_r
        rr = jax.nn.sigmoid(xr @ ffn_Wr.T)
        kk = jnp.square(jax.nn.relu(xk @ ffn_Wk.T))
        x = x + rr * (kk @ ffn_Wv.T)
        return x

    def _L1_xattn_ref(hidden_states, encoder_hidden_states, encoder_attention_mask, ln1_w, ln1_b, q_w, q_b, k_w, k_b, v_w, v_b, cproj_w, cproj_b, ln2_w, ln2_b, fc_w, fc_b, proj_w, proj_b):
        import jax, jax.numpy as jnp
        import numpy as np
        D = 512
        H = 16
        HD = D // H
        INNER = 4 * D
        EPS = 1e-05

        def layer_norm(x, w, b):
            mu = jnp.mean(x, axis=-1, keepdims=True)
            var = jnp.mean(jnp.square(x - mu), axis=-1, keepdims=True)
            return (x - mu) * jax.lax.rsqrt(var + EPS) * w + b
        B, LQ, _ = hidden_states.shape
        LK = encoder_hidden_states.shape[1]
        residual = hidden_states
        x = layer_norm(hidden_states, ln1_w, ln1_b)
        q = (x @ q_w + q_b).reshape(B, LQ, H, HD).transpose(0, 2, 1, 3)
        k = (encoder_hidden_states @ k_w + k_b).reshape(B, LK, H, HD).transpose(0, 2, 1, 3)
        v = (encoder_hidden_states @ v_w + v_b).reshape(B, LK, H, HD).transpose(0, 2, 1, 3)
        scale = 1.0 / np.sqrt(HD).astype(np.float32)
        scores = jnp.einsum('bhqd,bhkd->bhqk', q, k) * scale
        mask = encoder_attention_mask[:, None, None, :]
        mask_value = jnp.finfo(scores.dtype).min
        scores = jnp.where(mask, scores, mask_value)
        attn = jax.nn.softmax(scores, axis=-1)
        out = jnp.einsum('bhqk,bhkd->bhqd', attn, v)
        out = out.transpose(0, 2, 1, 3).reshape(B, LQ, D)
        out = out @ cproj_w + cproj_b
        hidden = out + residual
        residual = hidden
        y = layer_norm(hidden, ln2_w, ln2_b)
        y = jax.nn.gelu(y @ fc_w + fc_b, approximate=True)
        y = y @ proj_w + proj_b
        return residual + y
    x = _L0_xattn_ref(x, ctx_2048, L0_xattn_ln1_w, L0_xattn_ln1_b, L0_xattn_ln2_w, L0_xattn_ln2_b, L0_xattn_maa_x, L0_xattn_maa_w1, L0_xattn_maa_w2, L0_xattn_maa_stack, L0_xattn_time_decay, L0_xattn_decay_w1, L0_xattn_decay_w2, L0_xattn_faaaa, L0_xattn_Wr, L0_xattn_Wk, L0_xattn_Wv, L0_xattn_Wg, L0_xattn_Wo, L0_xattn_gn_w, L0_xattn_gn_b, L0_xattn_ffn_maa_k, L0_xattn_ffn_maa_r, L0_xattn_ffn_Wk, L0_xattn_ffn_Wr, L0_xattn_ffn_Wv, 0)
    x = _L1_xattn_ref(x, ctx_2048, mask_BxS2_bf1, L1_xattn_ln1_w, L1_xattn_ln1_b, L1_xattn_q_w, L1_xattn_q_b, L1_xattn_k_w, L1_xattn_k_b, L1_xattn_v_w, L1_xattn_v_b, L1_xattn_cproj_w, L1_xattn_cproj_b, L1_xattn_ln2_w, L1_xattn_ln2_b, L1_xattn_fc_w, L1_xattn_fc_b, L1_xattn_proj_w, L1_xattn_proj_b)
    return x

_drawn_inputs = setup_inputs


def setup_inputs(seed=0):
    import zlib

    import numpy as np

    out = dict(_drawn_inputs(seed))
    spreads = {'L0_xattn_ln1_w': (1.0, 0.2),
     'L0_xattn_ln1_b': (0.0, 0.1),
     'L0_xattn_ln2_w': (1.0, 0.6),
     'L0_xattn_ln2_b': (0.0, 0.8),
     'L0_xattn_gn_w': (1.0, 0.6),
     'L0_xattn_gn_b': (0.0, 0.685),
     'L1_xattn_ln1_w': (1.0, 0.6),
     'L1_xattn_ln1_b': (0.0, 0.8),
     'L1_xattn_q_b': (0.0, 0.8),
     'L1_xattn_k_b': (0.0, 0.8),
     'L1_xattn_v_b': (0.0, 0.1),
     'L1_xattn_cproj_b': (0.0, 0.1),
     'L1_xattn_ln2_w': (1.0, 0.2),
     'L1_xattn_ln2_b': (0.0, 0.336),
     'L1_xattn_fc_b': (0.0, 0.1),
     'L1_xattn_proj_b': (0.0, 0.1)}
    factors = {'ctx_2048': 4.719,
     'L0_xattn_maa_x': 8.0,
     'L0_xattn_maa_w1': 2.922,
     'L0_xattn_maa_w2': 2.925,
     'L0_xattn_maa_stack': 6.416,
     'L0_xattn_decay_w1': 8.0,
     'L0_xattn_decay_w2': 8.0,
     'L0_xattn_faaaa': 2.998,
     'L0_xattn_ffn_maa_k': 8.0,
     'L0_xattn_ffn_maa_r': 8.0,
     'L0_xattn_ffn_Wr': 4.177,
     'L1_xattn_q_w': 8.0,
     'L1_xattn_k_w': 8.0,
     'L1_xattn_v_w': 5.571}
    for name, (base, spread) in spreads.items():
        noise = np.random.default_rng([zlib.crc32(name.encode()), seed]).standard_normal(out[name].shape)
        drawn = base * np.exp(spread * noise) if base else spread * noise
        out[name] = jnp.asarray(drawn.astype(out[name].dtype))
    for name, factor in factors.items():
        out[name] = (out[name] * factor).astype(out[name].dtype)
    return out
```

```python
from contextlib import ExitStack

import concourse.bass as bass
from concourse import mybir

F32 = mybir.dt.float32
F32R = mybir.dt.float32r
U8 = mybir.dt.uint8
ALU = mybir.AluOpType
ACT = mybir.ActivationFunctionType

B, T, E = 16, 256, 512
EC = E // 128
TJ = T // 128
S = 16
MAA, NG, DEC = 32, 5, 64
AH, HD = 16, 32
INNER = 4 * E
FC = INNER // 128
EPS = 1e-5
SCALE = HD ** -0.5
MASKED = -3.4028234663852886e38
GK, GW, GV, GR, GG = range(NG)

VA = ["ln1_w", "ln1_b", "maa_x", "maa_k", "maa_w", "maa_v", "maa_r", "maa_g", "time_decay", "bonus",
      "gn_w", "gn_b", "ln2_w", "ln2_b", "ffn_maa_k", "ffn_maa_r"]
VB = ["ln1_w", "ln1_b", "q_b", "k_b", "ln2_w", "ln2_b"]


def alone(eng, sem):
    eng.sem_inc(sem, 1)


class Steps:

    def __init__(self, sem, names):
        self.sem, self.names, self.per = sem, names, len(names)

    def count(self, b, name):
        return b * self.per + self.names.index(name) + 1

    def after(self, eng, b, name):
        eng.wait_ge(self.sem, self.count(b, name))

    def before(self, eng, b, name):
        if not (isinstance(b, int) and b == 0):
            eng.wait_ge(self.sem, self.count(b - 1, name))


def build(nc, x, prev1, prev2, s0, ctxt, mask, vec_a, w_a, maa1, maa2, maa2b, dec1, dec2,
          vec_b, w_b, fc_b, rows_b, ident, blocks, sel_in, sel_out, scratch, out):
    ctx = ExitStack()
    with ctx:
        def sem(name):
            return ctx.enter_context(nc.semaphore(name))

        def steps(name, names):
            return Steps(sem(name), names)

        def sb(c, name, shape, dt=F32):
            return c.enter_context(nc.sbuf_tensor(name, shape, dt))

        W = sb(ctx, "W", [128, 8, EC, E])
        idn = sb(ctx, "idn", [128, 128])
        small = sb(ctx, "small", [128, 24])
        banks = [ctx.enter_context(nc.psum_tensor(f"bank{i}", [128, 512], F32)) for i in range(8)]

        ca = ctx.enter_context(ExitStack())
        va = sb(ca, "va", [128, len(VA), EC])
        half_gn = sb(ca, "half_gn", [128, 2, EC])
        m1 = sb(ca, "m1", [128, EC, NG * MAA])
        m2 = sb(ca, "m2", [128, E])
        m2b = sb(ca, "m2b", [MAA, E])
        d1 = sb(ca, "d1", [128, EC, DEC])
        d2 = sb(ca, "d2", [DEC, E])
        blk = sb(ca, "blk", [128, 3, 128])
        seli = sb(ca, "seli", [128, S, 128], F32R)
        selo = sb(ca, "selo", [128, S, 128])
        mhalf = sb(ca, "mhalf", [128, TJ])
        x_t = sb(ca, "x_t", [128, TJ, E])
        stat = sb(ca, "stat", [128, TJ, 6])
        mv = sb(ca, "mv", [128, TJ, 2])
        ve = sb(ca, "ve", [128, TJ])
        rstd = sb(ca, "rstd", [128, TJ])
        pr1 = sb(ca, "pr1", [128, EC])
        xn = sb(ca, "xn", [128, EC, T + 1])
        sx = sb(ca, "sx", [128, EC, T])
        h1 = sb(ca, "h1", [128, T])
        h2 = sb(ca, "h2", [MAA, T])
        x5 = sb(ca, "x5", [128, NG, EC, T])
        xx = x5[:, 0]
        seli32 = x5[:, 0:2].rearrange("p g c (h t) -> p (g c h) t", h=2)
        dh = sb(ca, "dh", [DEC, T])
        ez = sb(ca, "ez", [128, T])
        w_ = sb(ca, "w_", [128, EC, T])
        k_ = sb(ca, "k_", [128, EC, T])
        r_ = sb(ca, "r_", [128, EC, T])
        v_ = sb(ca, "v_", [128, EC, T])
        vhi = sb(ca, "vhi", [128, EC, T], F32R)
        vlo = sb(ca, "vlo", [128, EC, T], F32R)
        th = sb(ca, "th", [128, 2, T])
        g2 = sb(ca, "g2", [128, EC, T])
        s0t = sb(ca, "s0t", [128, EC, S])
        ru = sb(ca, "ru", [128, T])
        zv = sb(ca, "zv", [128, T])
        kv = sb(ca, "kv", [128, 2, 2, T])
        st = sb(ca, "st", [128, 2, 2, T + 1])
        rs = sb(ca, "rs", [128, 2, 2, T])
        att = sb(ca, "att", [128, EC, T])
        sq = sb(ca, "sq", [128, EC, T])
        x1 = sb(ca, "x1", [128, TJ, E])
        stat2 = sb(ca, "stat2", [128, TJ, 6])
        mv2 = sb(ca, "mv2", [128, TJ, 2])
        ve2 = sb(ca, "ve2", [128, TJ])
        rstd2 = sb(ca, "rstd2", [128, TJ])
        pr2 = sb(ca, "pr2", [128, EC])
        xl = sb(ca, "xl", [128, TJ, E])
        xn2 = sb(ca, "xn2", [128, EC, T + 1])
        sx2 = xl[:, :, :].rearrange("p j (a t) -> p (j a) t", a=2)
        xk = sb(ca, "xk", [128, EC, T])
        xr = sb(ca, "xr", [128, EC, T])
        kk = sb(ca, "kk", [128, EC, T])
        tr = xk[:, :, :].rearrange("p (j a) t -> p j (a t)", a=2)

        def vcol(name, c):
            return va[:, VA.index(name), c:c + 1]

        WR, WK, WV, WG, WO, FWK, FWR, FWV = range(8)

        weights_in = sem("weights_in")
        const_ready = sem("const_ready")
        passed = sem("passed")
        x_in = sem("x_in")
        s0_in = sem("s0_in")
        x1_in = sem("x1_in")
        saved = sem("saved")
        halves = ["a", "b"]
        cs = range(EC)
        X_PE = steps("X_PE", ["turn_a", "turn_b", "hid"] + [f"mix{g}{h}" for g in range(NG) for h in halves])
        X_ACT = steps("X_ACT", [f"xn{c}" for c in cs] + ["h1", "h2"])
        X_DVE = steps("X_DVE", ["stat", "mean", "norm", "prev", "shift"] + [f"xx{c}" for c in cs]
                      + [f"mix{g}{c}" for g in range(NG) for c in cs])
        X_POOL = steps("X_POOL", ["eps", "rstd"] + [f"x5{g}{h}" for g in range(NG) for h in halves])
        P_PE = steps("P_PE", ["dh"] + [f"{n}{c}" for c in cs for n in ("zk", "vr")])
        P_ACT = steps("P_ACT", ["dh"] + [f"{n}{c}" for c in cs for n in ("ez", "w", "k", "v", "vhi", "r")])
        P_DVE = steps("P_DVE", [f"vlo{c}" for c in cs])
        G_PE = steps("G_PE", ["ga", "gb"])
        G_ACT = steps("G_ACT", ["tha", "thb"])
        G_DVE = steps("G_DVE", ["ga", "gb"])
        qs = range(S // 2)
        S_PE = steps("S_PE", [n for c in cs for n in [f"z{c}"] + [f"v{c}{q}" for q in qs] + [f"o{c}{q}" for q in qs]])
        S_PE.names = [n for c in cs for n in [f"v{c}0", f"v{c}1", f"z{c}"]
                      + [m for q in qs for m in [f"o{c}{q}"] + ([f"v{c}{q + 2}"] if q + 2 < S // 2 else [])]]
        S_DVE = steps("S_DVE", [n for c in cs for n in [f"ru{c}", f"kv{c}0", f"zv{c}"]
                                + [m for q in qs for m in ([f"kv{c}{q}"] if q else []) + [f"scan{c}{q}"]]])
        S_POOL = steps("S_POOL", [n for c in cs for q in qs for n in (f"s0{c}{q}", f"rs{c}{q}")])
        S_ACT = steps("S_ACT", [n for c in cs for n in (f"att{c}", f"sq{c}")])
        N_PE = steps("N_PE", [f"var{h}" for h in halves])
        N_ACT = steps("N_ACT", [f"sd{h}" for h in halves])
        N_DVE = steps("N_DVE", ["rstd", "norm", "affine", "gate"])
        K_PE = steps("K_PE", ["wo0", "wo1", "turn_a", "turn_b"] + [f"fk{h}" for h in halves]
                     + ["fr0", "fr1", "fv0", "fv1"])
        K_ACT = steps("K_ACT", [f"xn{c}" for c in cs] + [f"{n}{h}" for h in halves for n in ("relu", "kk")]
                      + ["th0", "th1"])
        K_DVE = steps("K_DVE", ["x10", "x11", "stat", "mean", "norm", "prev", "shift", "xk", "xr"]
                      + [f"{n}{j}" for j in range(TJ) for n in ("rv", "out")])
        K_POOL = steps("K_POOL", ["eps", "rstd"])

        XB, PB, KB, VBK, AB = banks[0:2], banks[2:4], banks[4], banks[5:7], banks[7]


        def sp_x(sp, b):
            X_DVE.before(sp, b, "prev")
            X_PE.before(sp, b, "turn_b")
            sp.dma_start(x_t[:, :, :], x[b].rearrange("(j p) e -> p j e", p=128)).then_inc(x_in, 16)
            sp.dma_start(pr1[:, :], prev1[b]).then_inc(x_in, 16)

        def sp_s0(sp, b):
            S_POOL.before(sp, b, f"s0{EC - 1}{S // 2 - 1}")
            S_DVE.before(sp, b, f"scan{EC - 1}{S // 2 - 1}")
            sp.dma_start(s0t[:, :, :], s0[b].rearrange("p (c d) -> p c d", c=EC)).then_inc(s0_in, 16)

        def sp_x1(sp, b):
            K_DVE.before(sp, b, "out1")
            sp.dma_start(x1[:, :, :], x[b].rearrange("(j p) e -> p j e", p=128)).then_inc(x1_in, 16)
            sp.dma_start(pr2[:, :], prev2[b]).then_inc(x1_in, 16)

        def sp_save(sp, b):
            K_DVE.after(sp, b, "out1")
            sp.dma_start(scratch[b].rearrange("(j p) e -> p j e", p=128), tr[:, :, :]).then_inc(saved, 16)

        def x_pe1(pe, b):
            X_DVE.after(pe, b, "norm")
            for h in range(2):
                if h == 0:
                    X_DVE.before(pe, b, f"mix{NG - 1}1")
                else:
                    X_DVE.before(pe, b, f"mix{NG - 1}3")
                for c in (2 * h, 2 * h + 1):
                    for j in range(TJ):
                        o = (c % 2) * T + j * 128
                        last = pe.transpose(XB[h][:, o:o + 128], x_t[:, j, c * 128:(c + 1) * 128], idn[:, :])
                last.then_inc(X_PE.sem, 1)
            X_DVE.after(pe, b, "xx3")
            X_ACT.after(pe, b, "xn1")
            for m, (o, n) in enumerate(((0, 128), (T, MAA))):
                for c in cs:
                    last = pe.matmul(XB[0][0:n, o:o + T], m1[:, c, 128 * m:128 * m + n], xx[:, c, :],
                                     start=(c == 0), stop=(c == EC - 1))
            last.then_inc(X_PE.sem, 1)

        def x_pe2(pe, b):
            X_ACT.after(pe, b, "h2")
            for g in range(NG):
                for h in range(2):
                    if g:
                        X_DVE.after(pe, b, f"mix{g - 1}{2 * h + 1}")
                    for c in (2 * h, 2 * h + 1):
                        wt = m2[MAA * g:MAA * (g + 1), c * 128:(c + 1) * 128] if g < 4 else m2b[:, c * 128:(c + 1) * 128]
                        hid = h1[MAA * g:MAA * (g + 1), :] if g < 4 else h2[:, :]
                        last = pe.matmul(XB[h][:, (c % 2) * T:(c % 2 + 1) * T], wt, hid, start=True, stop=True)
                    last.then_inc(X_PE.sem, 1)

        def x_act1(act, b):
            X_DVE.before(act, b, "shift")
            X_POOL.before(act, b, f"x5{NG - 1}b")
            for c in cs:
                X_PE.after(act, b, "turn_a" if c < 2 else "turn_b")
                act.activation(xn[:, c, 1:T + 1], XB[c // 2][:, (c % 2) * T:(c % 2 + 1) * T], ACT.Identity,
                               bias=vcol("ln1_b", c), scale=vcol("ln1_w", c)).then_inc(X_ACT.sem, 1)
            X_PE.before(act, b, f"mix{NG - 1}b")
            X_PE.after(act, b, "hid")
            act.activation(h1[:, :], XB[0][:, 0:T], ACT.Tanh).then_inc(X_ACT.sem, 1)
            act.activation(h2[:, :], XB[0][0:MAA, T:2 * T], ACT.Tanh).then_inc(X_ACT.sem, 1)

        def x_dve1(dve, b):
            X_DVE.before(dve, b, f"mix{NG - 1}3")
            dve.wait_ge(x_in, 32 * b + 32)
            for j in range(TJ):
                last = dve.bn_stats(stat[:, j, :], x_t[:, j, :])
            last.then_inc(X_DVE.sem, 1)
            X_POOL.before(dve, b, "eps")
            X_DVE.after(dve, b, "stat")
            alone(dve, passed)
            for j in range(TJ):
                last = dve.bn_aggr(mv[:, j, :], stat[:, j, :])
            last.then_inc(X_DVE.sem, 1)
            X_POOL.after(dve, b, "rstd")
            X_DVE.after(dve, b, "mean")
            for j in range(TJ):
                last = dve.tensor_scalar(x_t[:, j, :], x_t[:, j, :], mv[:, j, 0:1], rstd[:, j:j + 1],
                                         ALU.subtract, ALU.mult)
            last.then_inc(X_DVE.sem, 1)
            X_POOL.before(dve, b, f"x5{NG - 1}b")
            dve.tensor_copy(xn[:, :, 0], pr1[:, :]).then_inc(X_DVE.sem, 1)
            X_ACT.after(dve, b, "xn3")
            X_DVE.after(dve, b, "prev")
            dve.tensor_tensor(sx[:, :, :], xn[:, :, 0:T], xn[:, :, 1:T + 1], ALU.subtract).then_inc(X_DVE.sem, 1)
            X_DVE.after(dve, b, "shift")
            P_PE.before(dve, b, f"zk{EC - 1}")
            for c in cs:
                dve.scalar_tensor_tensor(xx[:, c, :], sx[:, c, :], vcol("maa_x", c), xn[:, c, 1:T + 1],
                                         ALU.mult, ALU.add).then_inc(X_DVE.sem, 1)

        def x_dve2(dve, b):
            P_PE.before(dve, b, f"vr{EC - 1}")
            G_PE.before(dve, b, "gb")
            for g in range(NG):
                for c in cs:
                    if c % 2 == 0:
                        X_PE.after(dve, b, f"mix{g}{halves[c // 2]}")
                    dve.scalar_tensor_tensor(x5[:, g, c, :], XB[c // 2][:, (c % 2) * T:(c % 2 + 1) * T],
                                             va[:, VA.index("maa_k") + g, c:c + 1], sx[:, c, :],
                                             ALU.add, ALU.mult).then_inc(X_DVE.sem, 1)

        def x_pool1(pool, b):
            X_DVE.before(pool, b, "norm")
            X_POOL.before(pool, b, "rstd")
            X_DVE.after(pool, b, "mean")
            alone(pool, passed)
            pool.tensor_scalar(ve[:, :], mv[:, :, 1], 1.0, EPS, ALU.mult, ALU.add).then_inc(X_POOL.sem, 1)
            X_POOL.after(pool, b, "eps")
            pool.tensor_tensor(rstd[:, :], ve[:, :], mhalf[:, :], ALU.pow).then_inc(X_POOL.sem, 1)

        def x_pool2(pool, b):
            for g in range(NG):
                for h in range(2):
                    X_DVE.after(pool, b, f"mix{g}{2 * h + 1}")
                    pool.tensor_tensor(x5[:, g, 2 * h:2 * h + 2, :], x5[:, g, 2 * h:2 * h + 2, :],
                                       xn[:, 2 * h:2 * h + 2, 1:T + 1], ALU.add).then_inc(X_POOL.sem, 1)

        def project(pe, bank, half, wt, g, c):
            for i in cs:
                last = pe.matmul(bank[:, half * T:(half + 1) * T], W[:, wt, i, c * 128:(c + 1) * 128],
                                 x5[:, g, i, :], start=(i == 0), stop=(i == EC - 1))
            return last

        def p_pe(pe, b, c):
            if c == 0:
                X_POOL.after(pe, b, f"x5{NG - 1}b")
                G_DVE.before(pe, b, "ga")
                for i in cs:
                    last = pe.matmul(PB[0][0:DEC, 0:T], d1[:, i, :], x5[:, GW, i, :], start=(i == 0), stop=(i == EC - 1))
                last.then_inc(P_PE.sem, 1)
                P_ACT.after(pe, b, "dh")
            else:
                P_ACT.after(pe, b, f"k{c - 1}")
            pe.matmul(PB[0][:, T:2 * T], d2[:, c * 128:(c + 1) * 128], dh[:, :], start=True, stop=True)
            project(pe, PB[0], 0, WK, GK, c).then_inc(P_PE.sem, 1)
            if c:
                P_ACT.after(pe, b, f"r{c - 1}")
            else:
                G_DVE.before(pe, b, "gb")
            project(pe, PB[1], 0, WV, GV, c)
            project(pe, PB[1], 1, WR, GR, c).then_inc(P_PE.sem, 1)

        def p_act(act, b, c):
            if c == 0:
                P_PE.before(act, b, f"zk{EC - 1}")
                P_PE.after(act, b, "dh")
                act.activation(dh[:, :], PB[0][0:DEC, 0:T], ACT.Tanh).then_inc(P_ACT.sem, 1)
            S_DVE.before(act, b, f"scan{c}{S // 2 - 1}")
            if c:
                P_ACT.after(act, b, f"w{c - 1}")
            else:
                P_ACT.before(act, b, f"w{EC - 1}")
            P_PE.after(act, b, f"zk{c}")
            act.activation(ez[:, :], PB[0][:, T:2 * T], ACT.Exp, bias=vcol("time_decay", c)).then_inc(P_ACT.sem, 1)
            P_ACT.after(act, b, f"ez{c}")
            act.activation(w_[:, c, :], ez[:, :], ACT.Exp, scale=-1.0).then_inc(P_ACT.sem, 1)
            act.activation(k_[:, c, :], PB[0][:, 0:T], ACT.Copy).then_inc(P_ACT.sem, 1)
            P_PE.after(act, b, f"vr{c}")
            act.activation(v_[:, c, :], PB[1][:, 0:T], ACT.Copy).then_inc(P_ACT.sem, 1)
            S_PE.before(act, b, f"v{c}{S // 2 - 1}")
            P_DVE.before(act, b, f"vlo{c}")
            act.activation(vhi[:, c, :], PB[1][:, 0:T], ACT.Copy).then_inc(P_ACT.sem, 1)
            S_POOL.before(act, b, f"rs{c}{S // 2 - 1}")
            act.activation(r_[:, c, :], PB[1][:, T:2 * T], ACT.Copy).then_inc(P_ACT.sem, 1)

        def p_dve(dve, b, c):
            P_ACT.after(dve, b, f"vhi{c}")
            S_PE.before(dve, b, f"v{c}{S // 2 - 1}")
            dve.tensor_tensor(vlo[:, c, :], v_[:, c, :], vhi[:, c, :].bitcast(F32), ALU.subtract)\
               .then_inc(P_DVE.sem, 1)

        def g_pe(pe, b):
            for h in range(2):
                P_ACT.after(pe, b, f"{'kr'[h]}{EC - 1}")
                project(pe, PB[h], 0, WG, GG, 2 * h)
                project(pe, PB[h], 1, WG, GG, 2 * h + 1).then_inc(G_PE.sem, 1)

        def g_act(act, b):
            for h in range(2):
                if h:
                    G_DVE.after(act, b, "ga")
                else:
                    G_DVE.before(act, b, "gb")
                G_PE.after(act, b, f"g{halves[h]}")
                act.activation(th[:, :, :], PB[h][:, :].rearrange("p (c t) -> p c t", c=2), ACT.Tanh, scale=0.5)\
                   .then_inc(G_ACT.sem, 1)

        def g_dve(dve, b):
            N_DVE.before(dve, b, "gate")
            for h in range(2):
                G_ACT.after(dve, b, f"th{halves[h]}")
                dve.scalar_tensor_tensor(g2[:, 2 * h:2 * h + 2, :], th[:, :, :], 1.0,
                                         PB[h][:, :].rearrange("p (c t) -> p c t", c=2), ALU.add, ALU.mult)\
                   .then_inc(G_DVE.sem, 1)

        def s_values(pe, b, c, q):
            if q >= 2:
                S_DVE.after(pe, b, f"kv{c}{q - 2}")
            elif c:
                S_DVE.after(pe, b, f"kv{c - 1}{S // 2 - 2 + q}")
            else:
                S_DVE.before(pe, b, f"kv{EC - 1}{S // 2 - 2 + q}")
            for e in range(2):
                for part, v in enumerate((vhi, vlo)):
                    last = pe.matmul(VBK[q % 2][:, e * T:(e + 1) * T], seli[:, 2 * q + e, :], v[:, c, :],
                                     start=(part == 0), stop=(part == 1))
            last.then_inc(S_PE.sem, 1)

        def s_pe(pe, b, c):
            P_DVE.after(pe, b, f"vlo{c}")
            s_values(pe, b, c, 0)
            s_values(pe, b, c, 1)
            S_DVE.after(pe, b, f"ru{c}")
            if c:
                S_ACT.after(pe, b, f"sq{c - 1}")
            else:
                S_ACT.before(pe, b, f"sq{EC - 1}")
            pe.matmul(AB[:, T:2 * T], blk[:, 0, :], ru[:, :], start=True, stop=True).then_inc(S_PE.sem, 1)
            for q in qs:
                if q == 0:
                    S_DVE.after(pe, b, f"zv{c}")
                    pe.matmul(AB[:, 0:T], blk[:, 1, :], zv[:, :], start=True, stop=False)
                S_POOL.after(pe, b, f"rs{c}{q}")
                for e in range(2):
                    d = 2 * q + e
                    last = pe.matmul(AB[:, 0:T], selo[:, d, :], rs[:, q % 2, e, :],
                                     start=False, stop=(d == S - 1))
                last.then_inc(S_PE.sem, 1)
                if q + 2 < S // 2:
                    s_values(pe, b, c, q + 2)

        def s_dve(dve, b, c):
            def kv_product(q):
                S_PE.after(dve, b, f"v{c}{q}")
                if q >= 2:
                    S_DVE.after(dve, b, f"scan{c}{q - 2}")
                dve.tensor_tensor(kv[:, q % 2], VBK[q % 2][:, :].rearrange("p (e t) -> p e t", e=2),
                                  k_[:, c, :].unsqueeze(1).broadcast_to([128, 2, T]), ALU.mult)\
                   .then_inc(S_DVE.sem, 1)

            P_ACT.after(dve, b, f"r{c}")
            if c == 0:
                dve.wait_ge(s0_in, 16 * b + 16)
                S_DVE.before(dve, b, f"scan{EC - 1}{S // 2 - 1}")
                S_PE.before(dve, b, f"o{EC - 1}0")
            else:
                S_DVE.after(dve, b, f"scan{c - 1}{S // 2 - 1}")
                S_PE.after(dve, b, f"o{c - 1}0")
            dve.scalar_tensor_tensor(ru[:, :], r_[:, c, :], vcol("bonus", c), k_[:, c, :], ALU.mult, ALU.mult)\
               .then_inc(S_DVE.sem, 1)
            kv_product(0)
            S_PE.after(dve, b, f"z{c}")
            dve.tensor_tensor(zv[:, :], AB[:, T:2 * T], v_[:, c, :], ALU.mult).then_inc(S_DVE.sem, 1)
            for q in qs:
                if q:
                    kv_product(q)
                S_DVE.after(dve, b, f"kv{c}{q}")
                if q >= 2:
                    S_POOL.after(dve, b, f"rs{c}{q - 2}")
                elif c:
                    S_POOL.after(dve, b, f"rs{c - 1}{S // 2 - 2 + q}")
                else:
                    S_POOL.before(dve, b, f"rs{EC - 1}{S // 2 - 2 + q}")
                for e in range(2):
                    d = 2 * q + e
                    last = dve.tensor_tensor_scan(st[:, q % 2, e, 1:T + 1], w_[:, c, :], kv[:, q % 2, e, :],
                                                  s0t[:, c, d:d + 1], ALU.mult, ALU.add)
                last.then_inc(S_DVE.sem, 1)

        def s_pool(pool, b, c):
            if c == 0:
                pool.wait_ge(s0_in, 16 * b + 16)
                P_ACT.after(pool, b, f"r{EC - 1}")
            for q in qs:
                if q >= 2:
                    S_POOL.after(pool, b, f"rs{c}{q - 2}")
                elif c:
                    S_POOL.after(pool, b, f"rs{c - 1}{S // 2 - 2 + q}")
                else:
                    S_POOL.before(pool, b, f"rs{EC - 1}{S // 2 - 2 + q}")
                alone(pool, passed)
                pool.tensor_copy(st[:, q % 2, :, 0], s0t[:, c, 2 * q:2 * q + 2]).then_inc(S_POOL.sem, 1)
                S_POOL.after(pool, b, f"s0{c}{q}")
                S_DVE.after(pool, b, f"scan{c}{q}")
                if q >= 2:
                    S_PE.after(pool, b, f"o{c}{q - 2}")
                elif c:
                    S_PE.after(pool, b, f"o{c - 1}{S // 2 - 2 + q}")
                else:
                    S_PE.before(pool, b, f"o{EC - 1}{S // 2 - 2 + q}")
                pool.tensor_tensor(rs[:, q % 2], st[:, q % 2, :, 0:T],
                                   r_[:, c, :].unsqueeze(1).broadcast_to([128, 2, T]), ALU.mult)\
                    .then_inc(S_POOL.sem, 1)

        def s_act(act, b, c):
            if c == 0:
                K_PE.before(act, b, "wo1")
                N_DVE.before(act, b, "norm")
            S_PE.after(act, b, f"o{c}{S // 2 - 1}")
            act.activation(att[:, c, :], AB[:, 0:T], ACT.Copy).then_inc(S_ACT.sem, 1)
            act.activation(sq[:, c, :], AB[:, 0:T], ACT.Square).then_inc(S_ACT.sem, 1)

        def n_pe(pe, b):
            K_DVE.before(pe, b, "rv1")
            for h in range(2):
                if h:
                    N_ACT.after(pe, b, "sda")
                S_ACT.after(pe, b, f"sq{2 * h + 1}")
                for c in (2 * h, 2 * h + 1):
                    last = pe.matmul(KB[:, (c % 2) * T:(c % 2 + 1) * T], blk[:, 2, :], sq[:, c, :],
                                     start=True, stop=True)
                last.then_inc(N_PE.sem, 1)

        def n_act(act, b):
            for h in range(2):
                N_PE.after(act, b, f"var{halves[h]}")
                act.activation(sq[:, 2 * h:2 * h + 2, :], KB[:, :].rearrange("p (c t) -> p c t", c=2), ACT.Sqrt,
                               bias=small[:, 0:1]).then_inc(N_ACT.sem, 1)

        def n_dve(dve, b):
            N_ACT.after(dve, b, "sdb")
            dve.reciprocal(sq[:, :, :], sq[:, :, :]).then_inc(N_DVE.sem, 1)
            N_DVE.after(dve, b, "rstd")
            dve.tensor_tensor(att[:, :, :], att[:, :, :], sq[:, :, :], ALU.mult).then_inc(N_DVE.sem, 1)
            N_DVE.after(dve, b, "norm")
            for c in cs:
                last = dve.tensor_scalar(att[:, c, :], att[:, c, :], half_gn[:, 0, c:c + 1], half_gn[:, 1, c:c + 1],
                                         ALU.mult, ALU.add)
            last.then_inc(N_DVE.sem, 1)
            N_DVE.after(dve, b, "affine")
            G_DVE.after(dve, b, "gb")
            dve.tensor_tensor(att[:, :, :], att[:, :, :], g2[:, :, :], ALU.mult).then_inc(N_DVE.sem, 1)

        def k_pe1(pe, b):
            N_DVE.after(pe, b, "gate")
            for j in range(TJ):
                if j:
                    K_DVE.after(pe, b, "x10")
                else:
                    N_ACT.after(pe, b, "sdb")
                for c in cs:
                    last = pe.matmul(KB[:, :], att[:, c, j * 128:(j + 1) * 128], W[:, WO, c, :],
                                     start=(c == 0), stop=(c == EC - 1))
                last.then_inc(K_PE.sem, 1)

        def k_pe2(pe, b):
            K_DVE.after(pe, b, "norm")
            for h in range(2):
                if h:
                    K_ACT.after(pe, b, "xn1")
                for c in (2 * h, 2 * h + 1):
                    for j in range(TJ):
                        o = (c % 2) * T + j * 128
                        last = pe.transpose(KB[:, o:o + 128], xl[:, j, c * 128:(c + 1) * 128], idn[:, :])
                last.then_inc(K_PE.sem, 1)

        def k_pe3(pe, b):
            K_DVE.after(pe, b, "xk")
            K_ACT.after(pe, b, "xn3")
            for h in range(2):
                if h:
                    K_ACT.after(pe, b, "relua")
                for c in (2 * h, 2 * h + 1):
                    for i in cs:
                        last = pe.matmul(KB[:, (c % 2) * T:(c % 2 + 1) * T], W[:, FWK, i, c * 128:(c + 1) * 128],
                                         xk[:, i, :], start=(i == 0), stop=(i == EC - 1))
                last.then_inc(K_PE.sem, 1)

        def k_pe4(pe, b):
            K_DVE.after(pe, b, "xr")
            for j in range(TJ):
                K_ACT.after(pe, b, "relub" if j == 0 else "th0")
                for c in cs:
                    last = pe.matmul(KB[:, :], xr[:, c, j * 128:(j + 1) * 128], W[:, FWR, c, :],
                                     start=(c == 0), stop=(c == EC - 1))
                last.then_inc(K_PE.sem, 1)
            for j in range(TJ):
                if j == 0:
                    K_ACT.after(pe, b, "th1")
                else:
                    K_DVE.after(pe, b, "rv0")
                for c in cs:
                    last = pe.matmul(KB[:, :], kk[:, c, j * 128:(j + 1) * 128], W[:, FWV, c, :],
                                     start=(c == 0), stop=(c == EC - 1))
                last.then_inc(K_PE.sem, 1)

        def k_act1(act, b):
            K_DVE.before(act, b, "xr")
            for c in cs:
                K_PE.after(act, b, "turn_a" if c < 2 else "turn_b")
                act.activation(xn2[:, c, 1:T + 1], KB[:, (c % 2) * T:(c % 2 + 1) * T], ACT.Identity,
                               bias=vcol("ln2_b", c), scale=vcol("ln2_w", c)).then_inc(K_ACT.sem, 1)

        def k_act2(act, b):
            K_PE.before(act, b, "fv1")
            for h in range(2):
                kh = kk[:, 2 * h:2 * h + 2, :]
                K_PE.after(act, b, f"fk{halves[h]}")
                act.activation(kh, KB[:, :].rearrange("p (c t) -> p c t", c=2), ACT.Relu).then_inc(K_ACT.sem, 1)
                K_ACT.after(act, b, f"relu{halves[h]}")
                act.activation(kh, kh, ACT.Square).then_inc(K_ACT.sem, 1)

        def k_act3(act, b):
            if not (isinstance(b, int) and b == 0):
                act.wait_ge(saved, 16 * b)
            for j in range(TJ):
                K_PE.after(act, b, f"fr{j}")
                act.activation(tr[:, j, :], KB[:, :], ACT.Tanh, scale=0.5).then_inc(K_ACT.sem, 1)

        def k_dve1(dve, b):
            dve.wait_ge(x1_in, 32 * b + 32)
            for j in range(TJ):
                K_PE.after(dve, b, f"wo{j}")
                dve.tensor_tensor(x1[:, j, :], x1[:, j, :], KB[:, :], ALU.add).then_inc(K_DVE.sem, 1)
            K_DVE.after(dve, b, "x11")
            for j in range(TJ):
                last = dve.bn_stats(stat2[:, j, :], x1[:, j, :])
            last.then_inc(K_DVE.sem, 1)
            K_DVE.after(dve, b, "stat")
            alone(dve, passed)
            for j in range(TJ):
                last = dve.bn_aggr(mv2[:, j, :], stat2[:, j, :])
            last.then_inc(K_DVE.sem, 1)
            K_DVE.after(dve, b, "mean")
            K_POOL.after(dve, b, "rstd")
            for j in range(TJ):
                last = dve.tensor_scalar(xl[:, j, :], x1[:, j, :], mv2[:, j, 0:1], rstd2[:, j:j + 1],
                                         ALU.subtract, ALU.mult)
            last.then_inc(K_DVE.sem, 1)

        def k_dve2(dve, b):
            dve.tensor_copy(xn2[:, :, 0], pr2[:, :]).then_inc(K_DVE.sem, 1)
            K_DVE.after(dve, b, "prev")
            K_ACT.after(dve, b, "xn3")
            dve.tensor_tensor(sx2, xn2[:, :, 0:T], xn2[:, :, 1:T + 1], ALU.subtract).then_inc(K_DVE.sem, 1)
            K_DVE.after(dve, b, "shift")
            K_PE.before(dve, b, "fr1")
            if not (isinstance(b, int) and b == 0):
                dve.wait_ge(saved, 16 * b)
            for name, dst in (("ffn_maa_k", xk), ("ffn_maa_r", xr)):
                for c in cs:
                    last = dve.scalar_tensor_tensor(dst[:, c, :], sx2[:, c, :], vcol(name, c), xn2[:, c, 1:T + 1],
                                                    ALU.mult, ALU.add)
                last.then_inc(K_DVE.sem, 1)

        def k_dve3(dve, b):
            for j in range(TJ):
                K_ACT.after(dve, b, f"th{j}")
                K_PE.after(dve, b, f"fv{j}")
                dve.scalar_tensor_tensor(tr[:, j, :], tr[:, j, :], 1.0, KB[:, :], ALU.add, ALU.mult)\
                   .then_inc(K_DVE.sem, 1)
                K_DVE.after(dve, b, f"rv{j}")
                dve.scalar_tensor_tensor(tr[:, j, :], tr[:, j, :], 0.5, x1[:, j, :], ALU.mult, ALU.add)\
                   .then_inc(K_DVE.sem, 1)

        def k_pool(pool, b):
            K_DVE.before(pool, b, "norm")
            K_DVE.after(pool, b, "mean")
            alone(pool, passed)
            pool.tensor_scalar(ve2[:, :], mv2[:, :, 1], 1.0, EPS, ALU.mult, ALU.add).then_inc(K_POOL.sem, 1)
            K_POOL.after(pool, b, "eps")
            pool.tensor_tensor(rstd2[:, :], ve2[:, :], mhalf[:, :], ALU.pow).then_inc(K_POOL.sem, 1)

        NOTHING = {}

        def round_a(eng, p, i):
            first = isinstance(i, int) and i == 0
            last1 = isinstance(i, int) and i + 1 >= B
            last2 = isinstance(i, int) and i + 2 >= B

            def do(name, b, *more):
                if name in p:
                    p[name](eng, b, *more)

            do("s0", i)
            if not last2:
                do("x", i + 2)
            if not first:
                do("x1", i - 1)
                do("K1", i - 1)
            for c in cs:
                do("S", i, c)
                if not last1:
                    do("P", i + 1, c)
                if c < 3 and not first:
                    do(f"K{c + 2}", i - 1)
                if c == EC - 1 and not last2:
                    do("X1", i + 2)
            do("N", i)
            if not last1:
                do("G", i + 1)
            if not first:
                do("save", i - 1)
            if not last2:
                do("X2", i + 2)

        def phase_a(eng, p):
            def do(name, b, *more):
                if name in p:
                    p[name](eng, b, *more)

            do("x", 0)
            do("X1", 0)
            do("X2", 0)
            do("x", 1)
            for c in cs:
                do("P", 0, c)
            do("G", 0)
            do("X1", 1)
            do("X2", 1)
            round_a(eng, p, 0)
            round_a(eng, p, 1)
            with eng.Fori(2, B - 2) as i:
                round_a(eng, p, i)
            round_a(eng, p, B - 2)
            round_a(eng, p, B - 1)
            do("x1", B - 1)
            for c in cs:
                do(f"K{c + 1}", B - 1)
            do("save", B - 1)

        a_done = [X_PE, X_ACT, X_DVE, X_POOL, P_PE, P_ACT, P_DVE, G_PE, G_ACT, G_DVE, S_PE, S_DVE, S_POOL,
                  S_ACT, N_PE, N_ACT, N_DVE, K_PE, K_ACT, K_DVE, K_POOL]

        def end_a(eng):
            for s in a_done:
                eng.wait_ge(s.sem, B * s.per)
            eng.wait_ge(saved, 16 * B)

        ca.close()
        cb = ctx.enter_context(ExitStack())
        Wq = sb(cb, "Wq", [128, 4, EC, E])
        vb = sb(cb, "vb", [128, len(VB), EC])
        fcb = sb(cb, "fcb", [128, FC])
        rows = sb(cb, "rows", [128, 3, E])
        mhalf_b = sb(cb, "mhalf_b", [128, TJ])
        h_in = sb(cb, "h_in", [128, TJ, E])
        cx = sb(cb, "cx", [128, EC, T])
        mk8 = sb(cb, "mk8", [128, T], U8)
        mneg = sb(cb, "mneg", [128, T])
        bstat = sb(cb, "bstat", [128, TJ, 6])
        bmv = sb(cb, "bmv", [128, TJ, 2])
        bve = sb(cb, "bve", [128, TJ])
        brstd = sb(cb, "brstd", [128, TJ])
        hl = sb(cb, "hl", [128, TJ, E])
        hn = sb(cb, "hn", [128, EC, T])
        qt = sb(cb, "qt", [128, EC, T])
        kt = sb(cb, "kt", [128, EC, T])
        vt = sb(cb, "vt", [128, TJ, E])
        sc = sb(cb, "sc", [128, 2, TJ, T])
        pt = sb(cb, "pt", [128, 2, 2, T])
        mx = sb(cb, "mx", [128, 2, TJ])
        nmx = sb(cb, "nmx", [128, 2, TJ])
        den = sb(cb, "den", [128, TJ, AH])
        ao = sb(cb, "ao", [128, TJ, E])
        aot = sb(cb, "aot", [128, EC, T])
        hb = sb(cb, "hb", [128, TJ, E])
        hid = sb(cb, "hid", [128, TJ, E])
        hp = sb(cb, "hp", [128, TJ, E])
        gl = sb(cb, "gl", [128, FC, T])
        res = sb(cb, "res", [128, TJ, E])
        FCW, PRW = 0, 4

        b_in1 = sem("b_in1")
        b_in2 = sem("b_in2")
        hc_in = sem("hc_in")
        stored = sem("stored")
        b_const = sem("b_const")
        hs = range(AH)
        L_PE = steps("L_PE", ["turn_a", "turn_b", "q_a", "q_b", "k_a", "k_b", "v0", "v1"])
        L_ACT = steps("L_ACT", [f"hn{c}" for c in cs] + [f"q{c}" for c in cs] + [f"k{c}" for c in cs])
        L_DVE = steps("L_DVE", ["mask", "stat", "mean", "norm", "v0", "v1"])
        L_POOL = steps("L_POOL", ["eps", "rstd", "hb"])
        A_PE = steps("A_PE", [n for h in range(AH + 2) for n in ([f"s{h}"] if h < AH else [])
                              + ([f"t{h - 1}"] if 1 <= h <= AH else []) + ([f"o{h - 2}"] if h >= 2 else [])])
        A_ACT = steps("A_ACT", [n for h in range(AH) for n in (f"e{h}",)])
        A_DVE = steps("A_DVE", [n for h in range(AH + 1) for n in ([f"m{h}", f"n{h}"] if h < AH else [])
                                + ([f"p{h - 1}"] if h else [])])
        C_PE = steps("C_PE", ["turn_a", "turn_b", "c0", "c1", "nturn_a", "nturn_b"] + [f"f{n}" for n in range(FC // 2)]
                     + ["p0", "p1"])
        C_DVE = steps("C_DVE", ["rden", "ao", "hid0", "hid1", "stat", "mean", "norm", "out0", "out1"])
        C_ACT = steps("C_ACT", ["aot_a", "aot_b"] + [f"yn{c}" for c in cs] + [f"g{c}" for c in range(FC)])
        C_POOL = steps("C_POOL", ["eps", "rstd", "hp"])
        LB, SB, TBK, OB, CB = banks[0:2], banks[2:4], banks[4], banks[5:7], banks[7]

        FB = [CB, SB[0], SB[1], TBK]

        def bcol(name, c):
            return vb[:, VB.index(name), c:c + 1]

        def sp_hc(sp, b):
            L_DVE.before(sp, b, "norm")
            L_POOL.before(sp, b, "hb")
            L_PE.before(sp, b, "v1")
            sp.dma_start(h_in[:, :, :], scratch[b].rearrange("(j p) e -> p j e", p=128)).then_inc(hc_in, 16)
            sp.dma_start(cx[:, :, :], ctxt[b].rearrange("(c p) t -> p c t", p=128)).then_inc(hc_in, 16)
            sp.dma_start(mk8[:, :], mask[b].partition_broadcast(128)).then_inc(hc_in, 16)

        def sp_out(sp, b):
            C_DVE.after(sp, b, "out1")
            sp.dma_start(out[b].rearrange("(j p) e -> p j e", p=128), res[:, :, :]).then_inc(stored, 16)

        def l_pe(pe, b):
            L_DVE.after(pe, b, "norm")
            L_DVE.before(pe, b, "v1")
            for h in range(2):
                for c in (2 * h, 2 * h + 1):
                    for j in range(TJ):
                        o = (c % 2) * T + j * 128
                        last = pe.transpose(LB[h][:, o:o + 128], hl[:, j, c * 128:(c + 1) * 128], idn[:, :])
                last.then_inc(L_PE.sem, 1)
            for slot, src, done in ((0, hn, "hn"), (1, cx, "q")):
                for h in range(2):
                    L_ACT.after(pe, b, f"{done}3" if slot == 0 else f"{done}{2 * h + 1}")
                    for c in (2 * h, 2 * h + 1):
                        for i in cs:
                            last = pe.matmul(LB[h][:, (c % 2) * T:(c % 2 + 1) * T], Wq[:, slot, i, c * 128:(c + 1) * 128],
                                             src[:, i, :], start=(i == 0), stop=(i == EC - 1))
                    last.then_inc(L_PE.sem, 1)
            for j in range(TJ):
                L_ACT.after(pe, b, f"k{2 * j + 1}")
                for c in cs:
                    last = pe.matmul(LB[j][:, :], cx[:, c, j * 128:(j + 1) * 128], Wq[:, 2, c, :],
                                     start=(c == 0), stop=(c == EC - 1))
                last.then_inc(L_PE.sem, 1)

        def l_act(act, b):
            for name, dst, done, bias, scale in (("hn", hn, "turn", "ln1_b", "ln1_w"), ("q", qt, "q", "q_b", None),
                                                 ("k", kt, "k", "k_b", None)):
                if name == "hn":
                    L_PE.before(act, b, "q_b")
                else:
                    A_PE.before(act, b, f"s{AH - 1}")
                for c in cs:
                    L_PE.after(act, b, f"{done}_{halves[c // 2]}")
                    act.activation(dst[:, c, :], LB[c // 2][:, (c % 2) * T:(c % 2 + 1) * T], ACT.Identity,
                                   bias=bcol(bias, c), scale=bcol(scale, c) if scale else 1.0).then_inc(L_ACT.sem, 1)

        def l_dve(dve, b):
            dve.wait_ge(hc_in, 48 * b + 48)
            A_DVE.before(dve, b, f"m{AH - 1}")
            dve.tensor_scalar(mneg[:, :], mk8[:, :], 0.0, MASKED, ALU.is_equal, ALU.mult).then_inc(L_DVE.sem, 1)
            L_DVE.before(dve, b, "mean")
            for j in range(TJ):
                last = dve.bn_stats(bstat[:, j, :], h_in[:, j, :])
            last.then_inc(L_DVE.sem, 1)
            L_DVE.after(dve, b, "stat")
            L_POOL.before(dve, b, "eps")
            alone(dve, passed)
            for j in range(TJ):
                last = dve.bn_aggr(bmv[:, j, :], bstat[:, j, :])
            last.then_inc(L_DVE.sem, 1)
            L_DVE.after(dve, b, "mean")
            L_POOL.after(dve, b, "rstd")
            L_PE.before(dve, b, "turn_b")
            for j in range(TJ):
                last = dve.tensor_scalar(hl[:, j, :], h_in[:, j, :], bmv[:, j, 0:1], brstd[:, j:j + 1],
                                         ALU.subtract, ALU.mult)
            last.then_inc(L_DVE.sem, 1)
            A_PE.before(dve, b, f"o{AH - 1}")
            for j in range(TJ):
                L_PE.after(dve, b, f"v{j}")
                dve.tensor_tensor(vt[:, j, :], LB[j][:, :], rows[:, 0, :], ALU.add).then_inc(L_DVE.sem, 1)

        def l_pool(pool, b):
            L_DVE.before(pool, b, "norm")
            L_DVE.after(pool, b, "mean")
            alone(pool, passed)
            pool.tensor_scalar(bve[:, :], bmv[:, :, 1], 1.0, EPS, ALU.mult, ALU.add).then_inc(L_POOL.sem, 1)
            L_POOL.after(pool, b, "eps")
            pool.tensor_tensor(brstd[:, :], bve[:, :], mhalf_b[:, :], ALU.pow).then_inc(L_POOL.sem, 1)
            C_DVE.before(pool, b, "hid1")
            pool.tensor_tensor(hb[:, :, :], h_in[:, :, :], rows[:, 1, :].unsqueeze(1).broadcast_to([128, TJ, E]), ALU.add)\
                .then_inc(L_POOL.sem, 1)

        def head(h):
            return h // 4, 32 * (h % 4)

        def a_pe(pe, b):
            L_ACT.after(pe, b, f"k{EC - 1}")
            L_DVE.after(pe, b, "v1")
            C_DVE.before(pe, b, "out1")
            for h in range(AH + 2):
                if h < AH:
                    c, p = head(h)
                    if h >= 2:
                        A_DVE.after(pe, b, f"m{h - 2}")
                    for j in range(TJ):
                        last = pe.matmul(SB[h % 2][:, j * T:(j + 1) * T], qt[p:p + HD, c, j * 128:(j + 1) * 128],
                                         kt[p:p + HD, c, :], start=True, stop=True)
                    last.then_inc(A_PE.sem, 1)
                if 1 <= h <= AH:
                    A_ACT.after(pe, b, f"e{h - 1}")
                    if h >= 2:
                        A_DVE.after(pe, b, f"p{h - 2}")
                    for i in range(2):
                        for j in range(TJ):
                            o = i * T + j * 128
                            last = pe.transpose(TBK[:, o:o + 128], sc[:, (h - 1) % 2, j, i * 128:(i + 1) * 128], idn[:, :])
                    last.then_inc(A_PE.sem, 1)
                if h >= 2:
                    g = h - 2
                    A_DVE.after(pe, b, f"p{g}")
                    if g == 0:
                        C_DVE.before(pe, b, "ao")
                    for j in range(TJ):
                        for i in range(2):
                            last = pe.matmul(OB[j][:, g * HD:(g + 1) * HD], pt[:, g % 2, i, j * 128:(j + 1) * 128],
                                             vt[:, i, g * HD:(g + 1) * HD], start=(i == 0), stop=(i == 1))
                    last.then_inc(A_PE.sem, 1)

        def a_dve(dve, b):
            for h in range(AH + 1):
                if h < AH:
                    A_PE.after(dve, b, f"s{h}")
                    if h >= 2:
                        A_PE.after(dve, b, f"t{h - 2}")
                        A_ACT.after(dve, b, f"e{h - 2}")
                    else:
                        A_PE.before(dve, b, f"t{AH - 2 + h}")
                        A_ACT.before(dve, b, f"e{AH - 2 + h}")
                    if h == 0:
                        L_DVE.after(dve, b, "mask")
                        A_DVE.before(dve, b, f"p{AH - 1}")
                    alone(dve, passed)
                    for j in range(TJ):
                        last = dve.tensor_tensor_reduce(out=sc[:, h % 2, j, :], in0=SB[h % 2][:, j * T:(j + 1) * T],
                                                        in1=mneg[:, :], scale=1.0, scalar=MASKED, op0=ALU.add, op1=ALU.max,
                                                        accum_out=mx[:, h % 2, j:j + 1])
                    last.then_inc(A_DVE.sem, 1)
                    A_DVE.after(dve, b, f"m{h}")
                    dve.tensor_scalar(nmx[:, h % 2, :], mx[:, h % 2, :], -SCALE, None, ALU.mult).then_inc(A_DVE.sem, 1)
                if h:
                    A_PE.after(dve, b, f"t{h - 1}")
                    if h >= 3:
                        A_PE.after(dve, b, f"o{h - 3}")
                    elif h:
                        A_PE.before(dve, b, f"o{AH - 3 + h}")
                    dve.tensor_copy(pt[:, (h - 1) % 2], TBK[:, :].rearrange("p (i t) -> p i t", i=2))\
                       .then_inc(A_DVE.sem, 1)

        def a_act(act, b):
            C_DVE.before(act, b, "rden")
            for h in hs:
                A_DVE.after(act, b, f"n{h}")
                for j in range(TJ):
                    last = act.activation(sc[:, h % 2, j, :], sc[:, h % 2, j, :], ACT.Exp, bias=nmx[:, h % 2, j:j + 1],
                                          scale=SCALE, accum_out=den[:, j, h:h + 1])
                last.then_inc(A_ACT.sem, 1)

        def c_pe1(pe, b):
            C_DVE.after(pe, b, "ao")
            for h in range(2):
                if h:
                    C_ACT.after(pe, b, "aot_a")
                else:
                    C_DVE.before(pe, b, "out1")
                for c in (2 * h, 2 * h + 1):
                    for j in range(TJ):
                        o = (c % 2) * T + j * 128
                        last = pe.transpose(CB[:, o:o + 128], ao[:, j, c * 128:(c + 1) * 128], idn[:, :])
                last.then_inc(C_PE.sem, 1)
            for j in range(TJ):
                if j:
                    C_DVE.after(pe, b, "hid0")
                else:
                    C_ACT.after(pe, b, "aot_b")
                for c in cs:
                    last = pe.matmul(CB[:, :], aot[:, c, j * 128:(j + 1) * 128], Wq[:, 3, c, :],
                                     start=(c == 0), stop=(c == EC - 1))
                last.then_inc(C_PE.sem, 1)
            C_DVE.after(pe, b, "norm")
            for h in range(2):
                if h:
                    C_ACT.after(pe, b, "yn1")
                for c in (2 * h, 2 * h + 1):
                    for j in range(TJ):
                        o = (c % 2) * T + j * 128
                        last = pe.transpose(CB[:, o:o + 128], hl2(j)[:, c * 128:(c + 1) * 128], idn[:, :])
                last.then_inc(C_PE.sem, 1)

        def hl2(j):
            return ao[:, j, :]

        def c_pe2(pe, b):
            C_ACT.after(pe, b, "yn3")
            for n in range(FC // 2):
                if n >= 4:
                    C_ACT.after(pe, b, f"g{2 * n - 7}")
                for c in (2 * n, 2 * n + 1):
                    for i in cs:
                        last = pe.matmul(FB[n % 4][:, (c % 2) * T:(c % 2 + 1) * T],
                                         W[:, FCW + c // 4, i, (c % 4) * 128:(c % 4 + 1) * 128],
                                         aot[:, i, :], start=(i == 0), stop=(i == EC - 1))
                last.then_inc(C_PE.sem, 1)

        def c_pe3(pe, b):
            for j in range(TJ):
                for c in range(FC):
                    if j == 0:
                        C_ACT.after(pe, b, f"g{c}" if c else f"g{FC - 7}")
                    last = pe.matmul(FB[j][:, :], gl[:, c, j * 128:(j + 1) * 128], W[:, PRW + c // 4, c % 4, :],
                                     start=(c == 0), stop=(c == FC - 1))
                last.then_inc(C_PE.sem, 1)

        def c_dve1(dve, b):
            A_ACT.after(dve, b, f"e{AH - 1}")
            dve.reciprocal(den[:, :, :], den[:, :, :]).then_inc(C_DVE.sem, 1)
            C_DVE.after(dve, b, "rden")
            A_PE.after(dve, b, f"o{AH - 1}")
            C_PE.before(dve, b, "nturn_b")
            for j in range(TJ):
                last = dve.tensor_tensor(ao[:, j, :].rearrange("p (h d) -> p h d", h=AH),
                                         OB[j][:, :].rearrange("p (h d) -> p h d", h=AH),
                                         den[:, j, :].unsqueeze(2).broadcast_to([128, AH, HD]), ALU.mult)
            last.then_inc(C_DVE.sem, 1)
            L_POOL.after(dve, b, "hb")
            C_POOL.before(dve, b, "hp")
            for j in range(TJ):
                C_PE.after(dve, b, f"c{j}")
                dve.tensor_tensor(hid[:, j, :], CB[:, :], hb[:, j, :], ALU.add).then_inc(C_DVE.sem, 1)
            C_DVE.after(dve, b, "hid1")
            for j in range(TJ):
                last = dve.bn_stats(bstat2[:, j, :], hid[:, j, :])
            last.then_inc(C_DVE.sem, 1)
            C_DVE.after(dve, b, "stat")
            alone(dve, passed)
            for j in range(TJ):
                last = dve.bn_aggr(bmv2[:, j, :], bstat2[:, j, :])
            last.then_inc(C_DVE.sem, 1)
            C_DVE.after(dve, b, "mean")
            C_POOL.after(dve, b, "rstd")
            for j in range(TJ):
                last = dve.tensor_scalar(ao[:, j, :], hid[:, j, :], bmv2[:, j, 0:1], brstd2[:, j:j + 1],
                                         ALU.subtract, ALU.mult)
            last.then_inc(C_DVE.sem, 1)

        def c_dve2(dve, b):
            C_POOL.after(dve, b, "hp")
            if not (isinstance(b, int) and b == 0):
                dve.wait_ge(stored, 16 * b)
            for j in range(TJ):
                C_PE.after(dve, b, f"p{j}")
                dve.tensor_tensor(res[:, j, :], FB[j][:, :], hp[:, j, :], ALU.add).then_inc(C_DVE.sem, 1)

        def c_act1(act, b):
            C_PE.before(act, b, f"f{FC // 2 - 1}")
            for h in range(2):
                C_PE.after(act, b, f"turn_{halves[h]}")
                act.activation(aot[:, 2 * h:2 * h + 2, :], CB[:, :].rearrange("p (c t) -> p c t", c=2), ACT.Copy)\
                   .then_inc(C_ACT.sem, 1)
            for c in cs:
                C_PE.after(act, b, "nturn_a" if c < 2 else "nturn_b")
                act.activation(aot[:, c, :], CB[:, (c % 2) * T:(c % 2 + 1) * T], ACT.Identity,
                               bias=bcol("ln2_b", c), scale=bcol("ln2_w", c)).then_inc(C_ACT.sem, 1)

        def c_act2(act, b):
            C_PE.before(act, b, "p1")
            for c in range(FC):
                C_PE.after(act, b, f"f{c // 2}")
                act.activation(gl[:, c, :], FB[c // 2 % 4][:, (c % 2) * T:(c % 2 + 1) * T], ACT.Gelu_apprx_tanh,
                               bias=fcb[:, c:c + 1]).then_inc(C_ACT.sem, 1)

        def c_pool(pool, b):
            C_DVE.before(pool, b, "norm")
            C_DVE.after(pool, b, "mean")
            alone(pool, passed)
            pool.tensor_scalar(bve2[:, :], bmv2[:, :, 1], 1.0, EPS, ALU.mult, ALU.add).then_inc(C_POOL.sem, 1)
            C_POOL.after(pool, b, "eps")
            pool.tensor_tensor(brstd2[:, :], bve2[:, :], mhalf_b[:, :], ALU.pow).then_inc(C_POOL.sem, 1)
            C_DVE.before(pool, b, "out1")
            pool.tensor_tensor(hp[:, :, :], hid[:, :, :], rows[:, 2, :].unsqueeze(1).broadcast_to([128, TJ, E]), ALU.add)\
                .then_inc(C_POOL.sem, 1)

        bstat2 = sb(cb, "bstat2", [128, TJ, 6])
        bmv2 = sb(cb, "bmv2", [128, TJ, 2])
        bve2 = sb(cb, "bve2", [128, TJ])
        brstd2 = sb(cb, "brstd2", [128, TJ])

        def phase_b(eng, p):
            def do(name, b):
                if name in p:
                    p[name](eng, b)

            do("hc", 0)
            def round_b(i):
                do("A", i)
                do("hc", i + 1)
                do("C1", i)
                do("L", i + 1)
                do("C2", i)
                do("C3", i)
                do("out", i)

            do("L", 0)
            round_b(0)
            with eng.Fori(1, B - 1) as i:
                round_b(i)
            for name in ("A", "C1", "C2", "C3", "out"):
                do(name, B - 1)

        block = ctx.enter_context(nc.Block())
        loads_a = [(W[:, n, :, :], w_a[n].rearrange("(c p) e -> p c e", p=128)) for n in range(8)]
        loads_a += [(va[:, :, :], vec_a), (m1[:, :, :], maa1.rearrange("(c p) n -> p c n", p=128)), (m2[:, :], maa2),
                    (m2b[:, :], maa2b), (d1[:, :, :], dec1.rearrange("(c p) n -> p c n", p=128)), (d2[:, :], dec2),
                    (idn[:, :], ident), (blk[:, :, :], blocks), (seli32, sel_in), (selo[:, :, :], sel_out)]
        loads_b = [(Wq[:, n, :, :], w_b[n].rearrange("(c p) e -> p c e", p=128)) for n in range(4)]
        loads_b += [(vb[:, :, :], vec_b), (fcb[:, :], fc_b)]
        loads_b += [(rows[:, n, :], rows_b[n].partition_broadcast(128)) for n in range(3)]
        loads_b2 = [(W[:, n, :, :], w_b[4 + n].rearrange("(c p) e -> p c e", p=128)) for n in range(8)]

        @block.sync
        def _(sp):
            for dst, src in reversed(loads_a):
                sp.dma_start(dst, src).then_inc(weights_in, 16)
            phase_a(sp, {"x": sp_x, "s0": sp_s0, "x1": sp_x1, "save": sp_save})
            end_a(sp)
            for dst, src in loads_b:
                sp.dma_start(dst, src).then_inc(b_in1, 16)
            for dst, src in loads_b2:
                sp.dma_start(dst, src).then_inc(b_in2, 16)
            phase_b(sp, {"hc": sp_hc, "out": sp_out})
            sp.wait_ge(stored, 16 * B)

        @block.scalar
        def _(act):
            act.wait_ge(weights_in, 16 * len(loads_a))
            act.wait_ge(const_ready, 4)
            phase_a(act, {"X1": x_act1, "P": p_act, "G": g_act, "S": s_act, "N": n_act,
                          "K2": k_act1, "K3": k_act2, "K4": k_act3})
            end_a(act)
            act.wait_ge(b_in1, 16 * len(loads_b))
            phase_b(act, {"L": l_act, "A": a_act, "C1": c_act1, "C2": c_act2})

        @block.vector
        def _(dve):
            dve.wait_ge(weights_in, 16 * len(loads_a))
            dve.tensor_scalar(half_gn[:, 0:1, :], va[:, VA.index("gn_w"):VA.index("gn_w") + 1, :], 0.5, None, ALU.mult)\
               .then_inc(const_ready, 1)
            dve.tensor_scalar(half_gn[:, 1:2, :], va[:, VA.index("gn_b"):VA.index("gn_b") + 1, :], 0.5, None, ALU.mult)\
               .then_inc(const_ready, 1)
            dve.tensor_copy(seli[:, :, :], seli32).then_inc(const_ready, 1)
            dve.memset(small[:, 0:1], EPS).then_inc(const_ready, 1)
            dve.wait_ge(const_ready, 4)
            phase_a(dve, {"X1": x_dve1, "X2": x_dve2, "P": p_dve, "G": g_dve, "S": s_dve, "N": n_dve,
                          "K1": k_dve1, "K2": k_dve2, "K4": k_dve3})
            end_a(dve)
            dve.wait_ge(b_in1, 16 * len(loads_b))
            phase_b(dve, {"L": l_dve, "A": a_dve, "C1": c_dve1, "C3": c_dve2})

        @block.gpsimd
        def _(pool):
            pool.memset(mhalf[:, :], -0.5).then_inc(b_const, 1)
            pool.wait_ge(b_const, 1)
            pool.wait_ge(weights_in, 16 * len(loads_a))
            phase_a(pool, {"X1": x_pool1, "X2": x_pool2, "S": s_pool, "K1": k_pool})
            end_a(pool)
            pool.memset(mhalf_b[:, :], -0.5).then_inc(b_const, 1)
            pool.wait_ge(b_const, 2)
            pool.wait_ge(b_in1, 16 * len(loads_b))
            phase_b(pool, {"L": l_pool, "C1": c_pool})

        @block.tensor
        def _(pe):
            pe.wait_ge(weights_in, 16 * len(loads_a))
            pe.wait_ge(const_ready, 4)
            phase_a(pe, {"X1": x_pe1, "X2": x_pe2, "P": p_pe, "G": g_pe, "S": s_pe, "N": n_pe,
                         "K1": k_pe1, "K2": k_pe2, "K3": k_pe3, "K4": k_pe4})
            end_a(pe)
            pe.wait_ge(b_in1, 16 * len(loads_b))
            pe.wait_ge(b_in2, 16 * len(loads_b2))
            phase_b(pe, {"L": l_pe, "A": a_pe, "C1": c_pe1, "C2": c_pe2, "C3": c_pe3})


def kernel(**inputs):
    import numpy as np
    import concourse.bacc as bacc
    from concourse.bass_utils import run_bass_kernel_spmd

    a = {k: np.asarray(v) for k, v in inputs.items()}

    def l0(n):
        return a["L0_xattn_" + n]

    def l1(n):
        return a["L1_xattn_" + n]

    def cols(vectors):
        return np.ascontiguousarray(np.stack([v.reshape(EC, 128).T for v in vectors], axis=1))

    ctx_ = a["ctx_2048"]
    heads = np.arange(128) // S
    same = (heads[:, None] == heads[None, :]).astype(np.float32)
    index = np.arange(128) % S
    sel_in = same[:, None, :] * (index[:, None, None] == np.arange(S)[None, :, None]).astype(np.float32)
    sel_out = same[:, None, :] * ((index[None, None, :] == np.arange(S)[None, :, None]) - np.float32(1 / S)).astype(np.float32)
    arrays = {
        "x": a["x"],
        "prev1": np.ascontiguousarray(ctx_[:, 1, :].reshape(B, EC, 128).transpose(0, 2, 1)),
        "prev2": np.ascontiguousarray(ctx_[:, 0, :].reshape(B, EC, 128).transpose(0, 2, 1)),
        "s0": np.ascontiguousarray(ctx_[:, 2:2 + S, :].reshape(B, EC, 128, S).transpose(0, 2, 1, 3).reshape(B, 128, EC * S)),
        "ctxt": np.ascontiguousarray(ctx_.transpose(0, 2, 1)),
        "mask": a["mask_BxS2_bf1"].view(np.uint8),
        "vec_a": cols([l0("ln1_w"), l0("ln1_b"), l0("maa_x"), *l0("maa_stack"), l0("time_decay"),
                       l0("faaaa").reshape(E), l0("gn_w"), l0("gn_b"), l0("ln2_w"), l0("ln2_b"),
                       l0("ffn_maa_k"), l0("ffn_maa_r")]),
        "w_a": np.stack([np.ascontiguousarray(l0(n).T) for n in ("Wr", "Wk", "Wv", "Wg", "Wo", "ffn_Wk", "ffn_Wr", "ffn_Wv")]),
        "maa1": l0("maa_w1"),
        "maa2": np.ascontiguousarray(l0("maa_w2")[:4].reshape(4 * MAA, E)),
        "maa2b": np.ascontiguousarray(l0("maa_w2")[4]),
        "dec1": l0("decay_w1"),
        "dec2": l0("decay_w2"),
        "vec_b": cols([l1("ln1_w"), l1("ln1_b"), l1("q_b"), l1("k_b"), l1("ln2_w"), l1("ln2_b")]),
        "w_b": np.stack([l1("q_w"), l1("k_w"), l1("v_w"), l1("cproj_w")]
                        + [np.ascontiguousarray(l1("fc_w")[:, n * E:(n + 1) * E]) for n in range(4)]
                        + [l1("proj_w")[n * E:(n + 1) * E] for n in range(4)]),
        "fc_b": np.ascontiguousarray(l1("fc_b").reshape(FC, 128).T),
        "rows_b": np.stack([l1("v_b"), l1("cproj_b"), l1("proj_b")]),
        "ident": np.eye(128, dtype=np.float32),
        "blocks": np.ascontiguousarray(np.stack([same, np.eye(128, dtype=np.float32) - same / np.float32(S),
                                                 same / np.float32(S)], axis=1)),
        "sel_in": sel_in,
        "sel_out": sel_out,
    }
    nc = bacc.Bacc("TRN2", target_bir_lowering=False, num_devices=1)
    args = [nc.dram_tensor(f"in_{k}", v.shape, mybir.dt.from_np(v.dtype), kind="ExternalInput").ap()
            for k, v in arrays.items()]
    scratch = nc.dram_tensor("scratch", (B, T, E), F32, kind="Internal").ap()
    out = nc.dram_tensor("out_0", (B, T, E), F32, kind="ExternalOutput").ap()
    build(nc, *args, scratch, out)
    r = run_bass_kernel_spmd(nc, [{f"in_{k}": v for k, v in arrays.items()}], core_ids=[0])
    return r.results[0]["out_0"]
```

```python
from contextlib import ExitStack

import concourse.bass as bass
from concourse import mybir

F32 = mybir.dt.float32
F32R = mybir.dt.float32r
U8 = mybir.dt.uint8
ALU = mybir.AluOpType
ACT = mybir.ActivationFunctionType

B, T, E = 16, 256, 512
EC = E // 128
TJ = T // 128
S = 16
MAA, NG, DEC = 32, 5, 64
AH, HD = 16, 32
INNER = 4 * E
FC = INNER // 128
EPS = 1e-5
SCALE = HD ** -0.5
MASKED = -3.4028234663852886e38
GK, GW, GV, GR, GG = range(NG)

VA = ["ln1_w", "ln1_b", "maa_x", "maa_k", "maa_w", "maa_v", "maa_r", "maa_g", "time_decay", "bonus",
      "gn_w", "gn_b", "ln2_w", "ln2_b", "ffn_maa_k", "ffn_maa_r"]
VB = ["ln1_w", "ln1_b", "q_b", "k_b", "ln2_w", "ln2_b"]


def alone(eng, sem):
    eng.sem_inc(sem, 1)


class Steps:

    def __init__(self, sem, names):
        self.sem, self.names, self.per = sem, names, len(names)

    def count(self, b, name):
        return b * self.per + self.names.index(name) + 1


def later(b):
    return not isinstance(b, int) or b > 0


def build(nc, x, prev1, prev2, s0, ctxt, mask, vec_a, w_a, maa1, maa2, maa2b, dec1, dec2,
          vec_b, w_b, fc_b, rows_b, ident, blocks, sel_in, sel_out, scratch, out):
    ctx = ExitStack()
    with ctx:
        def sem(name):
            return ctx.enter_context(nc.semaphore(name))

        def steps(name, names):
            return Steps(sem(name), names)

        def sb(c, name, shape, dt=F32):
            return c.enter_context(nc.sbuf_tensor(name, shape, dt))

        W = sb(ctx, "W", [128, 8, EC, E])
        idn = sb(ctx, "idn", [128, 128])
        small = sb(ctx, "small", [128, 24])
        banks = [ctx.enter_context(nc.psum_tensor(f"bank{i}", [128, 512], F32)) for i in range(8)]

        ca = ctx.enter_context(ExitStack())
        va = sb(ca, "va", [128, len(VA), EC])
        half_gn = sb(ca, "half_gn", [128, 2, EC])
        m1 = sb(ca, "m1", [128, EC, NG * MAA])
        m2 = sb(ca, "m2", [128, E])
        m2b = sb(ca, "m2b", [MAA, E])
        d1 = sb(ca, "d1", [128, EC, DEC])
        d2 = sb(ca, "d2", [DEC, E])
        blk = sb(ca, "blk", [128, 3, 128])
        seli = sb(ca, "seli", [128, S, 128], F32R)
        selo = sb(ca, "selo", [128, S, 128])
        mhalf = sb(ca, "mhalf", [128, TJ])
        x_t = sb(ca, "x_t", [128, TJ, E])
        stat = sb(ca, "stat", [128, TJ, 6])
        mv = sb(ca, "mv", [128, TJ, 2])
        ve = sb(ca, "ve", [128, TJ])
        rstd = sb(ca, "rstd", [128, TJ])
        pr1 = sb(ca, "pr1", [128, EC])
        xn = sb(ca, "xn", [128, EC, T + 1])
        sx = sb(ca, "sx", [128, EC, T])
        h1 = sb(ca, "h1", [128, T])
        h2 = sb(ca, "h2", [MAA, T])
        x5 = sb(ca, "x5", [128, NG, EC, T])
        xx = x5[:, 0]
        seli32 = x5[:, 0:2].rearrange("p g c (h t) -> p (g c h) t", h=2)
        dh = sb(ca, "dh", [DEC, T])
        ez = sb(ca, "ez", [128, T])
        w_ = sb(ca, "w_", [128, EC, T])
        k_ = sb(ca, "k_", [128, EC, T])
        r_ = sb(ca, "r_", [128, EC, T])
        v_ = sb(ca, "v_", [128, EC, T])
        vhi = sb(ca, "vhi", [128, EC, T], F32R)
        vlo = sb(ca, "vlo", [128, EC, T], F32R)
        th = sb(ca, "th", [128, 2, T])
        g2 = sb(ca, "g2", [128, EC, T])
        s0t = sb(ca, "s0t", [128, EC, S])
        ru = sb(ca, "ru", [128, T])
        zv = sb(ca, "zv", [128, T])
        kv = sb(ca, "kv", [128, 2, 2, T])
        st = sb(ca, "st", [128, 2, 2, T + 1])
        rs = sb(ca, "rs", [128, 2, 2, T])
        att = sb(ca, "att", [128, EC, T])
        sq = sb(ca, "sq", [128, EC, T])
        x1 = sb(ca, "x1", [128, TJ, E])
        stat2 = sb(ca, "stat2", [128, TJ, 6])
        mv2 = sb(ca, "mv2", [128, TJ, 2])
        ve2 = sb(ca, "ve2", [128, TJ])
        rstd2 = sb(ca, "rstd2", [128, TJ])
        pr2 = sb(ca, "pr2", [128, EC])
        xl = sb(ca, "xl", [128, TJ, E])
        xn2 = sb(ca, "xn2", [128, EC, T + 1])
        sx2 = xl[:, :, :].rearrange("p j (a t) -> p (j a) t", a=2)
        xk = sb(ca, "xk", [128, EC, T])
        xr = sb(ca, "xr", [128, EC, T])
        kk = sb(ca, "kk", [128, EC, T])
        tr = xk[:, :, :].rearrange("p (j a) t -> p j (a t)", a=2)

        def vcol(name, c):
            return va[:, VA.index(name), c:c + 1]

        WR, WK, WV, WG, WO, FWK, FWR, FWV = range(8)

        weights_in = sem("weights_in")
        const_ready = sem("const_ready")
        passed = sem("passed")
        x_in = sem("x_in")
        s0_in = sem("s0_in")
        x1_in = sem("x1_in")
        saved = sem("saved")
        halves = ["a", "b"]
        cs = range(EC)
        X_PE = steps("X_PE", ["turn_a", "turn_b", "hid"] + [f"mix{g}{h}" for g in range(NG) for h in halves])
        X_ACT = steps("X_ACT", [f"xn{c}" for c in cs] + ["h1", "h2"])
        X_DVE = steps("X_DVE", ["stat", "mean", "norm", "prev", "shift"] + [f"xx{c}" for c in cs]
                      + [f"mix{g}{c}" for g in range(NG) for c in cs])
        X_POOL = steps("X_POOL", ["eps", "rstd"] + [f"x5{g}{h}" for g in range(NG) for h in halves])
        P_PE = steps("P_PE", ["dh"] + [f"{n}{c}" for c in cs for n in ("zk", "vr")])
        P_ACT = steps("P_ACT", ["dh"] + [f"{n}{c}" for c in cs for n in ("ez", "w", "k", "v", "vhi", "r")])
        P_DVE = steps("P_DVE", [f"vlo{c}" for c in cs])
        G_PE = steps("G_PE", ["ga", "gb"])
        G_ACT = steps("G_ACT", ["tha", "thb"])
        G_DVE = steps("G_DVE", ["ga", "gb"])
        qs = range(S // 2)
        NE = S // 2 + 1
        BONUS = NE - 1
        elements = [(c, e) for c in cs for e in range(NE)]

        def shifted(c, e, by):
            n = c * NE + e + by
            return n // NE, n % NE

        S_PE = steps("S_PE", ["v00", "v01"] + [n for c, e in elements for n in
                                               [f"o{c}{e}"] + (["v%d%d" % shifted(c, e, 2)] if shifted(c, e, 2)[0] < EC else [])])
        S_DVE = steps("S_DVE", [n for c, e in elements for n in
                                [f"kv{c}{e}"] + ([f"scan{c}{e}"] if e < BONUS else []) + ([f"ru{c}"] if e == 1 else [])])
        S_POOL = steps("S_POOL", [n for c in cs for q in qs for n in (f"s0{c}{q}", f"rs{c}{q}")])
        S_ACT = steps("S_ACT", [n for c in cs for n in (f"att{c}", f"sq{c}")])
        N_PE = steps("N_PE", [f"var{h}" for h in halves])
        N_ACT = steps("N_ACT", [f"sd{h}" for h in halves])
        N_DVE = steps("N_DVE", ["rstd", "norm", "affine", "gate"])
        K_PE = steps("K_PE", ["wo0", "wo1", "turn_a", "turn_b"] + [f"fk{h}" for h in halves]
                     + ["fr0", "fr1", "fv0", "fv1"])
        K_ACT = steps("K_ACT", [f"xn{c}" for c in cs] + [f"{n}{h}" for h in halves for n in ("relu", "kk")]
                      + ["th0", "th1"])
        K_DVE = steps("K_DVE", ["x10", "x11", "stat", "mean", "norm", "prev", "shift", "xk", "xr"]
                      + [f"{n}{j}" for j in range(TJ) for n in ("rv", "out")])
        K_POOL = steps("K_POOL", ["eps", "rstd"])

        XB, PB, KB, VBK, AB = banks[0:2], banks[2:4], banks[4], banks[5:7], banks[7]


        def sp_x(sp, b):
            if later(b):
                sp.wait_ge(X_DVE.sem, X_DVE.count(b - 1, "prev"))
            if later(b):
                sp.wait_ge(X_PE.sem, X_PE.count(b - 1, "turn_b"))
            sp.dma_start(x_t[:, :, :], x[b].rearrange("(j p) e -> p j e", p=128)).then_inc(x_in, 16)
            sp.dma_start(pr1[:, :], prev1[b]).then_inc(x_in, 16)

        def sp_s0(sp, b):
            if later(b):
                sp.wait_ge(S_POOL.sem, S_POOL.count(b - 1, f"s0{EC - 1}{S // 2 - 1}"))
            if later(b):
                sp.wait_ge(S_DVE.sem, S_DVE.count(b - 1, f"scan{EC - 1}{S // 2 - 1}"))
            sp.dma_start(s0t[:, :, :], s0[b].rearrange("p (c d) -> p c d", c=EC)).then_inc(s0_in, 16)

        def sp_x1(sp, b):
            if later(b):
                sp.wait_ge(K_DVE.sem, K_DVE.count(b - 1, "out1"))
            sp.dma_start(x1[:, :, :], x[b].rearrange("(j p) e -> p j e", p=128)).then_inc(x1_in, 16)
            sp.dma_start(pr2[:, :], prev2[b]).then_inc(x1_in, 16)

        def sp_save(sp, b):
            sp.wait_ge(K_DVE.sem, K_DVE.count(b, "out1"))
            sp.dma_start(scratch[b].rearrange("(j p) e -> p j e", p=128), tr[:, :, :]).then_inc(saved, 16)

        def x_pe1(pe, b):
            pe.wait_ge(X_DVE.sem, X_DVE.count(b, "norm"))
            for h in range(2):
                if h == 0:
                    if later(b):
                        pe.wait_ge(X_DVE.sem, X_DVE.count(b - 1, f"mix{NG - 1}1"))
                else:
                    if later(b):
                        pe.wait_ge(X_DVE.sem, X_DVE.count(b - 1, f"mix{NG - 1}3"))
                for c in (2 * h, 2 * h + 1):
                    for j in range(TJ):
                        o = (c % 2) * T + j * 128
                        last = pe.transpose(XB[h][:, o:o + 128], x_t[:, j, c * 128:(c + 1) * 128], idn[:, :])
                last.then_inc(X_PE.sem, 1)

        def x_pe_hid(pe, b):
            pe.wait_ge(X_DVE.sem, X_DVE.count(b, "xx3"))
            pe.wait_ge(X_ACT.sem, X_ACT.count(b, "xn1"))
            for m, (o, n) in enumerate(((0, 128), (T, MAA))):
                for c in cs:
                    last = pe.matmul(XB[0][0:n, o:o + T], m1[:, c, 128 * m:128 * m + n], xx[:, c, :],
                                     start=(c == 0), stop=(c == EC - 1))
            last.then_inc(X_PE.sem, 1)

        def x_pe2(pe, b, g):
            if g == 0:
                pe.wait_ge(X_ACT.sem, X_ACT.count(b, "h2"))
            for h in range(2):
                if g:
                    pe.wait_ge(X_DVE.sem, X_DVE.count(b, f"mix{g - 1}{2 * h + 1}"))
                for c in (2 * h, 2 * h + 1):
                    wt = m2[MAA * g:MAA * (g + 1), c * 128:(c + 1) * 128] if g < 4 else m2b[:, c * 128:(c + 1) * 128]
                    hid = h1[MAA * g:MAA * (g + 1), :] if g < 4 else h2[:, :]
                    last = pe.matmul(XB[h][:, (c % 2) * T:(c % 2 + 1) * T], wt, hid, start=True, stop=True)
                last.then_inc(X_PE.sem, 1)

        def x_act1(act, b):
            if later(b):
                act.wait_ge(X_DVE.sem, X_DVE.count(b - 1, "shift"))
            if later(b):
                act.wait_ge(X_POOL.sem, X_POOL.count(b - 1, f"x5{NG - 1}b"))
            for c in cs:
                act.wait_ge(X_PE.sem, X_PE.count(b, "turn_a" if c < 2 else "turn_b"))
                act.activation(xn[:, c, 1:T + 1], XB[c // 2][:, (c % 2) * T:(c % 2 + 1) * T], ACT.Identity,
                               bias=vcol("ln1_b", c), scale=vcol("ln1_w", c)).then_inc(X_ACT.sem, 1)

        def x_act_hid(act, b):
            if later(b):
                act.wait_ge(X_PE.sem, X_PE.count(b - 1, f"mix{NG - 1}b"))
            act.wait_ge(X_PE.sem, X_PE.count(b, "hid"))
            act.activation(h1[:, :], XB[0][:, 0:T], ACT.Tanh).then_inc(X_ACT.sem, 1)
            act.activation(h2[:, :], XB[0][0:MAA, T:2 * T], ACT.Tanh).then_inc(X_ACT.sem, 1)

        def x_dve1(dve, b):
            if later(b):
                dve.wait_ge(X_DVE.sem, X_DVE.count(b - 1, f"mix{NG - 1}3"))
            dve.wait_ge(x_in, 32 * b + 32)
            for j in range(TJ):
                last = dve.bn_stats(stat[:, j, :], x_t[:, j, :])
            last.then_inc(X_DVE.sem, 1)
            if later(b):
                dve.wait_ge(X_POOL.sem, X_POOL.count(b - 1, "eps"))
            dve.wait_ge(X_DVE.sem, X_DVE.count(b, "stat"))
            alone(dve, passed)
            for j in range(TJ):
                last = dve.bn_aggr(mv[:, j, :], stat[:, j, :])
            last.then_inc(X_DVE.sem, 1)

        def x_dve_norm(dve, b):
            dve.wait_ge(X_POOL.sem, X_POOL.count(b, "rstd"))
            dve.wait_ge(X_DVE.sem, X_DVE.count(b, "mean"))
            for j in range(TJ):
                last = dve.tensor_scalar(x_t[:, j, :], x_t[:, j, :], mv[:, j, 0:1], rstd[:, j:j + 1],
                                         ALU.subtract, ALU.mult)
            last.then_inc(X_DVE.sem, 1)

        def x_dve_shift(dve, b):
            if later(b):
                dve.wait_ge(X_POOL.sem, X_POOL.count(b - 1, f"x5{NG - 1}b"))
            dve.tensor_copy(xn[:, :, 0], pr1[:, :]).then_inc(X_DVE.sem, 1)
            dve.wait_ge(X_ACT.sem, X_ACT.count(b, "xn3"))
            dve.wait_ge(X_DVE.sem, X_DVE.count(b, "prev"))
            dve.tensor_tensor(sx[:, :, :], xn[:, :, 0:T], xn[:, :, 1:T + 1], ALU.subtract).then_inc(X_DVE.sem, 1)

        def x_dve_xx(dve, b):
            dve.wait_ge(X_DVE.sem, X_DVE.count(b, "shift"))
            if later(b):
                dve.wait_ge(P_PE.sem, P_PE.count(b - 1, f"zk{EC - 1}"))
            for c in cs:
                dve.scalar_tensor_tensor(xx[:, c, :], sx[:, c, :], vcol("maa_x", c), xn[:, c, 1:T + 1],
                                         ALU.mult, ALU.add).then_inc(X_DVE.sem, 1)

        def x_dve2(dve, b, g):
            if g == 0:
                if later(b):
                    dve.wait_ge(P_PE.sem, P_PE.count(b - 1, f"vr{EC - 1}"))
            if g == GG:
                if later(b):
                    dve.wait_ge(G_PE.sem, G_PE.count(b - 1, "gb"))
            for c in cs:
                if c % 2 == 0:
                    dve.wait_ge(X_PE.sem, X_PE.count(b, f"mix{g}{halves[c // 2]}"))
                dve.scalar_tensor_tensor(x5[:, g, c, :], XB[c // 2][:, (c % 2) * T:(c % 2 + 1) * T],
                                         va[:, VA.index("maa_k") + g, c:c + 1], sx[:, c, :],
                                         ALU.add, ALU.mult).then_inc(X_DVE.sem, 1)

        def x_pool1(pool, b):
            if later(b):
                pool.wait_ge(X_DVE.sem, X_DVE.count(b - 1, "norm"))
            if later(b):
                pool.wait_ge(X_POOL.sem, X_POOL.count(b - 1, "rstd"))
            pool.wait_ge(X_DVE.sem, X_DVE.count(b, "mean"))
            alone(pool, passed)
            pool.tensor_scalar(ve[:, :], mv[:, :, 1], 1.0, EPS, ALU.mult, ALU.add).then_inc(X_POOL.sem, 1)
            pool.wait_ge(X_POOL.sem, X_POOL.count(b, "eps"))
            pool.tensor_tensor(rstd[:, :], ve[:, :], mhalf[:, :], ALU.pow).then_inc(X_POOL.sem, 1)

        def x_pool2(pool, b, g):
            for h in range(2):
                pool.wait_ge(X_DVE.sem, X_DVE.count(b, f"mix{g}{2 * h + 1}"))
                pool.tensor_tensor(x5[:, g, 2 * h:2 * h + 2, :], x5[:, g, 2 * h:2 * h + 2, :],
                                   xn[:, 2 * h:2 * h + 2, 1:T + 1], ALU.add).then_inc(X_POOL.sem, 1)

        def project(pe, bank, half, wt, g, c):
            for i in cs:
                last = pe.matmul(bank[:, half * T:(half + 1) * T], W[:, wt, i, c * 128:(c + 1) * 128],
                                 x5[:, g, i, :], start=(i == 0), stop=(i == EC - 1))
            return last

        def p_pe(pe, b, c):
            if c == 0:
                pe.wait_ge(X_POOL.sem, X_POOL.count(b, f"x5{NG - 1}b"))
                if later(b):
                    pe.wait_ge(G_DVE.sem, G_DVE.count(b - 1, "ga"))
                for i in cs:
                    last = pe.matmul(PB[0][0:DEC, 0:T], d1[:, i, :], x5[:, GW, i, :], start=(i == 0), stop=(i == EC - 1))
                last.then_inc(P_PE.sem, 1)
                pe.wait_ge(P_ACT.sem, P_ACT.count(b, "dh"))
            else:
                pe.wait_ge(P_ACT.sem, P_ACT.count(b, f"k{c - 1}"))
            pe.matmul(PB[0][:, T:2 * T], d2[:, c * 128:(c + 1) * 128], dh[:, :], start=True, stop=True)
            project(pe, PB[0], 0, WK, GK, c).then_inc(P_PE.sem, 1)

        def p_pe_vr(pe, b, c):
            if c:
                pe.wait_ge(P_ACT.sem, P_ACT.count(b, f"r{c - 1}"))
            else:
                if later(b):
                    pe.wait_ge(G_DVE.sem, G_DVE.count(b - 1, "gb"))
            project(pe, PB[1], 0, WV, GV, c)
            project(pe, PB[1], 1, WR, GR, c).then_inc(P_PE.sem, 1)

        def p_act(act, b, c):
            if c == 0:
                if later(b):
                    act.wait_ge(P_PE.sem, P_PE.count(b - 1, f"zk{EC - 1}"))
                act.wait_ge(P_PE.sem, P_PE.count(b, "dh"))
                act.activation(dh[:, :], PB[0][0:DEC, 0:T], ACT.Tanh).then_inc(P_ACT.sem, 1)
            if later(b):
                act.wait_ge(S_DVE.sem, S_DVE.count(b - 1, f"scan{c}{S // 2 - 1}"))
            if c:
                act.wait_ge(P_ACT.sem, P_ACT.count(b, f"w{c - 1}"))
            else:
                if later(b):
                    act.wait_ge(P_ACT.sem, P_ACT.count(b - 1, f"w{EC - 1}"))
            act.wait_ge(P_PE.sem, P_PE.count(b, f"zk{c}"))
            act.activation(ez[:, :], PB[0][:, T:2 * T], ACT.Exp, bias=vcol("time_decay", c)).then_inc(P_ACT.sem, 1)
            act.wait_ge(P_ACT.sem, P_ACT.count(b, f"ez{c}"))
            act.activation(w_[:, c, :], ez[:, :], ACT.Exp, scale=-1.0).then_inc(P_ACT.sem, 1)
            act.activation(k_[:, c, :], PB[0][:, 0:T], ACT.Copy).then_inc(P_ACT.sem, 1)

        def p_act_vr(act, b, c):
            act.wait_ge(P_PE.sem, P_PE.count(b, f"vr{c}"))
            act.activation(v_[:, c, :], PB[1][:, 0:T], ACT.Copy).then_inc(P_ACT.sem, 1)
            if later(b):
                act.wait_ge(S_PE.sem, S_PE.count(b - 1, f"v{c}{S // 2 - 1}"))
            if later(b):
                act.wait_ge(P_DVE.sem, P_DVE.count(b - 1, f"vlo{c}"))
            act.activation(vhi[:, c, :], PB[1][:, 0:T], ACT.Copy).then_inc(P_ACT.sem, 1)
            if later(b):
                act.wait_ge(S_POOL.sem, S_POOL.count(b - 1, f"rs{c}{S // 2 - 1}"))
            act.activation(r_[:, c, :], PB[1][:, T:2 * T], ACT.Copy).then_inc(P_ACT.sem, 1)

        def p_dve(dve, b, c):
            dve.wait_ge(P_ACT.sem, P_ACT.count(b, f"vhi{c}"))
            if later(b):
                dve.wait_ge(S_PE.sem, S_PE.count(b - 1, f"v{c}{S // 2 - 1}"))
            dve.tensor_tensor(vlo[:, c, :], v_[:, c, :], vhi[:, c, :].bitcast(F32), ALU.subtract)\
               .then_inc(P_DVE.sem, 1)

        def g_pe(pe, b, h):
            pe.wait_ge(P_ACT.sem, P_ACT.count(b, f"{'kr'[h]}{EC - 1}"))
            project(pe, PB[h], 0, WG, GG, 2 * h)
            project(pe, PB[h], 1, WG, GG, 2 * h + 1).then_inc(G_PE.sem, 1)

        def g_act(act, b, h):
            if h:
                act.wait_ge(G_DVE.sem, G_DVE.count(b, "ga"))
            else:
                if later(b):
                    act.wait_ge(G_DVE.sem, G_DVE.count(b - 1, "gb"))
            act.wait_ge(G_PE.sem, G_PE.count(b, f"g{halves[h]}"))
            act.activation(th[:, :, :], PB[h][:, :].rearrange("p (c t) -> p c t", c=2), ACT.Tanh, scale=0.5)\
               .then_inc(G_ACT.sem, 1)

        def g_dve(dve, b, h):
            if h == 0:
                if later(b):
                    dve.wait_ge(N_DVE.sem, N_DVE.count(b - 1, "gate"))
            dve.wait_ge(G_ACT.sem, G_ACT.count(b, f"th{halves[h]}"))
            dve.scalar_tensor_tensor(g2[:, 2 * h:2 * h + 2, :], th[:, :, :], 1.0,
                                     PB[h][:, :].rearrange("p (c t) -> p c t", c=2), ALU.add, ALU.mult)\
               .then_inc(G_DVE.sem, 1)

        def value_bank(c, e):
            return VBK[(c * NE + e) % 2]

        def s_values(pe, b, c, e):
            at = shifted(c, e, -2)
            if at[0] >= 0:
                pe.wait_ge(S_DVE.sem, S_DVE.count(b, "kv%d%d" % at))
            else:
                if later(b):
                    pe.wait_ge(S_DVE.sem, S_DVE.count(b - 1, "kv%d%d" % shifted(EC, e, -2)))
            if e == BONUS:
                pe.wait_ge(S_DVE.sem, S_DVE.count(b, f"ru{c}"))
                last = pe.matmul(value_bank(c, e)[:, 0:T], blk[:, 0, :], ru[:, :], start=True, stop=True)
            else:
                for n in range(2):
                    for part, v in enumerate((vhi, vlo)):
                        last = pe.matmul(value_bank(c, e)[:, n * T:(n + 1) * T], seli[:, 2 * e + n, :], v[:, c, :],
                                         start=(part == 0), stop=(part == 1))
            last.then_inc(S_PE.sem, 1)

        def s_pe_begin(pe, b):
            pe.wait_ge(P_DVE.sem, P_DVE.count(b, f"vlo{EC - 1}"))
            s_values(pe, b, 0, 0)
            s_values(pe, b, 0, 1)

        def s_pe(pe, b, c, e):
            if e == 0:
                if c:
                    pe.wait_ge(S_ACT.sem, S_ACT.count(b, f"sq{c - 1}"))
                else:
                    if later(b):
                        pe.wait_ge(S_ACT.sem, S_ACT.count(b - 1, f"sq{EC - 1}"))
            if e == BONUS:
                pe.wait_ge(S_DVE.sem, S_DVE.count(b, f"kv{c}{e}"))
                last = pe.matmul(AB[:, 0:T], blk[:, 1, :], zv[:, :], start=False, stop=True)
            else:
                pe.wait_ge(S_POOL.sem, S_POOL.count(b, f"rs{c}{e}"))
                for n in range(2):
                    last = pe.matmul(AB[:, 0:T], selo[:, 2 * e + n, :], rs[:, e % 2, n, :],
                                     start=(e == 0 and n == 0), stop=False)
            last.then_inc(S_PE.sem, 1)
            if shifted(c, e, 2)[0] < EC:
                s_values(pe, b, *shifted(c, e, 2))

        def s_dve(dve, b, c, e):
            if c == 0 and e == 0:
                dve.wait_ge(P_ACT.sem, P_ACT.count(b, f"r{EC - 1}"))
                dve.wait_ge(s0_in, 16 * b + 16)
                if later(b):
                    dve.wait_ge(S_DVE.sem, S_DVE.count(b - 1, f"kv{EC - 1}{BONUS}"))
            dve.wait_ge(S_PE.sem, S_PE.count(b, f"v{c}{e}"))
            if e == BONUS:
                if c:
                    dve.wait_ge(S_PE.sem, S_PE.count(b, f"o{c - 1}{e}"))
                else:
                    if later(b):
                        dve.wait_ge(S_PE.sem, S_PE.count(b - 1, f"o{EC - 1}{e}"))
                dve.tensor_tensor(zv[:, :], value_bank(c, e)[:, 0:T], v_[:, c, :], ALU.mult).then_inc(S_DVE.sem, 1)
                return
            if e >= 2:
                dve.wait_ge(S_DVE.sem, S_DVE.count(b, f"scan{c}{e - 2}"))
            elif c:
                dve.wait_ge(S_DVE.sem, S_DVE.count(b, f"scan{c - 1}{BONUS - 2 + e}"))
            dve.tensor_tensor(kv[:, e % 2], value_bank(c, e)[:, :].rearrange("p (e t) -> p e t", e=2),
                              k_[:, c, :].unsqueeze(1).broadcast_to([128, 2, T]), ALU.mult)\
               .then_inc(S_DVE.sem, 1)
            dve.wait_ge(S_DVE.sem, S_DVE.count(b, f"kv{c}{e}"))
            if e >= 2:
                dve.wait_ge(S_POOL.sem, S_POOL.count(b, f"rs{c}{e - 2}"))
            elif c:
                dve.wait_ge(S_POOL.sem, S_POOL.count(b, f"rs{c - 1}{BONUS - 2 + e}"))
            else:
                if later(b):
                    dve.wait_ge(S_POOL.sem, S_POOL.count(b - 1, f"rs{EC - 1}{BONUS - 2 + e}"))
            for n in range(2):
                d = 2 * e + n
                last = dve.tensor_tensor_scan(st[:, e % 2, n, 1:T + 1], w_[:, c, :], kv[:, e % 2, n, :],
                                              s0t[:, c, d:d + 1], ALU.mult, ALU.add)
            last.then_inc(S_DVE.sem, 1)
            if e == 1:
                if c:
                    dve.wait_ge(S_PE.sem, S_PE.count(b, f"v{c - 1}{BONUS}"))
                else:
                    if later(b):
                        dve.wait_ge(S_PE.sem, S_PE.count(b - 1, f"v{EC - 1}{BONUS}"))
                dve.scalar_tensor_tensor(ru[:, :], r_[:, c, :], vcol("bonus", c), k_[:, c, :], ALU.mult, ALU.mult)\
                   .then_inc(S_DVE.sem, 1)

        def s_pool(pool, b, c, q):
            if q == BONUS:
                return
            if c == 0 and q == 0:
                pool.wait_ge(s0_in, 16 * b + 16)
                pool.wait_ge(P_ACT.sem, P_ACT.count(b, f"r{EC - 1}"))
            if q >= 2:
                pool.wait_ge(S_POOL.sem, S_POOL.count(b, f"rs{c}{q - 2}"))
            elif c:
                pool.wait_ge(S_POOL.sem, S_POOL.count(b, f"rs{c - 1}{S // 2 - 2 + q}"))
            else:
                if later(b):
                    pool.wait_ge(S_POOL.sem, S_POOL.count(b - 1, f"rs{EC - 1}{S // 2 - 2 + q}"))
            alone(pool, passed)
            pool.tensor_copy(st[:, q % 2, :, 0], s0t[:, c, 2 * q:2 * q + 2]).then_inc(S_POOL.sem, 1)
            pool.wait_ge(S_POOL.sem, S_POOL.count(b, f"s0{c}{q}"))
            pool.wait_ge(S_DVE.sem, S_DVE.count(b, f"scan{c}{q}"))
            if q >= 2:
                pool.wait_ge(S_PE.sem, S_PE.count(b, f"o{c}{q - 2}"))
            elif c:
                pool.wait_ge(S_PE.sem, S_PE.count(b, f"o{c - 1}{S // 2 - 2 + q}"))
            else:
                if later(b):
                    pool.wait_ge(S_PE.sem, S_PE.count(b - 1, f"o{EC - 1}{S // 2 - 2 + q}"))
            pool.tensor_tensor(rs[:, q % 2], st[:, q % 2, :, 0:T],
                               r_[:, c, :].unsqueeze(1).broadcast_to([128, 2, T]), ALU.mult)\
                .then_inc(S_POOL.sem, 1)

        def s_act(act, b, c, e):
            if e < BONUS:
                return
            if c == 0:
                if later(b):
                    act.wait_ge(K_PE.sem, K_PE.count(b - 1, "wo1"))
                if later(b):
                    act.wait_ge(N_DVE.sem, N_DVE.count(b - 1, "norm"))
            act.wait_ge(S_PE.sem, S_PE.count(b, f"o{c}{BONUS}"))
            act.activation(att[:, c, :], AB[:, 0:T], ACT.Copy).then_inc(S_ACT.sem, 1)
            act.activation(sq[:, c, :], AB[:, 0:T], ACT.Square).then_inc(S_ACT.sem, 1)

        def n_pe(pe, b, h):
            if h:
                pe.wait_ge(N_ACT.sem, N_ACT.count(b, "sda"))
            else:
                if later(b):
                    pe.wait_ge(K_DVE.sem, K_DVE.count(b - 1, "rv1"))
            pe.wait_ge(S_ACT.sem, S_ACT.count(b, f"sq{2 * h + 1}"))
            for c in (2 * h, 2 * h + 1):
                last = pe.matmul(KB[:, (c % 2) * T:(c % 2 + 1) * T], blk[:, 2, :], sq[:, c, :],
                                 start=True, stop=True)
            last.then_inc(N_PE.sem, 1)

        def n_act(act, b, h):
            act.wait_ge(N_PE.sem, N_PE.count(b, f"var{halves[h]}"))
            act.activation(sq[:, 2 * h:2 * h + 2, :], KB[:, :].rearrange("p (c t) -> p c t", c=2), ACT.Sqrt,
                           bias=small[:, 0:1]).then_inc(N_ACT.sem, 1)

        def n_dve(dve, b):
            dve.wait_ge(N_ACT.sem, N_ACT.count(b, "sdb"))
            dve.reciprocal(sq[:, :, :], sq[:, :, :]).then_inc(N_DVE.sem, 1)
            dve.wait_ge(N_DVE.sem, N_DVE.count(b, "rstd"))
            dve.tensor_tensor(att[:, :, :], att[:, :, :], sq[:, :, :], ALU.mult).then_inc(N_DVE.sem, 1)
            dve.wait_ge(N_DVE.sem, N_DVE.count(b, "norm"))
            for c in cs:
                last = dve.tensor_scalar(att[:, c, :], att[:, c, :], half_gn[:, 0, c:c + 1], half_gn[:, 1, c:c + 1],
                                         ALU.mult, ALU.add)
            last.then_inc(N_DVE.sem, 1)
            dve.wait_ge(N_DVE.sem, N_DVE.count(b, "affine"))
            dve.wait_ge(G_DVE.sem, G_DVE.count(b, "gb"))
            dve.tensor_tensor(att[:, :, :], att[:, :, :], g2[:, :, :], ALU.mult).then_inc(N_DVE.sem, 1)

        def k_pe_wo(pe, b, j):
            if j:
                pe.wait_ge(K_DVE.sem, K_DVE.count(b, "x10"))
            else:
                pe.wait_ge(N_DVE.sem, N_DVE.count(b, "gate"))
                pe.wait_ge(N_ACT.sem, N_ACT.count(b, "sdb"))
            for c in cs:
                last = pe.matmul(KB[:, :], att[:, c, j * 128:(j + 1) * 128], W[:, WO, c, :],
                                 start=(c == 0), stop=(c == EC - 1))
            last.then_inc(K_PE.sem, 1)

        def k_pe2(pe, b):
            pe.wait_ge(K_DVE.sem, K_DVE.count(b, "norm"))
            for h in range(2):
                if h:
                    pe.wait_ge(K_ACT.sem, K_ACT.count(b, "xn1"))
                for c in (2 * h, 2 * h + 1):
                    for j in range(TJ):
                        o = (c % 2) * T + j * 128
                        last = pe.transpose(KB[:, o:o + 128], xl[:, j, c * 128:(c + 1) * 128], idn[:, :])
                last.then_inc(K_PE.sem, 1)

        def k_pe_fk(pe, b, h):
            if h:
                pe.wait_ge(K_ACT.sem, K_ACT.count(b, "relua"))
            else:
                pe.wait_ge(K_DVE.sem, K_DVE.count(b, "xk"))
                pe.wait_ge(K_ACT.sem, K_ACT.count(b, "xn3"))
            for c in (2 * h, 2 * h + 1):
                for i in cs:
                    last = pe.matmul(KB[:, (c % 2) * T:(c % 2 + 1) * T], W[:, FWK, i, c * 128:(c + 1) * 128],
                                     xk[:, i, :], start=(i == 0), stop=(i == EC - 1))
            last.then_inc(K_PE.sem, 1)

        def k_pe_fr(pe, b, j):
            if j == 0:
                pe.wait_ge(K_DVE.sem, K_DVE.count(b, "xr"))
            pe.wait_ge(K_ACT.sem, K_ACT.count(b, "relub" if j == 0 else "th0"))
            for c in cs:
                last = pe.matmul(KB[:, :], xr[:, c, j * 128:(j + 1) * 128], W[:, FWR, c, :],
                                 start=(c == 0), stop=(c == EC - 1))
            last.then_inc(K_PE.sem, 1)

        def k_pe_fv(pe, b, j):
            if j == 0:
                pe.wait_ge(K_ACT.sem, K_ACT.count(b, "th1"))
            else:
                pe.wait_ge(K_DVE.sem, K_DVE.count(b, "rv0"))
            for c in cs:
                last = pe.matmul(KB[:, :], kk[:, c, j * 128:(j + 1) * 128], W[:, FWV, c, :],
                                 start=(c == 0), stop=(c == EC - 1))
            last.then_inc(K_PE.sem, 1)

        def k_act1(act, b):
            if later(b):
                act.wait_ge(K_DVE.sem, K_DVE.count(b - 1, "xr"))
            for c in cs:
                act.wait_ge(K_PE.sem, K_PE.count(b, "turn_a" if c < 2 else "turn_b"))
                act.activation(xn2[:, c, 1:T + 1], KB[:, (c % 2) * T:(c % 2 + 1) * T], ACT.Identity,
                               bias=vcol("ln2_b", c), scale=vcol("ln2_w", c)).then_inc(K_ACT.sem, 1)

        def k_act_fk(act, b, h):
            if h == 0:
                if later(b):
                    act.wait_ge(K_PE.sem, K_PE.count(b - 1, "fv1"))
            kh = kk[:, 2 * h:2 * h + 2, :]
            act.wait_ge(K_PE.sem, K_PE.count(b, f"fk{halves[h]}"))
            act.activation(kh, KB[:, :].rearrange("p (c t) -> p c t", c=2), ACT.Relu).then_inc(K_ACT.sem, 1)
            act.wait_ge(K_ACT.sem, K_ACT.count(b, f"relu{halves[h]}"))
            act.activation(kh, kh, ACT.Square).then_inc(K_ACT.sem, 1)

        def k_act_fr(act, b, j):
            act.wait_ge(K_PE.sem, K_PE.count(b, f"fr{j}"))
            act.activation(tr[:, j, :], KB[:, :], ACT.Tanh, scale=0.5).then_inc(K_ACT.sem, 1)

        def k_dve_wo(dve, b, j):
            if j == 0:
                dve.wait_ge(x1_in, 32 * b + 32)
            dve.wait_ge(K_PE.sem, K_PE.count(b, f"wo{j}"))
            dve.tensor_tensor(x1[:, j, :], x1[:, j, :], KB[:, :], ALU.add).then_inc(K_DVE.sem, 1)

        def k_dve_stat(dve, b):
            dve.wait_ge(K_DVE.sem, K_DVE.count(b, "x11"))
            for j in range(TJ):
                last = dve.bn_stats(stat2[:, j, :], x1[:, j, :])
            last.then_inc(K_DVE.sem, 1)
            dve.wait_ge(K_DVE.sem, K_DVE.count(b, "stat"))
            alone(dve, passed)
            for j in range(TJ):
                last = dve.bn_aggr(mv2[:, j, :], stat2[:, j, :])
            last.then_inc(K_DVE.sem, 1)

        def k_dve_norm(dve, b):
            dve.wait_ge(K_DVE.sem, K_DVE.count(b, "mean"))
            dve.wait_ge(K_POOL.sem, K_POOL.count(b, "rstd"))
            for j in range(TJ):
                last = dve.tensor_scalar(xl[:, j, :], x1[:, j, :], mv2[:, j, 0:1], rstd2[:, j:j + 1],
                                         ALU.subtract, ALU.mult)
            last.then_inc(K_DVE.sem, 1)

        def k_dve2(dve, b):
            dve.tensor_copy(xn2[:, :, 0], pr2[:, :]).then_inc(K_DVE.sem, 1)
            dve.wait_ge(K_DVE.sem, K_DVE.count(b, "prev"))
            dve.wait_ge(K_ACT.sem, K_ACT.count(b, "xn3"))
            dve.tensor_tensor(sx2, xn2[:, :, 0:T], xn2[:, :, 1:T + 1], ALU.subtract).then_inc(K_DVE.sem, 1)
            dve.wait_ge(K_DVE.sem, K_DVE.count(b, "shift"))
            if later(b):
                dve.wait_ge(K_PE.sem, K_PE.count(b - 1, "fr1"))
            if later(b):
                dve.wait_ge(saved, 16 * b)
            for name, dst in (("ffn_maa_k", xk), ("ffn_maa_r", xr)):
                for c in cs:
                    last = dve.scalar_tensor_tensor(dst[:, c, :], sx2[:, c, :], vcol(name, c), xn2[:, c, 1:T + 1],
                                                    ALU.mult, ALU.add)
                last.then_inc(K_DVE.sem, 1)

        def k_dve_fv(dve, b, j):
            dve.wait_ge(K_ACT.sem, K_ACT.count(b, f"th{j}"))
            dve.wait_ge(K_PE.sem, K_PE.count(b, f"fv{j}"))
            dve.scalar_tensor_tensor(tr[:, j, :], tr[:, j, :], 1.0, KB[:, :], ALU.add, ALU.mult)\
               .then_inc(K_DVE.sem, 1)
            dve.wait_ge(K_DVE.sem, K_DVE.count(b, f"rv{j}"))
            dve.scalar_tensor_tensor(tr[:, j, :], tr[:, j, :], 0.5, x1[:, j, :], ALU.mult, ALU.add)\
               .then_inc(K_DVE.sem, 1)

        def k_pool(pool, b):
            if later(b):
                pool.wait_ge(K_DVE.sem, K_DVE.count(b - 1, "norm"))
            pool.wait_ge(K_DVE.sem, K_DVE.count(b, "mean"))
            alone(pool, passed)
            pool.tensor_scalar(ve2[:, :], mv2[:, :, 1], 1.0, EPS, ALU.mult, ALU.add).then_inc(K_POOL.sem, 1)
            pool.wait_ge(K_POOL.sem, K_POOL.count(b, "eps"))
            pool.tensor_tensor(rstd2[:, :], ve2[:, :], mhalf[:, :], ALU.pow).then_inc(K_POOL.sem, 1)

        LAG = 2
        SLOTS = {
            -1: [("X_mix", 1, 0)],
            0: [("wo", -1, 0)], 1: [("X_mix", 1, 1)], 2: [("X_mix", 1, 2)], 3: [("wo", -1, 1)],
            4: [("k_stat", -1), ("X_mix", 1, 3)], 5: [("k_norm", -1)], 6: [("X_mix", 1, 4)], 7: [("k_turn", -1)],
            8: [("P_zk", 1, 0), ("k_shift", -1)], 10: [("P_vr", 1, 0)], 12: [("fk", -1, 0)], 14: [("fk", -1, 1)],
            17: [("P_zk", 1, 1)], 18: [("X_stat", 2)], 19: [("P_vr", 1, 1)], 20: [("X_norm", 2)],
            21: [("fr", -1, 0)], 22: [("X_turn", 2)], 23: [("fr", -1, 1)], 24: [("X_shift", 2)],
            26: [("P_zk", 1, 2)], 28: [("P_vr", 1, 2)], 30: [("fv", -1, 0)], 32: [("fv", -1, 1)], 33: [("save", -1)],
        }
        TAIL = [("P_zk", 1, 3), ("X_xx", 2), ("N", 0, 0), ("N", 0, 1), ("P_vr", 1, 3), ("X_hid", 2), ("S_begin", 1),
                ("G", 1, 0), ("G", 1, 1), ("N_out", 0), ("G_out", 1, 0), ("G_out", 1, 1)]

        def round_a(eng, p, i, lag):
            def do(name, ahead, *more):
                b = i + ahead
                if name in p and (not isinstance(b, int) or 0 <= b < B):
                    p[name](eng, b, *more)

            do("s0", 0)
            do("x", 2)
            do("x1", -1)
            for slot in range(-1, len(elements) + lag):
                if 0 <= slot < len(elements):
                    do("S", 0, *elements[slot])
                for name, ahead, *more in SLOTS.get(slot - lag, ()):
                    do(name, ahead, *more)
            for name, ahead, *more in TAIL:
                do(name, ahead, *more)

        def phase_a(eng, p, lag=0):
            def do(name, b, *more):
                if name in p:
                    p[name](eng, b, *more)

            for b in range(2):
                do("x", b)
                for name in ("X_stat", "X_norm", "X_turn", "X_shift"):
                    do(name, b)
                if b:
                    for c in cs:
                        do("P_zk", 0, c)
                        do("P_vr", 0, c)
                do("X_xx", b)
                do("X_hid", b)
                if b:
                    do("S_begin", 0)
                    for h in range(2):
                        do("G", 0, h)
                        do("G_out", 0, h)
                else:
                    for g in range(NG):
                        do("X_mix", 0, g)
            round_a(eng, p, 0, lag)
            round_a(eng, p, 1, lag)
            with eng.Fori(2, B - 2) as i:
                round_a(eng, p, i, lag)
            round_a(eng, p, B - 2, lag)
            do("first_b", B - 1)
            round_a(eng, p, B - 1, lag)
            do("x1", B - 1)
            for name, *more in (("wo", 0), ("wo", 1), ("k_stat",), ("k_norm",), ("k_turn",), ("k_shift",),
                                ("fk", 0), ("fk", 1), ("fr", 0), ("fr", 1), ("fv", 0), ("fv", 1), ("save",)):
                do(name, B - 1, *more)

        a_done = [X_PE, X_ACT, X_DVE, X_POOL, P_PE, P_ACT, P_DVE, G_PE, G_ACT, G_DVE, S_PE, S_DVE, S_POOL,
                  S_ACT, N_PE, N_ACT, N_DVE, K_PE, K_ACT, K_DVE, K_POOL]

        def end_a(eng):
            for s in a_done:
                eng.wait_ge(s.sem, B * s.per)
            eng.wait_ge(saved, 16 * B)

        ca.close()
        cb = ctx.enter_context(ExitStack())
        Wp = sb(cb, "Wp", [128, 4, EC, E])
        vb = sb(cb, "vb", [128, len(VB), EC])
        fcb = sb(cb, "fcb", [128, FC])
        rows = sb(cb, "rows", [128, 3, E])
        mhalf_b = sb(cb, "mhalf_b", [128, TJ])
        h_in = sb(cb, "h_in", [128, TJ, E])
        cx = sb(cb, "cx", [128, EC, T])
        mk8 = sb(cb, "mk8", [128, T], U8)
        mneg = sb(cb, "mneg", [128, T])
        bstat = sb(cb, "bstat", [128, TJ, 6])
        bmv = sb(cb, "bmv", [128, TJ, 2])
        bve = sb(cb, "bve", [128, TJ])
        brstd = sb(cb, "brstd", [128, TJ])
        hl = sb(cb, "hl", [128, TJ, E])
        hn = sb(cb, "hn", [128, EC, T])
        qt = sb(cb, "qt", [128, EC, T])
        kt = sb(cb, "kt", [128, EC, T])
        vt = sb(cb, "vt", [128, TJ, E])
        sc = sb(cb, "sc", [128, 2, TJ, T])
        pt = sb(cb, "pt", [128, 2, 2, T])
        mx = sb(cb, "mx", [128, 2, TJ])
        nmx = sb(cb, "nmx", [128, 2, TJ])
        den = sb(cb, "den", [128, TJ, AH])
        ao = sb(cb, "ao", [128, TJ, E])
        aot = sb(cb, "aot", [128, EC, T])
        hb = sb(cb, "hb", [128, TJ, E])
        hid = sb(cb, "hid", [128, TJ, E])
        hp = sb(cb, "hp", [128, TJ, E])
        gl = sb(cb, "gl", [128, FC, T])
        res = sb(cb, "res", [128, TJ, E])
        Wq = W[:, 0:4]
        FCW = 4

        b_in1 = sem("b_in1")
        b_in2 = sem("b_in2")
        q_in = sem("q_in")
        hc_in = sem("hc_in")
        stored = sem("stored")
        b_const = sem("b_const")
        hs = range(AH)
        L_PE = steps("L_PE", ["turn_a", "turn_b", "q_a", "k_a", "q_b", "k_b", "v0", "v1"])
        L_ACT = steps("L_ACT", [f"hn{c}" for c in cs] + ["q0", "q1", "k0", "k1", "q2", "q3", "k2", "k3"])
        L_DVE = steps("L_DVE", ["stat", "mean", "norm", "mask", "v0", "v1"])
        L_POOL = steps("L_POOL", ["eps", "rstd", "hb"])
        A_PE = steps("A_PE", [n for h in range(AH + 2) for n in ([f"s{h}"] if h < AH else [])
                              + ([f"t{h - 1}"] if 1 <= h <= AH else []) + ([f"o{h - 2}"] if h >= 2 else [])])
        A_ACT = steps("A_ACT", [n for h in range(AH) for n in (f"e{h}",)])
        A_DVE = steps("A_DVE", [n for h in range(AH + 1) for n in ([f"m{h}", f"n{h}"] if h < AH else [])
                                + ([f"p{h - 1}"] if h else [])])
        C_PE = steps("C_PE", ["turn_a", "turn_b", "c0", "c1", "nturn_a", "nturn_b"] + [f"f{n}" for n in range(FC // 2)]
                     + ["p0", "p1"])
        C_DVE = steps("C_DVE", ["rden", "ao", "hid0", "hid1", "stat", "mean", "norm", "out0", "out1"])
        C_ACT = steps("C_ACT", ["aot_a", "aot_b"] + [f"yn{c}" for c in cs] + [f"g{c}" for c in range(FC)])
        C_POOL = steps("C_POOL", ["eps", "rstd", "hp"])
        LB, SB, TBK, OB, CB = banks[0:2], banks[2:4], banks[4], banks[5:7], banks[7]

        FB = [CB, SB[0], SB[1], TBK]

        def bcol(name, c):
            return vb[:, VB.index(name), c:c + 1]

        def sp_hc(sp, b):
            if later(b):
                sp.wait_ge(L_DVE.sem, L_DVE.count(b - 1, "mask"))
            if later(b):
                sp.wait_ge(L_POOL.sem, L_POOL.count(b - 1, "hb"))
            if later(b):
                sp.wait_ge(L_PE.sem, L_PE.count(b - 1, "v1"))
            sp.dma_start(h_in[:, :, :], scratch[b].rearrange("(j p) e -> p j e", p=128)).then_inc(hc_in, 16)
            sp.dma_start(cx[:, :, :], ctxt[b].rearrange("(c p) t -> p c t", p=128)).then_inc(hc_in, 16)
            sp.dma_start(mk8[:, :], mask[b].partition_broadcast(128)).then_inc(hc_in, 16)

        def sp_out(sp, b):
            sp.wait_ge(C_DVE.sem, C_DVE.count(b, "out1"))
            sp.dma_start(out[b].rearrange("(j p) e -> p j e", p=128), res[:, :, :]).then_inc(stored, 16)

        def l_pe(pe, b):
            pe.wait_ge(L_DVE.sem, L_DVE.count(b, "norm"))
            if later(b):
                pe.wait_ge(L_DVE.sem, L_DVE.count(b - 1, "v1"))
            for h in range(2):
                for c in (2 * h, 2 * h + 1):
                    for j in range(TJ):
                        o = (c % 2) * T + j * 128
                        last = pe.transpose(LB[h][:, o:o + 128], hl[:, j, c * 128:(c + 1) * 128], idn[:, :])
                last.then_inc(L_PE.sem, 1)

        def l_pe_qk(pe, b, slot, h):
            pe.wait_ge(L_ACT.sem, L_ACT.count(b, f"{'qk'[slot]}1" if h else "hn3"))
            for c in (2 * h, 2 * h + 1):
                for i in cs:
                    last = pe.matmul(LB[slot][:, (c % 2) * T:(c % 2 + 1) * T], Wq[:, slot, i, c * 128:(c + 1) * 128],
                                     (hn, cx)[slot][:, i, :], start=(i == 0), stop=(i == EC - 1))
            last.then_inc(L_PE.sem, 1)

        def l_pe_v(pe, b, j):
            pe.wait_ge(L_ACT.sem, L_ACT.count(b, f"{'qk'[j]}3"))
            for c in cs:
                last = pe.matmul(LB[j][:, :], cx[:, c, j * 128:(j + 1) * 128], Wq[:, 2, c, :],
                                 start=(c == 0), stop=(c == EC - 1))
            last.then_inc(L_PE.sem, 1)

        def l_act(act, b):
            if later(b):
                act.wait_ge(L_PE.sem, L_PE.count(b - 1, "q_b"))
            for c in cs:
                act.wait_ge(L_PE.sem, L_PE.count(b, f"turn_{halves[c // 2]}"))
                act.activation(hn[:, c, :], LB[c // 2][:, (c % 2) * T:(c % 2 + 1) * T], ACT.Identity,
                               bias=bcol("ln1_b", c), scale=bcol("ln1_w", c)).then_inc(L_ACT.sem, 1)

        def l_act_qk(act, b, slot, h):
            if later(b):
                act.wait_ge(A_PE.sem, A_PE.count(b - 1, f"s{8 * h + 7}"))
            act.wait_ge(L_PE.sem, L_PE.count(b, f"{'qk'[slot]}_{halves[h]}"))
            for c in (2 * h, 2 * h + 1):
                act.activation((qt, kt)[slot][:, c, :], LB[slot][:, (c % 2) * T:(c % 2 + 1) * T], ACT.Identity,
                               bias=bcol(("q_b", "k_b")[slot], c)).then_inc(L_ACT.sem, 1)

        def l_dve(dve, b):
            dve.wait_ge(hc_in, 48 * b + 48)
            if later(b):
                dve.wait_ge(L_DVE.sem, L_DVE.count(b - 1, "mean"))
            for j in range(TJ):
                last = dve.bn_stats(bstat[:, j, :], h_in[:, j, :])
            last.then_inc(L_DVE.sem, 1)
            dve.wait_ge(L_DVE.sem, L_DVE.count(b, "stat"))
            if later(b):
                dve.wait_ge(L_POOL.sem, L_POOL.count(b - 1, "eps"))
            alone(dve, passed)
            for j in range(TJ):
                last = dve.bn_aggr(bmv[:, j, :], bstat[:, j, :])
            last.then_inc(L_DVE.sem, 1)

        def l_dve_norm(dve, b):
            dve.wait_ge(L_DVE.sem, L_DVE.count(b, "mean"))
            dve.wait_ge(L_POOL.sem, L_POOL.count(b, "rstd"))
            if later(b):
                dve.wait_ge(L_PE.sem, L_PE.count(b - 1, "turn_b"))
            for j in range(TJ):
                last = dve.tensor_scalar(hl[:, j, :], h_in[:, j, :], bmv[:, j, 0:1], brstd[:, j:j + 1],
                                         ALU.subtract, ALU.mult)
            last.then_inc(L_DVE.sem, 1)

        def l_dve_mask(dve, b):
            if later(b):
                dve.wait_ge(A_DVE.sem, A_DVE.count(b - 1, f"m{AH - 1}"))
            dve.tensor_scalar(mneg[:, :], mk8[:, :], 0.0, MASKED, ALU.is_equal, ALU.mult).then_inc(L_DVE.sem, 1)

        def l_dve_v(dve, b, j):
            if j == 0:
                if later(b):
                    dve.wait_ge(A_PE.sem, A_PE.count(b - 1, f"o{AH - 1}"))
            dve.wait_ge(L_PE.sem, L_PE.count(b, f"v{j}"))
            dve.tensor_tensor(vt[:, j, :], LB[j][:, :], rows[:, 0, :], ALU.add).then_inc(L_DVE.sem, 1)

        def l_pool(pool, b):
            if later(b):
                pool.wait_ge(L_DVE.sem, L_DVE.count(b - 1, "norm"))
            pool.wait_ge(L_DVE.sem, L_DVE.count(b, "mean"))
            alone(pool, passed)
            pool.tensor_scalar(bve[:, :], bmv[:, :, 1], 1.0, EPS, ALU.mult, ALU.add).then_inc(L_POOL.sem, 1)
            pool.wait_ge(L_POOL.sem, L_POOL.count(b, "eps"))
            pool.tensor_tensor(brstd[:, :], bve[:, :], mhalf_b[:, :], ALU.pow).then_inc(L_POOL.sem, 1)

        def l_pool_hb(pool, b):
            if later(b):
                pool.wait_ge(C_DVE.sem, C_DVE.count(b - 1, "hid1"))
            pool.wait_ge(L_DVE.sem, L_DVE.count(b, "norm"))
            pool.tensor_tensor(hb[:, :, :], h_in[:, :, :], rows[:, 1, :].unsqueeze(1).broadcast_to([128, TJ, E]), ALU.add)\
                .then_inc(L_POOL.sem, 1)

        def head(h):
            return h // 4, 32 * (h % 4)

        def a_pe(pe, b, h):
            if h == 0:
                pe.wait_ge(L_ACT.sem, L_ACT.count(b, f"k{EC - 1}"))
                pe.wait_ge(L_DVE.sem, L_DVE.count(b, "v1"))
                if later(b):
                    pe.wait_ge(C_ACT.sem, C_ACT.count(b - 1, f"g{FC - 1}"))
            if h < AH:
                c, p = head(h)
                if h >= 2:
                    pe.wait_ge(A_DVE.sem, A_DVE.count(b, f"m{h - 2}"))
                for j in range(TJ):
                    last = pe.matmul(SB[h % 2][:, j * T:(j + 1) * T], qt[p:p + HD, c, j * 128:(j + 1) * 128],
                                     kt[p:p + HD, c, :], start=True, stop=True)
                last.then_inc(A_PE.sem, 1)
            if 1 <= h <= AH:
                pe.wait_ge(A_ACT.sem, A_ACT.count(b, f"e{h - 1}"))
                if h >= 2:
                    pe.wait_ge(A_DVE.sem, A_DVE.count(b, f"p{h - 2}"))
                for i in range(2):
                    for j in range(TJ):
                        o = i * T + j * 128
                        last = pe.transpose(TBK[:, o:o + 128], sc[:, (h - 1) % 2, j, i * 128:(i + 1) * 128], idn[:, :])
                last.then_inc(A_PE.sem, 1)
            if h >= 2:
                g = h - 2
                pe.wait_ge(A_DVE.sem, A_DVE.count(b, f"p{g}"))
                if g == 0:
                    if later(b):
                        pe.wait_ge(C_DVE.sem, C_DVE.count(b - 1, "ao"))
                for j in range(TJ):
                    for i in range(2):
                        last = pe.matmul(OB[j][:, g * HD:(g + 1) * HD], pt[:, g % 2, i, j * 128:(j + 1) * 128],
                                         vt[:, i, g * HD:(g + 1) * HD], start=(i == 0), stop=(i == 1))
                last.then_inc(A_PE.sem, 1)

        def a_dve(dve, b, h):
            if h <= AH:
                if h < AH:
                    dve.wait_ge(A_PE.sem, A_PE.count(b, f"s{h}"))
                    if h >= 2:
                        dve.wait_ge(A_PE.sem, A_PE.count(b, f"t{h - 2}"))
                        dve.wait_ge(A_ACT.sem, A_ACT.count(b, f"e{h - 2}"))
                    else:
                        if later(b):
                            dve.wait_ge(A_PE.sem, A_PE.count(b - 1, f"t{AH - 2 + h}"))
                        if later(b):
                            dve.wait_ge(A_ACT.sem, A_ACT.count(b - 1, f"e{AH - 2 + h}"))
                    if h == 0:
                        dve.wait_ge(L_DVE.sem, L_DVE.count(b, "mask"))
                        if later(b):
                            dve.wait_ge(A_DVE.sem, A_DVE.count(b - 1, f"p{AH - 1}"))
                    alone(dve, passed)
                    for j in range(TJ):
                        last = dve.tensor_tensor_reduce(out=sc[:, h % 2, j, :], in0=SB[h % 2][:, j * T:(j + 1) * T],
                                                        in1=mneg[:, :], scale=1.0, scalar=MASKED, op0=ALU.add, op1=ALU.max,
                                                        accum_out=mx[:, h % 2, j:j + 1])
                    last.then_inc(A_DVE.sem, 1)
                    dve.wait_ge(A_DVE.sem, A_DVE.count(b, f"m{h}"))
                    dve.tensor_scalar(nmx[:, h % 2, :], mx[:, h % 2, :], -SCALE, None, ALU.mult).then_inc(A_DVE.sem, 1)
                if h:
                    dve.wait_ge(A_PE.sem, A_PE.count(b, f"t{h - 1}"))
                    if h >= 3:
                        dve.wait_ge(A_PE.sem, A_PE.count(b, f"o{h - 3}"))
                    elif h:
                        if later(b):
                            dve.wait_ge(A_PE.sem, A_PE.count(b - 1, f"o{AH - 3 + h}"))
                    dve.tensor_copy(pt[:, (h - 1) % 2], TBK[:, :].rearrange("p (i t) -> p i t", i=2))\
                       .then_inc(A_DVE.sem, 1)

        def a_act(act, b, h):
            if h == 0:
                if later(b):
                    act.wait_ge(C_DVE.sem, C_DVE.count(b - 1, "ao"))
            if h < AH:
                act.wait_ge(A_DVE.sem, A_DVE.count(b, f"n{h}"))
                for j in range(TJ):
                    last = act.activation(sc[:, h % 2, j, :], sc[:, h % 2, j, :], ACT.Exp, bias=nmx[:, h % 2, j:j + 1],
                                          scale=SCALE, accum_out=den[:, j, h:h + 1])
                last.then_inc(A_ACT.sem, 1)

        def turn_rows(pe, rows_of):
            for h in range(2):
                for c in (2 * h, 2 * h + 1):
                    for j in range(TJ):
                        o = (c % 2) * T + j * 128
                        last = pe.transpose(SB[h][:, o:o + 128], rows_of(j)[:, c * 128:(c + 1) * 128], idn[:, :])
                last.then_inc(C_PE.sem, 1)

        def c_pe_turn(pe, b):
            pe.wait_ge(C_DVE.sem, C_DVE.count(b, "ao"))
            turn_rows(pe, lambda j: ao[:, j, :])

        def c_pe_out(pe, b):
            if later(b):
                pe.wait_ge(C_DVE.sem, C_DVE.count(b - 1, "out1"))
            pe.wait_ge(C_ACT.sem, C_ACT.count(b, "aot_b"))
            for j in range(TJ):
                for c in cs:
                    last = pe.matmul((CB, TBK)[j][:, :], aot[:, c, j * 128:(j + 1) * 128], Wq[:, 3, c, :],
                                     start=(c == 0), stop=(c == EC - 1))
                last.then_inc(C_PE.sem, 1)

        def c_pe_nturn(pe, b):
            pe.wait_ge(C_DVE.sem, C_DVE.count(b, "norm"))
            turn_rows(pe, hl2)

        def hl2(j):
            return ao[:, j, :]

        def c_pe2(pe, b):
            if isinstance(b, int) and b == 0:
                pe.wait_ge(b_in2, 16 * len(loads_b2))
            pe.wait_ge(C_ACT.sem, C_ACT.count(b, "yn3"))
            for n in range(FC // 2):
                if n >= 4:
                    pe.wait_ge(C_ACT.sem, C_ACT.count(b, f"g{2 * n - 7}"))
                for c in (2 * n, 2 * n + 1):
                    for i in cs:
                        last = pe.matmul(FB[n % 4][:, (c % 2) * T:(c % 2 + 1) * T],
                                         W[:, FCW + c // 4, i, (c % 4) * 128:(c % 4 + 1) * 128],
                                         aot[:, i, :], start=(i == 0), stop=(i == EC - 1))
                last.then_inc(C_PE.sem, 1)

        def c_pe3(pe, b, n):
            j = n // 8
            if n == 0:
                pe.wait_ge(C_ACT.sem, C_ACT.count(b, f"g{FC - 1}"))
            elif n == 8:
                pe.wait_ge(C_DVE.sem, C_DVE.count(b, "out0"))
            for c in (2 * (n % 8), 2 * (n % 8) + 1):
                last = pe.matmul(CB[:, :], gl[:, c, j * 128:(j + 1) * 128], Wp[:, c // 4, c % 4, :],
                                 start=(c == 0), stop=(c == FC - 1))
            if n % 8 == 7:
                last.then_inc(C_PE.sem, 1)

        def c_dve1(dve, b):
            dve.wait_ge(A_ACT.sem, A_ACT.count(b, f"e{AH - 1}"))
            dve.reciprocal(den[:, :, :], den[:, :, :]).then_inc(C_DVE.sem, 1)
            dve.wait_ge(C_DVE.sem, C_DVE.count(b, "rden"))
            dve.wait_ge(A_PE.sem, A_PE.count(b, f"o{AH - 1}"))
            if later(b):
                dve.wait_ge(C_PE.sem, C_PE.count(b - 1, "nturn_b"))
            for j in range(TJ):
                last = dve.tensor_tensor(ao[:, j, :].rearrange("p (h d) -> p h d", h=AH),
                                         OB[j][:, :].rearrange("p (h d) -> p h d", h=AH),
                                         den[:, j, :].unsqueeze(2).broadcast_to([128, AH, HD]), ALU.mult)
            last.then_inc(C_DVE.sem, 1)

        def c_dve_hid(dve, b):
            dve.wait_ge(L_POOL.sem, L_POOL.count(b, "hb"))
            if later(b):
                dve.wait_ge(C_POOL.sem, C_POOL.count(b - 1, "hp"))
            for j in range(TJ):
                dve.wait_ge(C_PE.sem, C_PE.count(b, f"c{j}"))
                dve.tensor_tensor(hid[:, j, :], (CB, TBK)[j][:, :], hb[:, j, :], ALU.add).then_inc(C_DVE.sem, 1)
            dve.wait_ge(C_DVE.sem, C_DVE.count(b, "hid1"))
            for j in range(TJ):
                last = dve.bn_stats(bstat2[:, j, :], hid[:, j, :])
            last.then_inc(C_DVE.sem, 1)
            dve.wait_ge(C_DVE.sem, C_DVE.count(b, "stat"))
            alone(dve, passed)
            for j in range(TJ):
                last = dve.bn_aggr(bmv2[:, j, :], bstat2[:, j, :])
            last.then_inc(C_DVE.sem, 1)
            dve.wait_ge(C_DVE.sem, C_DVE.count(b, "mean"))
            dve.wait_ge(C_POOL.sem, C_POOL.count(b, "rstd"))
            for j in range(TJ):
                last = dve.tensor_scalar(ao[:, j, :], hid[:, j, :], bmv2[:, j, 0:1], brstd2[:, j:j + 1],
                                         ALU.subtract, ALU.mult)
            last.then_inc(C_DVE.sem, 1)

        def c_dve2(dve, b, n):
            if n % 8 < 7:
                return
            j = n // 8
            if j == 0:
                dve.wait_ge(C_POOL.sem, C_POOL.count(b, "hp"))
                if later(b):
                    dve.wait_ge(stored, 16 * b)
            dve.wait_ge(C_PE.sem, C_PE.count(b, f"p{j}"))
            dve.tensor_tensor(res[:, j, :], CB[:, :], hp[:, j, :], ALU.add).then_inc(C_DVE.sem, 1)

        def c_act1(act, b):
            if later(b):
                act.wait_ge(C_PE.sem, C_PE.count(b - 1, f"f{FC // 2 - 1}"))
            for h in range(2):
                act.wait_ge(C_PE.sem, C_PE.count(b, f"turn_{halves[h]}"))
                act.activation(aot[:, 2 * h:2 * h + 2, :], SB[h][:, :].rearrange("p (c t) -> p c t", c=2), ACT.Copy)\
                   .then_inc(C_ACT.sem, 1)

        def c_act_nturn(act, b):
            act.wait_ge(C_PE.sem, C_PE.count(b, "c1"))
            for c in cs:
                act.wait_ge(C_PE.sem, C_PE.count(b, f"nturn_{halves[c // 2]}"))
                act.activation(aot[:, c, :], SB[c // 2][:, (c % 2) * T:(c % 2 + 1) * T], ACT.Identity,
                               bias=bcol("ln2_b", c), scale=bcol("ln2_w", c)).then_inc(C_ACT.sem, 1)

        def c_act2(act, b):
            if later(b):
                act.wait_ge(C_PE.sem, C_PE.count(b - 1, "p1"))
            for c in range(FC):
                act.wait_ge(C_PE.sem, C_PE.count(b, f"f{c // 2}"))
                act.activation(gl[:, c, :], FB[c // 2 % 4][:, (c % 2) * T:(c % 2 + 1) * T], ACT.Gelu_apprx_tanh,
                               bias=fcb[:, c:c + 1]).then_inc(C_ACT.sem, 1)

        def c_pool(pool, b):
            if later(b):
                pool.wait_ge(C_DVE.sem, C_DVE.count(b - 1, "norm"))
            pool.wait_ge(C_DVE.sem, C_DVE.count(b, "mean"))
            alone(pool, passed)
            pool.tensor_scalar(bve2[:, :], bmv2[:, :, 1], 1.0, EPS, ALU.mult, ALU.add).then_inc(C_POOL.sem, 1)
            pool.wait_ge(C_POOL.sem, C_POOL.count(b, "eps"))
            pool.tensor_tensor(brstd2[:, :], bve2[:, :], mhalf_b[:, :], ALU.pow).then_inc(C_POOL.sem, 1)
            if later(b):
                pool.wait_ge(C_DVE.sem, C_DVE.count(b - 1, "out1"))
            pool.tensor_tensor(hp[:, :, :], hid[:, :, :], rows[:, 2, :].unsqueeze(1).broadcast_to([128, TJ, E]), ALU.add)\
                .then_inc(C_POOL.sem, 1)

        bstat2 = sb(cb, "bstat2", [128, TJ, 6])
        bmv2 = sb(cb, "bmv2", [128, TJ, 2])
        bve2 = sb(cb, "bve2", [128, TJ])
        brstd2 = sb(cb, "brstd2", [128, TJ])

        B_SLOTS = {h: [("C_mlp2", -1, h)] for h in range(8)} | {h: [("C_mlp2", -1, h - 1)] for h in range(9, 17)}
        B_SLOTS[2] += [("L_stat", 1)]
        B_SLOTS[3] += [("L_norm", 1)]
        B_SLOTS[5] += [("L_turn", 1)]
        B_SLOTS[8] = [("L_qk", 1, 0, 0)]
        B_SLOTS[16] += [("out", -1)]
        B_SLOTS[17] = [("L_qk", 1, 1, 0)]
        B_TAIL = [("C_ao", 0), ("L_mask", 1), ("L_qk", 1, 0, 1), ("C_turn", 0), ("L_qk", 1, 1, 1), ("C_out", 0),
                  ("C_hid", 0), ("L_v", 1, 0), ("C_nturn", 0), ("L_v", 1, 1), ("L_hb", 1), ("C_mlp1", 0)]

        def round_b(eng, p, i, lag):
            def do(name, ahead, *more):
                b = i + ahead
                if name in p and (not isinstance(b, int) or 0 <= b < B):
                    p[name](eng, b, *more)

            do("hc", 1)
            for slot in range(AH + 2 + lag):
                if slot < AH + 2:
                    do("A", 0, slot)
                for name, ahead, *more in B_SLOTS.get(slot - lag, ()):
                    do(name, ahead, *more)
            for name, ahead, *more in B_TAIL:
                do(name, ahead, *more)

        def phase_b(eng, p, lag=0):
            def do(name, b, *more):
                if name in p:
                    p[name](eng, b, *more)

            for name, *more in (("hc",), ("L_stat",), ("L_norm",), ("L_turn",), ("L_qk", 0, 0), ("L_qk", 1, 0), ("L_mask",),
                                ("L_qk", 0, 1), ("L_qk", 1, 1), ("L_v", 0), ("L_v", 1), ("L_hb",)):
                do(name, 0, *more)
            round_b(eng, p, 0, lag)
            round_b(eng, p, 1, lag)
            with eng.Fori(2, B - 1) as i:
                round_b(eng, p, i, lag)
            round_b(eng, p, B - 1, lag)
            for n in range(16):
                do("C_mlp2", B - 1, n)
            do("out", B - 1)

        block = ctx.enter_context(nc.Block())
        loads_a = [(W[:, n, :, :], w_a[n].rearrange("(c p) e -> p c e", p=128)) for n in range(8)]
        loads_a += [(va[:, :, :], vec_a), (m1[:, :, :], maa1.rearrange("(c p) n -> p c n", p=128)), (m2[:, :], maa2),
                    (m2b[:, :], maa2b), (d1[:, :, :], dec1.rearrange("(c p) n -> p c n", p=128)), (d2[:, :], dec2),
                    (idn[:, :], ident), (blk[:, :, :], blocks), (seli32, sel_in), (selo[:, :, :], sel_out)]
        loads_q = [(Wq[:, n, :, :], w_b[n].rearrange("(c p) e -> p c e", p=128)) for n in range(4)]
        loads_b = [(vb[:, :, :], vec_b), (fcb[:, :], fc_b)]
        loads_b += [(rows[:, n, :], rows_b[n].partition_broadcast(128)) for n in range(3)]
        loads_b2 = [(W[:, FCW + n, :, :], w_b[4 + n].rearrange("(c p) e -> p c e", p=128)) for n in range(4)]
        loads_b2 += [(Wp[:, n, :, :], w_b[8 + n].rearrange("(c p) e -> p c e", p=128)) for n in range(4)]

        def sp_first_b(sp, b):
            sp.wait_ge(G_PE.sem, G_PE.count(b, "gb"))
            for dst, src in loads_q:
                sp.dma_start(dst, src).then_inc(q_in, 16)

        @block.sync
        def _(sp):
            for dst, src in reversed(loads_a):
                sp.dma_start(dst, src).then_inc(weights_in, 16)
            phase_a(sp, {"x": sp_x, "s0": sp_s0, "x1": sp_x1, "save": sp_save, "first_b": sp_first_b})
            end_a(sp)
            for dst, src in loads_b:
                sp.dma_start(dst, src).then_inc(b_in1, 16)
            for dst, src in loads_b2:
                sp.dma_start(dst, src).then_inc(b_in2, 16)
            phase_b(sp, {"hc": sp_hc, "out": sp_out})
            sp.wait_ge(stored, 16 * B)

        @block.scalar
        def _(act):
            act.wait_ge(weights_in, 16 * len(loads_a))
            act.wait_ge(const_ready, 4)
            phase_a(act, {"X_turn": x_act1, "X_hid": x_act_hid, "P_zk": p_act, "P_vr": p_act_vr, "G": g_act,
                          "S": s_act, "N": n_act, "k_turn": k_act1, "fk": k_act_fk, "fr": k_act_fr})
            end_a(act)
            act.wait_ge(b_in1, 16 * len(loads_b))
            phase_b(act, {"L_turn": l_act, "L_qk": l_act_qk, "A": a_act, "C_turn": c_act1, "C_nturn": c_act_nturn,
                          "C_mlp1": c_act2})

        @block.vector
        def _(dve):
            dve.wait_ge(weights_in, 16 * len(loads_a))
            dve.tensor_scalar(half_gn[:, 0:1, :], va[:, VA.index("gn_w"):VA.index("gn_w") + 1, :], 0.5, None, ALU.mult)\
               .then_inc(const_ready, 1)
            dve.tensor_scalar(half_gn[:, 1:2, :], va[:, VA.index("gn_b"):VA.index("gn_b") + 1, :], 0.5, None, ALU.mult)\
               .then_inc(const_ready, 1)
            dve.tensor_copy(seli[:, :, :], seli32).then_inc(const_ready, 1)
            dve.memset(small[:, 0:1], EPS).then_inc(const_ready, 1)
            dve.wait_ge(const_ready, 4)
            phase_a(dve, {"X_stat": x_dve1, "X_norm": x_dve_norm, "X_shift": x_dve_shift, "X_xx": x_dve_xx,
                          "X_mix": x_dve2, "P_vr": p_dve, "G_out": g_dve, "S": s_dve, "N_out": n_dve,
                          "wo": k_dve_wo, "k_stat": k_dve_stat, "k_norm": k_dve_norm, "k_shift": k_dve2,
                          "fv": k_dve_fv}, LAG)
            end_a(dve)
            dve.wait_ge(b_in1, 16 * len(loads_b))
            phase_b(dve, {"L_stat": l_dve, "L_norm": l_dve_norm, "L_mask": l_dve_mask, "L_v": l_dve_v, "A": a_dve,
                          "C_ao": c_dve1, "C_hid": c_dve_hid, "C_mlp2": c_dve2}, 1)

        @block.gpsimd
        def _(pool):
            pool.memset(mhalf[:, :], -0.5).then_inc(b_const, 1)
            pool.wait_ge(b_const, 1)
            pool.wait_ge(weights_in, 16 * len(loads_a))
            phase_a(pool, {"X_stat": x_pool1, "X_mix": x_pool2, "S": s_pool, "k_stat": k_pool}, LAG)
            end_a(pool)
            pool.memset(mhalf_b[:, :], -0.5).then_inc(b_const, 1)
            pool.wait_ge(b_const, 2)
            pool.wait_ge(b_in1, 16 * len(loads_b))
            phase_b(pool, {"L_stat": l_pool, "L_hb": l_pool_hb, "C_hid": c_pool})

        @block.tensor
        def _(pe):
            pe.wait_ge(weights_in, 16 * len(loads_a))
            pe.wait_ge(const_ready, 4)
            phase_a(pe, {"X_turn": x_pe1, "X_hid": x_pe_hid, "X_mix": x_pe2, "P_zk": p_pe, "P_vr": p_pe_vr,
                         "G": g_pe, "S": s_pe, "S_begin": s_pe_begin, "N": n_pe, "wo": k_pe_wo, "k_turn": k_pe2,
                         "fk": k_pe_fk, "fr": k_pe_fr, "fv": k_pe_fv})
            end_a(pe)
            pe.wait_ge(q_in, 16 * len(loads_q))
            phase_b(pe, {"L_turn": l_pe, "L_qk": l_pe_qk, "L_v": l_pe_v, "A": a_pe, "C_turn": c_pe_turn,
                         "C_out": c_pe_out, "C_nturn": c_pe_nturn, "C_mlp1": c_pe2, "C_mlp2": c_pe3})


def kernel(**inputs):
    import numpy as np
    import concourse.bacc as bacc
    from concourse.bass_utils import run_bass_kernel_spmd

    a = {k: np.asarray(v) for k, v in inputs.items()}

    def l0(n):
        return a["L0_xattn_" + n]

    def l1(n):
        return a["L1_xattn_" + n]

    def cols(vectors):
        return np.ascontiguousarray(np.stack([v.reshape(EC, 128).T for v in vectors], axis=1))

    ctx_ = a["ctx_2048"]
    heads = np.arange(128) // S
    same = (heads[:, None] == heads[None, :]).astype(np.float32)
    index = np.arange(128) % S
    sel_in = same[:, None, :] * (index[:, None, None] == np.arange(S)[None, :, None]).astype(np.float32)
    sel_out = same[:, None, :] * ((index[None, None, :] == np.arange(S)[None, :, None]) - np.float32(1 / S)).astype(np.float32)
    arrays = {
        "x": a["x"],
        "prev1": np.ascontiguousarray(ctx_[:, 1, :].reshape(B, EC, 128).transpose(0, 2, 1)),
        "prev2": np.ascontiguousarray(ctx_[:, 0, :].reshape(B, EC, 128).transpose(0, 2, 1)),
        "s0": np.ascontiguousarray(ctx_[:, 2:2 + S, :].reshape(B, EC, 128, S).transpose(0, 2, 1, 3).reshape(B, 128, EC * S)),
        "ctxt": np.ascontiguousarray(ctx_.transpose(0, 2, 1)),
        "mask": a["mask_BxS2_bf1"].view(np.uint8),
        "vec_a": cols([l0("ln1_w"), l0("ln1_b"), l0("maa_x"), *l0("maa_stack"), l0("time_decay"),
                       l0("faaaa").reshape(E), l0("gn_w"), l0("gn_b"), l0("ln2_w"), l0("ln2_b"),
                       l0("ffn_maa_k"), l0("ffn_maa_r")]),
        "w_a": np.stack([np.ascontiguousarray(l0(n).T) for n in ("Wr", "Wk", "Wv", "Wg", "Wo", "ffn_Wk", "ffn_Wr", "ffn_Wv")]),
        "maa1": l0("maa_w1"),
        "maa2": np.ascontiguousarray(l0("maa_w2")[:4].reshape(4 * MAA, E)),
        "maa2b": np.ascontiguousarray(l0("maa_w2")[4]),
        "dec1": l0("decay_w1"),
        "dec2": l0("decay_w2"),
        "vec_b": cols([l1("ln1_w"), l1("ln1_b"), l1("q_b"), l1("k_b"), l1("ln2_w"), l1("ln2_b")]),
        "w_b": np.stack([l1("q_w"), l1("k_w"), l1("v_w"), l1("cproj_w")]
                        + [np.ascontiguousarray(l1("fc_w")[:, n * E:(n + 1) * E]) for n in range(4)]
                        + [l1("proj_w")[n * E:(n + 1) * E] for n in range(4)]),
        "fc_b": np.ascontiguousarray(l1("fc_b").reshape(FC, 128).T),
        "rows_b": np.stack([l1("v_b"), l1("cproj_b"), l1("proj_b")]),
        "ident": np.eye(128, dtype=np.float32),
        "blocks": np.ascontiguousarray(np.stack([same, np.eye(128, dtype=np.float32) - same / np.float32(S),
                                                 same / np.float32(S)], axis=1)),
        "sel_in": sel_in,
        "sel_out": sel_out,
    }
    nc = bacc.Bacc("TRN2", target_bir_lowering=False, num_devices=1)
    args = [nc.dram_tensor(f"in_{k}", v.shape, mybir.dt.from_np(v.dtype), kind="ExternalInput").ap()
            for k, v in arrays.items()]
    scratch = nc.dram_tensor("scratch", (B, T, E), F32, kind="Internal").ap()
    out = nc.dram_tensor("out_0", (B, T, E), F32, kind="ExternalOutput").ap()
    build(nc, *args, scratch, out)
    r = run_bass_kernel_spmd(nc, [{f"in_{k}": v for k, v in arrays.items()}], core_ids=[0])
    return r.results[0]["out_0"]
```

```python
from contextlib import ExitStack

import concourse.bass as bass
from concourse import mybir

F32 = mybir.dt.float32
F32R = mybir.dt.float32r
U8 = mybir.dt.uint8
ALU = mybir.AluOpType
ACT = mybir.ActivationFunctionType

B, T, E = 16, 256, 512
EC = E // 128
TJ = T // 128
S = 16
MAA, NG, DEC = 32, 5, 64
AH, HD = 16, 32
INNER = 4 * E
FC = INNER // 128
EPS = 1e-5
SCALE = HD ** -0.5
MASKED = -3.4028234663852886e38
GK, GW, GV, GR, GG = range(NG)

VA = ["ln1_w", "ln1_b", "maa_x", "maa_k", "maa_w", "maa_v", "maa_r", "maa_g", "time_decay", "bonus",
      "gn_w", "gn_b", "ln2_w", "ln2_b", "ffn_maa_k", "ffn_maa_r"]
VB = ["ln1_w", "ln1_b", "q_b", "k_b"]
VM = ["ln2_w", "ln2_b"]
QKVO = (1, 0, 2, 3)


def alone(eng, sem):
    eng.sem_inc(sem, 1)


class Steps:

    def __init__(self, sem, names):
        self.sem, self.names, self.per = sem, names, len(names)

    def count(self, b, name):
        return b * self.per + self.names.index(name) + 1


def later(b):
    return not isinstance(b, int) or b > 0


def build(nc, x, prev1, prev2, s0, ctxt, mask, vec_a, w_a, maa1, maa2, maa2b, dec1, dec2,
          vec_b, vec_m, w_b, fc_b, rows_b, ident, blocks, sel_in, sel_out, scratch, scratch2, out):
    ctx = ExitStack()
    with ctx:
        def sem(name):
            return ctx.enter_context(nc.semaphore(name))

        def steps(name, names):
            return Steps(sem(name), names)

        def sb(c, name, shape, dt=F32):
            return c.enter_context(nc.sbuf_tensor(name, shape, dt))

        W = sb(ctx, "W", [128, 6, EC, E])
        idn = sb(ctx, "idn", [128, 128])
        vb = sb(ctx, "vb", [128, len(VB), EC])
        small = sb(ctx, "small", [128, 24])
        banks = [ctx.enter_context(nc.psum_tensor(f"bank{i}", [128, 512], F32)) for i in range(8)]

        ca = ctx.enter_context(ExitStack())
        Wf = sb(ca, "Wf", [128, 2, EC, E])
        va = sb(ca, "va", [128, len(VA), EC])
        half_gn = sb(ca, "half_gn", [128, 2, EC])
        m1 = sb(ca, "m1", [128, EC, NG * MAA])
        m2 = sb(ca, "m2", [128, E])
        m2b = sb(ca, "m2b", [MAA, E])
        d1 = sb(ca, "d1", [128, EC, DEC])
        d2 = sb(ca, "d2", [DEC, E])
        blk = sb(ca, "blk", [128, 3, 128])
        seli = sb(ca, "seli", [128, S, 128], F32R)
        selo = sb(ca, "selo", [128, S, 128])
        mhalf = sb(ca, "mhalf", [128, TJ])
        x_t = sb(ca, "x_t", [128, TJ, E])
        stat = sb(ca, "stat", [128, TJ, 6])
        mv = sb(ca, "mv", [128, TJ, 2])
        ve = sb(ca, "ve", [128, TJ])
        rstd = sb(ca, "rstd", [128, TJ])
        pr1 = sb(ca, "pr1", [128, EC])
        xn = sb(ca, "xn", [128, EC, T + 1])
        sx = sb(ca, "sx", [128, EC, T])
        h1 = sb(ca, "h1", [128, T])
        h2 = sb(ca, "h2", [MAA, T])
        x5 = sb(ca, "x5", [128, NG, EC, T])
        xx = x5[:, 0]
        seli32 = x5[:, 0:2].rearrange("p g c (h t) -> p (g c h) t", h=2)
        dh = sb(ca, "dh", [DEC, T])
        ez = sb(ca, "ez", [128, T])
        w_ = sb(ca, "w_", [128, EC, T])
        k_ = sb(ca, "k_", [128, EC, T])
        r_ = sb(ca, "r_", [128, EC, T])
        v_ = sb(ca, "v_", [128, EC, T])
        vhi = sb(ca, "vhi", [128, EC, T], F32R)
        vlo = sb(ca, "vlo", [128, EC, T], F32R)
        th = sb(ca, "th", [128, 2, T])
        g2 = sb(ca, "g2", [128, EC, T])
        s0t = sb(ca, "s0t", [128, EC, S])
        ru = sb(ca, "ru", [128, T])
        zv = sb(ca, "zv", [128, T])
        kv = sb(ca, "kv", [128, 2, 2, T])
        st = sb(ca, "st", [128, 2, 2, T + 1])
        rs = sb(ca, "rs", [128, 2, 2, T])
        att = sb(ca, "att", [128, EC, T])
        sq = sb(ca, "sq", [128, EC, T])
        x1 = sb(ca, "x1", [128, TJ, E])
        stat2 = sb(ca, "stat2", [128, TJ, 6])
        mv2 = sb(ca, "mv2", [128, TJ, 2])
        ve2 = sb(ca, "ve2", [128, TJ])
        rstd2 = sb(ca, "rstd2", [128, TJ])
        pr2 = sb(ca, "pr2", [128, EC])
        xl = sb(ca, "xl", [128, TJ, E])
        xn2 = sb(ca, "xn2", [128, EC, T + 1])
        sx2 = xl[:, :, :].rearrange("p j (a t) -> p (j a) t", a=2)
        xk = sb(ca, "xk", [128, EC, T])
        xr = sb(ca, "xr", [128, EC, T])
        kk = sb(ca, "kk", [128, EC, T])
        tr = xk[:, :, :].rearrange("p (j a) t -> p j (a t)", a=2)

        def vcol(name, c):
            return va[:, VA.index(name), c:c + 1]

        WR, WK, WV, WG, WO, FWK, FWR, FWV = range(8)

        mix_in = sem("mix_in")
        proj_in = sem("proj_in")
        weights_in = sem("weights_in")
        const_ready = sem("const_ready")
        passed = sem("passed")
        x_in = sem("x_in")
        s0_in = sem("s0_in")
        x1_in = sem("x1_in")
        saved = sem("saved")
        halves = ["a", "b"]
        cs = range(EC)
        X_PE = steps("X_PE", ["turn_a", "turn_b", "hid"] + [f"mix{g}{h}" for g in range(NG) for h in halves])
        X_ACT = steps("X_ACT", [f"xn{c}" for c in cs] + ["h1", "h2"])
        X_DVE = steps("X_DVE", ["stat", "mean", "norm", "prev", "shift"] + [f"xx{c}" for c in cs]
                      + [f"mix{g}{c}" for g in range(NG) for c in cs])
        X_POOL = steps("X_POOL", ["eps", "rstd"] + [f"x5{g}{h}" for g in range(NG) for h in halves])
        P_PE = steps("P_PE", ["dh"] + [f"{n}{c}" for c in cs for n in ("zk", "vr")])
        P_ACT = steps("P_ACT", ["dh"] + [f"{n}{c}" for c in cs for n in ("ez", "w", "k", "v", "vhi", "r")])
        P_DVE = steps("P_DVE", [f"vlo{c}" for c in cs])
        G_PE = steps("G_PE", ["ga", "gb"])
        G_ACT = steps("G_ACT", ["tha", "thb"])
        G_DVE = steps("G_DVE", ["ga", "gb"])
        qs = range(S // 2)
        NE = S // 2 + 1
        BONUS = NE - 1
        elements = [(c, e) for c in cs for e in range(NE)]

        def shifted(c, e, by):
            n = c * NE + e + by
            return n // NE, n % NE

        S_PE = steps("S_PE", ["v00", "v01"] + [n for c, e in elements for n in
                                               [f"o{c}{e}"] + (["v%d%d" % shifted(c, e, 2)] if shifted(c, e, 2)[0] < EC else [])])
        S_DVE = steps("S_DVE", [n for c, e in elements for n in
                                [f"kv{c}{e}"] + ([f"scan{c}{e}"] if e < BONUS else []) + ([f"ru{c}"] if e == 1 else [])])
        S_POOL = steps("S_POOL", [n for c in cs for q in qs for n in (f"s0{c}{q}", f"rs{c}{q}")])
        S_ACT = steps("S_ACT", [n for c in cs for n in (f"att{c}", f"sq{c}")])
        N_PE = steps("N_PE", [f"var{h}" for h in halves])
        N_ACT = steps("N_ACT", [f"sd{h}" for h in halves])
        N_DVE = steps("N_DVE", [f"{n}{c}" for c in cs for n in ("rstd", "norm", "affine", "gate")])
        K_PE = steps("K_PE", ["wo0", "wo1", "turn_a", "turn_b"] + [f"fk{h}" for h in halves]
                     + ["fr0", "fr1", "fv0", "fv1"])
        K_ACT = steps("K_ACT", [f"xn{c}" for c in cs] + [f"{n}{h}" for h in halves for n in ("relu", "kk")]
                      + ["th0", "th1"])
        K_DVE = steps("K_DVE", ["x10", "x11", "stat", "mean", "norm", "prev", "shift", "xk", "xr"]
                      + [f"{n}{j}" for j in range(TJ) for n in ("rv", "out")])
        K_POOL = steps("K_POOL", ["eps", "rstd"])

        XB, PB, KB, VBK, AB = banks[0:2], banks[2:4], banks[4], banks[5:7], banks[7]


        def sp_x(sp, b):
            if later(b):
                sp.wait_ge(X_DVE.sem, X_DVE.count(b - 1, "prev"))
            if later(b):
                sp.wait_ge(X_PE.sem, X_PE.count(b - 1, "turn_b"))
            sp.dma_start(x_t[:, :, :], x[b].rearrange("(j p) e -> p j e", p=128)).then_inc(x_in, 16)
            sp.dma_start(pr1[:, :], prev1[b]).then_inc(x_in, 16)

        def sp_s0(sp, b):
            if later(b):
                sp.wait_ge(S_POOL.sem, S_POOL.count(b - 1, f"s0{EC - 1}{S // 2 - 1}"))
            if later(b):
                sp.wait_ge(S_DVE.sem, S_DVE.count(b - 1, f"scan{EC - 1}{S // 2 - 1}"))
            sp.dma_start(s0t[:, :, :], s0[b].rearrange("p (c d) -> p c d", c=EC)).then_inc(s0_in, 16)

        def sp_x1(sp, b):
            if later(b):
                sp.wait_ge(K_DVE.sem, K_DVE.count(b - 1, "out1"))
            sp.dma_start(x1[:, :, :], x[b].rearrange("(j p) e -> p j e", p=128)).then_inc(x1_in, 16)
            sp.dma_start(pr2[:, :], prev2[b]).then_inc(x1_in, 16)

        def sp_save(sp, b):
            sp.wait_ge(K_DVE.sem, K_DVE.count(b, "out1"))
            sp.dma_start(scratch[b].rearrange("(j p) e -> p j e", p=128), tr[:, :, :]).then_inc(saved, 16)

        def x_pe1(pe, b):
            pe.wait_ge(X_DVE.sem, X_DVE.count(b, "norm"))
            for h in range(2):
                if h == 0:
                    if later(b):
                        pe.wait_ge(X_DVE.sem, X_DVE.count(b - 1, f"mix{NG - 1}1"))
                else:
                    if later(b):
                        pe.wait_ge(X_DVE.sem, X_DVE.count(b - 1, f"mix{NG - 1}3"))
                for c in (2 * h, 2 * h + 1):
                    for j in range(TJ):
                        o = (c % 2) * T + j * 128
                        last = pe.transpose(XB[h][:, o:o + 128], x_t[:, j, c * 128:(c + 1) * 128], idn[:, :])
                last.then_inc(X_PE.sem, 1)

        def x_pe_hid(pe, b):
            pe.wait_ge(X_DVE.sem, X_DVE.count(b, "xx3"))
            pe.wait_ge(X_ACT.sem, X_ACT.count(b, "xn1"))
            for m, (o, n) in enumerate(((0, 128), (T, MAA))):
                for c in cs:
                    last = pe.matmul(XB[0][0:n, o:o + T], m1[:, c, 128 * m:128 * m + n], xx[:, c, :],
                                     start=(c == 0), stop=(c == EC - 1))
            last.then_inc(X_PE.sem, 1)

        def x_pe2(pe, b, g):
            if g == 0:
                pe.wait_ge(X_ACT.sem, X_ACT.count(b, "h2"))
            for h in range(2):
                if g:
                    pe.wait_ge(X_DVE.sem, X_DVE.count(b, f"mix{g - 1}{2 * h + 1}"))
                for c in (2 * h, 2 * h + 1):
                    wt = m2[MAA * g:MAA * (g + 1), c * 128:(c + 1) * 128] if g < 4 else m2b[:, c * 128:(c + 1) * 128]
                    hid = h1[MAA * g:MAA * (g + 1), :] if g < 4 else h2[:, :]
                    last = pe.matmul(XB[h][:, (c % 2) * T:(c % 2 + 1) * T], wt, hid, start=True, stop=True)
                last.then_inc(X_PE.sem, 1)

        def x_act1(act, b):
            if later(b):
                act.wait_ge(X_DVE.sem, X_DVE.count(b - 1, "shift"))
            if later(b):
                act.wait_ge(X_POOL.sem, X_POOL.count(b - 1, f"x5{NG - 1}b"))
            for c in cs:
                act.wait_ge(X_PE.sem, X_PE.count(b, "turn_a" if c < 2 else "turn_b"))
                act.activation(xn[:, c, 1:T + 1], XB[c // 2][:, (c % 2) * T:(c % 2 + 1) * T], ACT.Identity,
                               bias=vcol("ln1_b", c), scale=vcol("ln1_w", c)).then_inc(X_ACT.sem, 1)

        def x_act_hid(act, b):
            if later(b):
                act.wait_ge(X_PE.sem, X_PE.count(b - 1, f"mix{NG - 1}b"))
            act.wait_ge(X_PE.sem, X_PE.count(b, "hid"))
            act.activation(h1[:, :], XB[0][:, 0:T], ACT.Tanh).then_inc(X_ACT.sem, 1)
            act.activation(h2[:, :], XB[0][0:MAA, T:2 * T], ACT.Tanh).then_inc(X_ACT.sem, 1)

        def x_dve1(dve, b):
            if later(b):
                dve.wait_ge(X_DVE.sem, X_DVE.count(b - 1, f"mix{NG - 1}3"))
            dve.wait_ge(x_in, 32 * b + 32)
            for j in range(TJ):
                last = dve.bn_stats(stat[:, j, :], x_t[:, j, :])
            last.then_inc(X_DVE.sem, 1)
            if later(b):
                dve.wait_ge(X_POOL.sem, X_POOL.count(b - 1, "eps"))
            dve.wait_ge(X_DVE.sem, X_DVE.count(b, "stat"))
            alone(dve, passed)
            for j in range(TJ):
                last = dve.bn_aggr(mv[:, j, :], stat[:, j, :])
            last.then_inc(X_DVE.sem, 1)

        def x_dve_norm(dve, b):
            dve.wait_ge(X_POOL.sem, X_POOL.count(b, "rstd"))
            dve.wait_ge(X_DVE.sem, X_DVE.count(b, "mean"))
            for j in range(TJ):
                last = dve.tensor_scalar(x_t[:, j, :], x_t[:, j, :], mv[:, j, 0:1], rstd[:, j:j + 1],
                                         ALU.subtract, ALU.mult)
            last.then_inc(X_DVE.sem, 1)

        def x_dve_shift(dve, b):
            if later(b):
                dve.wait_ge(X_POOL.sem, X_POOL.count(b - 1, f"x5{NG - 1}b"))
            dve.tensor_copy(xn[:, :, 0], pr1[:, :]).then_inc(X_DVE.sem, 1)
            dve.wait_ge(X_ACT.sem, X_ACT.count(b, "xn3"))
            dve.wait_ge(X_DVE.sem, X_DVE.count(b, "prev"))
            dve.tensor_tensor(sx[:, :, :], xn[:, :, 0:T], xn[:, :, 1:T + 1], ALU.subtract).then_inc(X_DVE.sem, 1)

        def x_dve_xx(dve, b):
            dve.wait_ge(X_DVE.sem, X_DVE.count(b, "shift"))
            if later(b):
                dve.wait_ge(P_PE.sem, P_PE.count(b - 1, f"zk{EC - 1}"))
            for c in cs:
                dve.scalar_tensor_tensor(xx[:, c, :], sx[:, c, :], vcol("maa_x", c), xn[:, c, 1:T + 1],
                                         ALU.mult, ALU.add).then_inc(X_DVE.sem, 1)

        def x_dve2(dve, b, g):
            if g == 0:
                if later(b):
                    dve.wait_ge(P_PE.sem, P_PE.count(b - 1, f"vr{EC - 1}"))
            if g == GG:
                if later(b):
                    dve.wait_ge(G_PE.sem, G_PE.count(b - 1, "gb"))
            for c in cs:
                if c % 2 == 0:
                    dve.wait_ge(X_PE.sem, X_PE.count(b, f"mix{g}{halves[c // 2]}"))
                dve.scalar_tensor_tensor(x5[:, g, c, :], XB[c // 2][:, (c % 2) * T:(c % 2 + 1) * T],
                                         va[:, VA.index("maa_k") + g, c:c + 1], sx[:, c, :],
                                         ALU.add, ALU.mult).then_inc(X_DVE.sem, 1)

        def x_pool1(pool, b):
            if later(b):
                pool.wait_ge(X_DVE.sem, X_DVE.count(b - 1, "norm"))
            if later(b):
                pool.wait_ge(X_POOL.sem, X_POOL.count(b - 1, "rstd"))
            pool.wait_ge(X_DVE.sem, X_DVE.count(b, "mean"))
            alone(pool, passed)
            pool.tensor_scalar(ve[:, :], mv[:, :, 1], 1.0, EPS, ALU.mult, ALU.add).then_inc(X_POOL.sem, 1)
            pool.wait_ge(X_POOL.sem, X_POOL.count(b, "eps"))
            pool.tensor_tensor(rstd[:, :], ve[:, :], mhalf[:, :], ALU.pow).then_inc(X_POOL.sem, 1)

        def x_pool2(pool, b, g):
            for h in range(2):
                pool.wait_ge(X_DVE.sem, X_DVE.count(b, f"mix{g}{2 * h + 1}"))
                pool.tensor_tensor(x5[:, g, 2 * h:2 * h + 2, :], x5[:, g, 2 * h:2 * h + 2, :],
                                   xn[:, 2 * h:2 * h + 2, 1:T + 1], ALU.add).then_inc(X_POOL.sem, 1)

        def project(pe, bank, half, wt, g, c):
            for i in cs:
                last = pe.matmul(bank[:, half * T:(half + 1) * T], W[:, wt, i, c * 128:(c + 1) * 128],
                                 x5[:, g, i, :], start=(i == 0), stop=(i == EC - 1))
            return last

        def p_pe(pe, b, c):
            if c == 0:
                pe.wait_ge(X_POOL.sem, X_POOL.count(b, f"x5{GW}b"))
                if later(b):
                    pe.wait_ge(G_DVE.sem, G_DVE.count(b - 1, "ga"))
                for i in cs:
                    last = pe.matmul(PB[0][0:DEC, 0:T], d1[:, i, :], x5[:, GW, i, :], start=(i == 0), stop=(i == EC - 1))
                last.then_inc(P_PE.sem, 1)
                pe.wait_ge(P_ACT.sem, P_ACT.count(b, "dh"))
            else:
                pe.wait_ge(P_ACT.sem, P_ACT.count(b, f"k{c - 1}"))
            pe.matmul(PB[0][:, T:2 * T], d2[:, c * 128:(c + 1) * 128], dh[:, :], start=True, stop=True)
            project(pe, PB[0], 0, WK, GK, c).then_inc(P_PE.sem, 1)

        def p_pe_vr(pe, b, c, u):
            if u:
                if c == 0:
                    pe.wait_ge(X_POOL.sem, X_POOL.count(b, f"x5{GR}b"))
                project(pe, PB[1], 1, WR, GR, c).then_inc(P_PE.sem, 1)
                return
            if c:
                pe.wait_ge(P_ACT.sem, P_ACT.count(b, f"r{c - 1}"))
            else:
                pe.wait_ge(X_POOL.sem, X_POOL.count(b, f"x5{GV}b"))
                if later(b):
                    pe.wait_ge(G_DVE.sem, G_DVE.count(b - 1, "gb"))
            project(pe, PB[1], 0, WV, GV, c)

        def p_act(act, b, c):
            if c == 0:
                if later(b):
                    act.wait_ge(P_PE.sem, P_PE.count(b - 1, f"zk{EC - 1}"))
                act.wait_ge(P_PE.sem, P_PE.count(b, "dh"))
                act.activation(dh[:, :], PB[0][0:DEC, 0:T], ACT.Tanh).then_inc(P_ACT.sem, 1)
            if later(b):
                act.wait_ge(S_DVE.sem, S_DVE.count(b - 1, f"scan{c}{S // 2 - 1}"))
            if c:
                act.wait_ge(P_ACT.sem, P_ACT.count(b, f"w{c - 1}"))
            else:
                if later(b):
                    act.wait_ge(P_ACT.sem, P_ACT.count(b - 1, f"w{EC - 1}"))
            act.wait_ge(P_PE.sem, P_PE.count(b, f"zk{c}"))
            act.activation(ez[:, :], PB[0][:, T:2 * T], ACT.Exp, bias=vcol("time_decay", c)).then_inc(P_ACT.sem, 1)
            act.wait_ge(P_ACT.sem, P_ACT.count(b, f"ez{c}"))
            act.activation(w_[:, c, :], ez[:, :], ACT.Exp, scale=-1.0).then_inc(P_ACT.sem, 1)
            act.activation(k_[:, c, :], PB[0][:, 0:T], ACT.Copy).then_inc(P_ACT.sem, 1)

        def p_act_vr(act, b, c, u):
            if u == 0:
                return
            act.wait_ge(P_PE.sem, P_PE.count(b, f"vr{c}"))
            if later(b):
                act.wait_ge(S_DVE.sem, S_DVE.count(b - 1, f"kv{c}{BONUS}"))
            act.activation(v_[:, c, :], PB[1][:, 0:T], ACT.Copy).then_inc(P_ACT.sem, 1)
            if later(b):
                act.wait_ge(S_PE.sem, S_PE.count(b - 1, f"v{c}{S // 2 - 1}"))
            if later(b):
                act.wait_ge(P_DVE.sem, P_DVE.count(b - 1, f"vlo{c}"))
            act.activation(vhi[:, c, :], PB[1][:, 0:T], ACT.Copy).then_inc(P_ACT.sem, 1)
            if later(b):
                act.wait_ge(S_POOL.sem, S_POOL.count(b - 1, f"rs{c}{S // 2 - 1}"))
            act.activation(r_[:, c, :], PB[1][:, T:2 * T], ACT.Copy).then_inc(P_ACT.sem, 1)

        def p_dve(dve, b, c, u):
            if u == 0:
                return
            dve.wait_ge(P_ACT.sem, P_ACT.count(b, f"vhi{c}"))
            if later(b):
                dve.wait_ge(S_PE.sem, S_PE.count(b - 1, f"v{c}{S // 2 - 1}"))
            dve.tensor_tensor(vlo[:, c, :], v_[:, c, :], vhi[:, c, :].bitcast(F32), ALU.subtract)\
               .then_inc(P_DVE.sem, 1)

        def g_pe(pe, b, h, u):
            if u:
                project(pe, PB[h], 1, WG, GG, 2 * h + 1).then_inc(G_PE.sem, 1)
                return
            pe.wait_ge(P_ACT.sem, P_ACT.count(b, f"{'kr'[h]}{EC - 1}"))
            if h == 0:
                pe.wait_ge(X_POOL.sem, X_POOL.count(b, f"x5{GG}b"))
            project(pe, PB[h], 0, WG, GG, 2 * h)

        def g_act(act, b, h, u):
            if u == 0:
                return
            if h:
                act.wait_ge(G_DVE.sem, G_DVE.count(b, "ga"))
            else:
                if later(b):
                    act.wait_ge(G_DVE.sem, G_DVE.count(b - 1, "gb"))
            act.wait_ge(G_PE.sem, G_PE.count(b, f"g{halves[h]}"))
            act.activation(th[:, :, :], PB[h][:, :].rearrange("p (c t) -> p c t", c=2), ACT.Tanh, scale=0.5)\
               .then_inc(G_ACT.sem, 1)

        def g_dve(dve, b, h):
            if later(b):
                dve.wait_ge(N_DVE.sem, N_DVE.count(b - 1, f"gate{2 * h + 1}"))
            dve.wait_ge(G_ACT.sem, G_ACT.count(b, f"th{halves[h]}"))
            dve.scalar_tensor_tensor(g2[:, 2 * h:2 * h + 2, :], th[:, :, :], 1.0,
                                     PB[h][:, :].rearrange("p (c t) -> p c t", c=2), ALU.add, ALU.mult)\
               .then_inc(G_DVE.sem, 1)

        def value_bank(c, e):
            return VBK[(c * NE + e) % 2]

        def s_values(pe, b, c, e):
            at = shifted(c, e, -2)
            if at[0] >= 0:
                pe.wait_ge(S_DVE.sem, S_DVE.count(b, "kv%d%d" % at))
            else:
                if later(b):
                    pe.wait_ge(S_DVE.sem, S_DVE.count(b - 1, "kv%d%d" % shifted(EC, e, -2)))
            if e == BONUS:
                pe.wait_ge(S_DVE.sem, S_DVE.count(b, f"ru{c}"))
                last = pe.matmul(value_bank(c, e)[:, 0:T], blk[:, 0, :], ru[:, :], start=True, stop=True)
            else:
                for n in range(2):
                    for part, v in enumerate((vhi, vlo)):
                        last = pe.matmul(value_bank(c, e)[:, n * T:(n + 1) * T], seli[:, 2 * e + n, :], v[:, c, :],
                                         start=(part == 0), stop=(part == 1))
            last.then_inc(S_PE.sem, 1)

        def s_pe_begin(pe, b):
            pe.wait_ge(P_DVE.sem, P_DVE.count(b, f"vlo{EC - 1}"))
            s_values(pe, b, 0, 0)
            s_values(pe, b, 0, 1)

        def s_pe(pe, b, c, e):
            if e == 0:
                if c:
                    pe.wait_ge(S_ACT.sem, S_ACT.count(b, f"sq{c - 1}"))
                else:
                    if later(b):
                        pe.wait_ge(S_ACT.sem, S_ACT.count(b - 1, f"sq{EC - 1}"))
            if e == BONUS:
                pe.wait_ge(S_DVE.sem, S_DVE.count(b, f"kv{c}{e}"))
                last = pe.matmul(AB[:, 0:T], blk[:, 1, :], zv[:, :], start=False, stop=True)
            else:
                pe.wait_ge(S_POOL.sem, S_POOL.count(b, f"rs{c}{e}"))
                for n in range(2):
                    last = pe.matmul(AB[:, 0:T], selo[:, 2 * e + n, :], rs[:, e % 2, n, :],
                                     start=(e == 0 and n == 0), stop=False)
            last.then_inc(S_PE.sem, 1)
            if shifted(c, e, 2)[0] < EC:
                s_values(pe, b, *shifted(c, e, 2))

        def s_dve(dve, b, c, e):
            if c == 0 and e == 0:
                dve.wait_ge(P_ACT.sem, P_ACT.count(b, f"r{EC - 1}"))
                dve.wait_ge(s0_in, 16 * b + 16)
                if later(b):
                    dve.wait_ge(S_DVE.sem, S_DVE.count(b - 1, f"kv{EC - 1}{BONUS}"))
            dve.wait_ge(S_PE.sem, S_PE.count(b, f"v{c}{e}"))
            if e == BONUS:
                if c:
                    dve.wait_ge(S_PE.sem, S_PE.count(b, f"o{c - 1}{e}"))
                else:
                    if later(b):
                        dve.wait_ge(S_PE.sem, S_PE.count(b - 1, f"o{EC - 1}{e}"))
                dve.tensor_tensor(zv[:, :], value_bank(c, e)[:, 0:T], v_[:, c, :], ALU.mult).then_inc(S_DVE.sem, 1)
                return
            if e >= 2:
                dve.wait_ge(S_DVE.sem, S_DVE.count(b, f"scan{c}{e - 2}"))
            elif c:
                dve.wait_ge(S_DVE.sem, S_DVE.count(b, f"scan{c - 1}{BONUS - 2 + e}"))
            dve.tensor_tensor(kv[:, e % 2], value_bank(c, e)[:, :].rearrange("p (e t) -> p e t", e=2),
                              k_[:, c, :].unsqueeze(1).broadcast_to([128, 2, T]), ALU.mult)\
               .then_inc(S_DVE.sem, 1)
            dve.wait_ge(S_DVE.sem, S_DVE.count(b, f"kv{c}{e}"))
            if e >= 2:
                dve.wait_ge(S_POOL.sem, S_POOL.count(b, f"rs{c}{e - 2}"))
            elif c:
                dve.wait_ge(S_POOL.sem, S_POOL.count(b, f"rs{c - 1}{BONUS - 2 + e}"))
            else:
                if later(b):
                    dve.wait_ge(S_POOL.sem, S_POOL.count(b - 1, f"rs{EC - 1}{BONUS - 2 + e}"))
            for n in range(2):
                d = 2 * e + n
                last = dve.tensor_tensor_scan(st[:, e % 2, n, 1:T + 1], w_[:, c, :], kv[:, e % 2, n, :],
                                              s0t[:, c, d:d + 1], ALU.mult, ALU.add)
            last.then_inc(S_DVE.sem, 1)
            if e == 1:
                if c:
                    dve.wait_ge(S_PE.sem, S_PE.count(b, f"v{c - 1}{BONUS}"))
                else:
                    if later(b):
                        dve.wait_ge(S_PE.sem, S_PE.count(b - 1, f"v{EC - 1}{BONUS}"))
                dve.scalar_tensor_tensor(ru[:, :], r_[:, c, :], vcol("bonus", c), k_[:, c, :], ALU.mult, ALU.mult)\
                   .then_inc(S_DVE.sem, 1)

        def s_pool(pool, b, c, q):
            if q == BONUS:
                return
            if c == 0 and q == 0:
                pool.wait_ge(s0_in, 16 * b + 16)
                pool.wait_ge(P_ACT.sem, P_ACT.count(b, f"r{EC - 1}"))
            if q >= 2:
                pool.wait_ge(S_POOL.sem, S_POOL.count(b, f"rs{c}{q - 2}"))
            elif c:
                pool.wait_ge(S_POOL.sem, S_POOL.count(b, f"rs{c - 1}{S // 2 - 2 + q}"))
            else:
                if later(b):
                    pool.wait_ge(S_POOL.sem, S_POOL.count(b - 1, f"rs{EC - 1}{S // 2 - 2 + q}"))
            alone(pool, passed)
            pool.tensor_copy(st[:, q % 2, :, 0], s0t[:, c, 2 * q:2 * q + 2]).then_inc(S_POOL.sem, 1)
            pool.wait_ge(S_POOL.sem, S_POOL.count(b, f"s0{c}{q}"))
            pool.wait_ge(S_DVE.sem, S_DVE.count(b, f"scan{c}{q}"))
            if q >= 2:
                pool.wait_ge(S_PE.sem, S_PE.count(b, f"o{c}{q - 2}"))
            elif c:
                pool.wait_ge(S_PE.sem, S_PE.count(b, f"o{c - 1}{S // 2 - 2 + q}"))
            else:
                if later(b):
                    pool.wait_ge(S_PE.sem, S_PE.count(b - 1, f"o{EC - 1}{S // 2 - 2 + q}"))
            pool.tensor_tensor(rs[:, q % 2], st[:, q % 2, :, 0:T],
                               r_[:, c, :].unsqueeze(1).broadcast_to([128, 2, T]), ALU.mult)\
                .then_inc(S_POOL.sem, 1)

        def s_act(act, b, c, e):
            if e < BONUS:
                return
            if c == 0:
                if later(b):
                    act.wait_ge(K_PE.sem, K_PE.count(b - 1, "wo1"))
                if later(b):
                    act.wait_ge(N_DVE.sem, N_DVE.count(b - 1, f"norm{EC - 1}"))
            act.wait_ge(S_PE.sem, S_PE.count(b, f"o{c}{BONUS}"))
            act.activation(att[:, c, :], AB[:, 0:T], ACT.Copy).then_inc(S_ACT.sem, 1)
            act.activation(sq[:, c, :], AB[:, 0:T], ACT.Square).then_inc(S_ACT.sem, 1)

        def n_pe(pe, b, h):
            if later(b):
                if h:
                    pe.wait_ge(K_DVE.sem, K_DVE.count(b - 1, "rv1"))
                else:
                    pe.wait_ge(K_ACT.sem, K_ACT.count(b - 1, "th1"))
            else:
                if h:
                    pe.wait_ge(N_ACT.sem, N_ACT.count(b, "sda"))
            pe.wait_ge(S_ACT.sem, S_ACT.count(b, f"sq{2 * h + 1}"))
            for c in (2 * h, 2 * h + 1):
                last = pe.matmul(KB[:, (c % 2) * T:(c % 2 + 1) * T], blk[:, 2, :], sq[:, c, :],
                                 start=True, stop=True)
            last.then_inc(N_PE.sem, 1)

        def n_act(act, b, h):
            act.wait_ge(N_PE.sem, N_PE.count(b, f"var{halves[h]}"))
            act.activation(sq[:, 2 * h:2 * h + 2, :], KB[:, :].rearrange("p (c t) -> p c t", c=2), ACT.Sqrt,
                           bias=small[:, 0:1]).then_inc(N_ACT.sem, 1)

        def n_dve(dve, b, c):
            dve.wait_ge(N_ACT.sem, N_ACT.count(b, f"sd{halves[c // 2]}"))
            dve.reciprocal(sq[:, c, :], sq[:, c, :]).then_inc(N_DVE.sem, 1)
            dve.wait_ge(N_DVE.sem, N_DVE.count(b, f"rstd{c}"))
            dve.tensor_tensor(att[:, c, :], att[:, c, :], sq[:, c, :], ALU.mult).then_inc(N_DVE.sem, 1)
            dve.wait_ge(N_DVE.sem, N_DVE.count(b, f"norm{c}"))
            dve.tensor_scalar(att[:, c, :], att[:, c, :], half_gn[:, 0, c:c + 1], half_gn[:, 1, c:c + 1],
                              ALU.mult, ALU.add).then_inc(N_DVE.sem, 1)
            dve.wait_ge(N_DVE.sem, N_DVE.count(b, f"affine{c}"))
            dve.wait_ge(G_DVE.sem, G_DVE.count(b, "gb"))
            dve.tensor_tensor(att[:, c, :], att[:, c, :], g2[:, c, :], ALU.mult).then_inc(N_DVE.sem, 1)

        def k_pe_wo(pe, b, j, u):
            if u == 0:
                if j:
                    pe.wait_ge(K_DVE.sem, K_DVE.count(b, "x10"))
                else:
                    pe.wait_ge(N_DVE.sem, N_DVE.count(b, f"gate{EC - 1}"))
                    pe.wait_ge(N_ACT.sem, N_ACT.count(b, "sdb"))
            for c in (2 * u, 2 * u + 1):
                last = pe.matmul(KB[:, :], att[:, c, j * 128:(j + 1) * 128], W[:, WO, c, :],
                                 start=(c == 0), stop=(c == EC - 1))
            if u:
                last.then_inc(K_PE.sem, 1)

        def k_pe2(pe, b, h):
            if h:
                pe.wait_ge(K_ACT.sem, K_ACT.count(b, "xn1"))
            else:
                pe.wait_ge(K_DVE.sem, K_DVE.count(b, "norm"))
            for c in (2 * h, 2 * h + 1):
                for j in range(TJ):
                    o = (c % 2) * T + j * 128
                    last = pe.transpose(KB[:, o:o + 128], xl[:, j, c * 128:(c + 1) * 128], idn[:, :])
            last.then_inc(K_PE.sem, 1)

        def k_pe_fk(pe, b, h, u):
            if u == 0:
                if h:
                    pe.wait_ge(K_ACT.sem, K_ACT.count(b, "relua"))
                else:
                    pe.wait_ge(K_DVE.sem, K_DVE.count(b, "xk"))
                    pe.wait_ge(K_ACT.sem, K_ACT.count(b, "xn3"))
            c = 2 * h + u
            for i in cs:
                last = pe.matmul(KB[:, u * T:(u + 1) * T], W[:, FWK, i, c * 128:(c + 1) * 128],
                                 xk[:, i, :], start=(i == 0), stop=(i == EC - 1))
            if u:
                last.then_inc(K_PE.sem, 1)

        def k_pe_fr(pe, b, j, u):
            if u == 0:
                if j == 0:
                    pe.wait_ge(K_DVE.sem, K_DVE.count(b, "xr"))
                pe.wait_ge(K_ACT.sem, K_ACT.count(b, "relub" if j == 0 else "th0"))
            for c in (2 * u, 2 * u + 1):
                last = pe.matmul(KB[:, :], xr[:, c, j * 128:(j + 1) * 128], Wf[:, 0, c, :],
                                 start=(c == 0), stop=(c == EC - 1))
            if u:
                last.then_inc(K_PE.sem, 1)

        def k_pe_fv(pe, b, j, u):
            if u == 0:
                if j:
                    pe.wait_ge(K_DVE.sem, K_DVE.count(b, "rv0"))
                else:
                    pe.wait_ge(K_ACT.sem, K_ACT.count(b, "th1"))
                    if not isinstance(b, int) or b < B - 1:
                        pe.wait_ge(N_ACT.sem, N_ACT.count(b + 1, "sda"))
            for c in (2 * u, 2 * u + 1):
                last = pe.matmul(KB[:, :], kk[:, c, j * 128:(j + 1) * 128], Wf[:, 1, c, :],
                                 start=(c == 0), stop=(c == EC - 1))
            if u:
                last.then_inc(K_PE.sem, 1)

        def k_act1(act, b, h):
            if h == 0:
                if later(b):
                    act.wait_ge(K_DVE.sem, K_DVE.count(b - 1, "xr"))
            act.wait_ge(K_PE.sem, K_PE.count(b, f"turn_{halves[h]}"))
            for c in (2 * h, 2 * h + 1):
                act.activation(xn2[:, c, 1:T + 1], KB[:, (c % 2) * T:(c % 2 + 1) * T], ACT.Identity,
                               bias=vcol("ln2_b", c), scale=vcol("ln2_w", c)).then_inc(K_ACT.sem, 1)

        def k_act_fk(act, b, h, u):
            if u == 0:
                return
            if h == 0:
                if later(b):
                    act.wait_ge(K_PE.sem, K_PE.count(b - 1, "fv1"))
            kh = kk[:, 2 * h:2 * h + 2, :]
            act.wait_ge(K_PE.sem, K_PE.count(b, f"fk{halves[h]}"))
            act.activation(kh, KB[:, :].rearrange("p (c t) -> p c t", c=2), ACT.Relu).then_inc(K_ACT.sem, 1)
            act.wait_ge(K_ACT.sem, K_ACT.count(b, f"relu{halves[h]}"))
            act.activation(kh, kh, ACT.Square).then_inc(K_ACT.sem, 1)

        def k_act_fr(act, b, j, u):
            if u == 0:
                return
            act.wait_ge(K_PE.sem, K_PE.count(b, f"fr{j}"))
            act.activation(tr[:, j, :], KB[:, :], ACT.Tanh, scale=0.5).then_inc(K_ACT.sem, 1)

        def k_dve_wo(dve, b, j, u):
            if u == 0:
                return
            if j == 0:
                dve.wait_ge(x1_in, 32 * b + 32)
            dve.wait_ge(K_PE.sem, K_PE.count(b, f"wo{j}"))
            dve.tensor_tensor(x1[:, j, :], x1[:, j, :], KB[:, :], ALU.add).then_inc(K_DVE.sem, 1)

        def k_dve_stat(dve, b):
            dve.wait_ge(K_DVE.sem, K_DVE.count(b, "x11"))
            for j in range(TJ):
                last = dve.bn_stats(stat2[:, j, :], x1[:, j, :])
            last.then_inc(K_DVE.sem, 1)
            dve.wait_ge(K_DVE.sem, K_DVE.count(b, "stat"))
            alone(dve, passed)
            for j in range(TJ):
                last = dve.bn_aggr(mv2[:, j, :], stat2[:, j, :])
            last.then_inc(K_DVE.sem, 1)

        def k_dve_norm(dve, b):
            dve.wait_ge(K_DVE.sem, K_DVE.count(b, "mean"))
            dve.wait_ge(K_POOL.sem, K_POOL.count(b, "rstd"))
            for j in range(TJ):
                last = dve.tensor_scalar(xl[:, j, :], x1[:, j, :], mv2[:, j, 0:1], rstd2[:, j:j + 1],
                                         ALU.subtract, ALU.mult)
            last.then_inc(K_DVE.sem, 1)

        def k_dve2(dve, b):
            dve.tensor_copy(xn2[:, :, 0], pr2[:, :]).then_inc(K_DVE.sem, 1)
            dve.wait_ge(K_DVE.sem, K_DVE.count(b, "prev"))
            dve.wait_ge(K_ACT.sem, K_ACT.count(b, "xn3"))
            dve.tensor_tensor(sx2, xn2[:, :, 0:T], xn2[:, :, 1:T + 1], ALU.subtract).then_inc(K_DVE.sem, 1)

        def k_dve_xk(dve, b):
            dve.wait_ge(K_DVE.sem, K_DVE.count(b, "shift"))
            if later(b):
                dve.wait_ge(saved, 16 * b)
            for c in cs:
                last = dve.scalar_tensor_tensor(xk[:, c, :], sx2[:, c, :], vcol("ffn_maa_k", c), xn2[:, c, 1:T + 1],
                                                ALU.mult, ALU.add)
            last.then_inc(K_DVE.sem, 1)

        def k_dve_xr(dve, b):
            dve.wait_ge(K_DVE.sem, K_DVE.count(b, "shift"))
            if later(b):
                dve.wait_ge(K_PE.sem, K_PE.count(b - 1, "fr1"))
            for c in cs:
                last = dve.scalar_tensor_tensor(xr[:, c, :], sx2[:, c, :], vcol("ffn_maa_r", c), xn2[:, c, 1:T + 1],
                                                ALU.mult, ALU.add)
            last.then_inc(K_DVE.sem, 1)

        def k_dve_fv(dve, b, j, u):
            if u == 0:
                return
            dve.wait_ge(K_ACT.sem, K_ACT.count(b, f"th{j}"))
            dve.wait_ge(K_PE.sem, K_PE.count(b, f"fv{j}"))
            dve.scalar_tensor_tensor(tr[:, j, :], tr[:, j, :], 1.0, KB[:, :], ALU.add, ALU.mult)\
               .then_inc(K_DVE.sem, 1)
            dve.wait_ge(K_DVE.sem, K_DVE.count(b, f"rv{j}"))
            dve.scalar_tensor_tensor(tr[:, j, :], tr[:, j, :], 0.5, x1[:, j, :], ALU.mult, ALU.add)\
               .then_inc(K_DVE.sem, 1)

        def k_pool(pool, b):
            if later(b):
                pool.wait_ge(K_DVE.sem, K_DVE.count(b - 1, "norm"))
            pool.wait_ge(K_DVE.sem, K_DVE.count(b, "mean"))
            alone(pool, passed)
            pool.tensor_scalar(ve2[:, :], mv2[:, :, 1], 1.0, EPS, ALU.mult, ALU.add).then_inc(K_POOL.sem, 1)
            pool.wait_ge(K_POOL.sem, K_POOL.count(b, "eps"))
            pool.tensor_tensor(rstd2[:, :], ve2[:, :], mhalf[:, :], ALU.pow).then_inc(K_POOL.sem, 1)

        LAG = 2
        SLOTS = {
            -1: [("G", 0, 0, 0), ("N_out", -1, 2)], 0: [("G", 0, 0, 1), ("N_out", -1, 3)], 1: [("G", 0, 1, 0)],
            2: [("G", 0, 1, 1), ("G_out", 0, 0)], 3: [("X_mix", 1, 0), ("G_out", 0, 1)], 4: [("wo", -1, 0, 0)],
            5: [("wo", -1, 0, 1)], 6: [("X_mix", 1, 1)], 7: [("wo", -1, 1, 0)], 8: [("wo", -1, 1, 1), ("k_stat", -1)],
            9: [("X_mix", 1, 2)], 10: [("P_zk", 1, 0), ("k_norm", -1)], 11: [("X_mix", 1, 3)],
            12: [("k_turn", -1, 0), ("P_vr", 1, 0, 0)], 13: [("k_turn", -1, 1), ("X_mix", 1, 4)],
            14: [("P_vr", 1, 0, 1), ("k_shift", -1)], 15: [("k_xk", -1)], 16: [("P_zk", 1, 1)], 17: [("fk", -1, 0, 0)],
            18: [("fk", -1, 0, 1), ("k_xr", -1)], 19: [("P_vr", 1, 1, 0)], 20: [("fk", -1, 1, 0)],
            21: [("fk", -1, 1, 1)], 22: [("P_vr", 1, 1, 1)],
            23: [("fr", -1, 0, 0)], 24: [("fr", -1, 0, 1), ("X_stat", 2)],
            25: [("fr", -1, 1, 0)], 26: [("fr", -1, 1, 1), ("X_norm", 2)], 27: [("P_zk", 1, 2)], 28: [("N", 0, 0)],
            29: [("P_vr", 1, 2, 0), ("N_out", 0, 0)], 30: [("X_turn", 2)], 31: [("P_vr", 1, 2, 1)],
            32: [("fv", -1, 0, 0), ("X_shift", 2)], 33: [("fv", -1, 0, 1)], 34: [("fv", -1, 1, 0), ("N_out", 0, 1)],
            35: [("fv", -1, 1, 1)],
        }
        TAIL = [("P_zk", 1, 3), ("X_xx", 2), ("P_vr", 1, 3, 0), ("P_vr", 1, 3, 1), ("N", 0, 1), ("S_begin", 1),
                ("X_hid", 2), ("save", -1)]

        def round_a(eng, p, i, lag):
            def do(name, ahead, *more):
                b = i + ahead
                if name in p and (not isinstance(b, int) or 0 <= b < B):
                    p[name](eng, b, *more)

            do("s0", 0)
            do("x", 2)
            do("x1", -1)
            for slot in range(-1, len(elements) + lag):
                if 0 <= slot < len(elements):
                    do("S", 0, *elements[slot])
                for name, ahead, *more in SLOTS.get(slot - lag, ()):
                    do(name, ahead, *more)
            for name, ahead, *more in TAIL:
                do(name, ahead, *more)

        def phase_a(eng, p, lag=0):
            def do(name, b, *more):
                if name in p:
                    p[name](eng, b, *more)

            for b in range(2):
                do("x", b)
                do("loads", b)
                for name in ("X_stat", "X_norm", "X_turn", "X_shift"):
                    do(name, b)
                if b:
                    do("proj_in", 0)
                    for c in cs:
                        do("P_zk", 0, c)
                        do("P_vr", 0, c, 0)
                        do("P_vr", 0, c, 1)
                do("X_xx", b)
                do("X_hid", b)
                if b:
                    do("S_begin", 0)
                else:
                    for g in range(NG):
                        do("X_mix", 0, g)
            do("weights_in", 0)
            round_a(eng, p, 0, lag)
            round_a(eng, p, 1, lag)
            with eng.Fori(2, B - 2) as i:
                round_a(eng, p, i, lag)
            round_a(eng, p, B - 2, lag)
            round_a(eng, p, B - 1, lag)
            do("x1", B - 1)
            do("first_b", B - 1)
            do("N_out", B - 1, 2)
            do("N_out", B - 1, 3)
            for name, *more in (("wo", 0), ("wo", 1), ("k_stat",), ("k_norm",), ("k_turn", 0), ("k_turn", 1), ("k_shift",), ("k_xk",), ("k_xr",),
                                ("fk", 0), ("fk", 1), ("fr", 0), ("fr", 1), ("fv", 0), ("fv", 1), ("save",)):
                if name in ("wo", "fk", "fr", "fv"):
                    do(name, B - 1, *more, 0)
                    do(name, B - 1, *more, 1)
                    continue
                do(name, B - 1, *more)

        a_done = [X_PE, X_ACT, X_DVE, X_POOL, P_PE, P_ACT, P_DVE, G_PE, G_ACT, G_DVE, S_PE, S_DVE, S_POOL,
                  S_ACT, N_PE, N_ACT, N_DVE, K_PE, K_ACT, K_DVE, K_POOL]

        def end_a(eng):
            for s in a_done:
                eng.wait_ge(s.sem, B * s.per)
            eng.wait_ge(saved, 16 * B)

        ca.close()
        cb = ctx.enter_context(ExitStack())
        WQH = sb(cb, "WQH", [128, 4, EC, E], F32R)
        WQL = sb(cb, "WQL", [128, 4, EC, E], F32R)
        rows = sb(cb, "rows", [128, 2, E])
        mhalf_b = sb(cb, "mhalf_b", [128, TJ])
        h_in = sb(cb, "h_in", [128, TJ, E])
        cx = sb(cb, "cx", [128, EC, T])
        cxh = sb(cb, "cxh", [128, EC, T], F32R)
        cxl = sb(cb, "cxl", [128, EC, T], F32R)
        mk8 = sb(cb, "mk8", [128, T], U8)
        mneg = sb(cb, "mneg", [128, T])
        bstat = sb(cb, "bstat", [128, TJ, 6])
        bmv = sb(cb, "bmv", [128, TJ, 2])
        bve = sb(cb, "bve", [128, TJ])
        brstd = sb(cb, "brstd", [128, TJ])
        hn = sb(cb, "hn", [128, EC, T])
        hnl = sb(cb, "hnl", [128, EC, T], F32R)
        hnh = sb(cb, "hnh", [128, EC, T], F32R)
        qt = sb(cb, "qt", [128, EC, T])
        kt = sb(cb, "kt", [128, EC, T])
        vt = sb(cb, "vt", [128, TJ, E])
        NSC = 4
        sc = sb(cb, "sc", [128, NSC, TJ, T])
        pt = sb(cb, "pt", [128, 2, 2, T])
        mx = sb(cb, "mx", [128, 2, TJ])
        nmx = sb(cb, "nmx", [128, 2, TJ])
        den = sb(cb, "den", [128, 2, TJ])
        rden = sb(cb, "rden", [128, 2, TJ])
        aot = sb(cb, "aot", [128, EC, T])
        aol = sb(cb, "aol", [128, EC, T], F32R)
        aoh = sb(cb, "aoh", [128, EC, T], F32R)
        hb = sb(cb, "hb", [128, TJ, E])

        b_in1 = sem("b_in1")
        m_in = sem("m_in")
        q_in = sem("q_in")
        hc_in = sem("hc_in")
        hb_in = sem("hb_in")
        hid_out = sem("hid_out")
        b_const = sem("b_const")
        split_hi = sem("split_hi")
        split_lo = sem("split_lo")
        hs = range(AH)
        L_PE = steps("L_PE", ["turn_a", "turn_b", "k_a", "q_a", "k_b", "q_b"])
        L_ACT = steps("L_ACT", ["cxh"] + [f"{n}{c}" for c in cs for n in ("hn", "hnh")]
                      + ["k0", "k1", "q0", "q1", "k2", "k3", "q2", "q3"])
        L_DVE = steps("L_DVE", ["stat", "mean", "norm", "cxl", "hnl", "mask"])
        V_PE = steps("V_PE", ["v1", "v0"])
        V_DVE = steps("V_DVE", ["v1", "v0"])
        L_POOL = steps("L_POOL", ["eps", "rstd"])
        TURN, OUT = 3, 4
        A_SLOTS = range(AH + OUT)
        A_PE = steps("A_PE", [n for h in A_SLOTS for n in ([f"s{h}"] if h < AH else [])
                              + ([f"t{h - TURN}"] if 0 <= h - TURN < AH else []) + ([f"o{h - OUT}"] if h >= OUT else [])])
        A_ACT = steps("A_ACT", [n for h in A_SLOTS for n in ([f"p{h - TURN}"] if 0 <= h - TURN < AH else [])
                                + ([f"e{h}"] if h < AH else [])])
        A_DVE = steps("A_DVE", [n for h in A_SLOTS for n in ([f"m{h}", f"n{h}"] if h < AH else [])
                                + ([f"r{h - 1}", f"w{h - 1}"] if 1 <= h <= AH else [])])
        C_PE = steps("C_PE", ["c0", "c1"])
        C_DVE = steps("C_DVE", ["aol_a", "aol_b", "hid0", "hid1"])
        C_ACT = steps("C_ACT", [f"{n}_{h}" for h in halves for n in ("aot", "aoh")])
        C_POOL = steps("C_POOL", ["hb"])
        LB, SB, TBK, OB, CB = banks[0:2], banks[2:4], banks[4], banks[5:7], banks[7]

        def bcol(name, c):
            return vb[:, VB.index(name), c:c + 1]

        def thirds(pe, dst, high, low, moving_high, moving_low, start, stop):
            pe.matmul(dst, high, moving_high, start=start, stop=False)
            pe.matmul(dst, high, moving_low, start=False, stop=False)
            return pe.matmul(dst, low, moving_high, start=False, stop=stop)

        def sp_hc(sp, b):
            if later(b):
                sp.wait_ge(L_DVE.sem, L_DVE.count(b - 1, "mask"))
            sp.dma_start(h_in[:, :, :], scratch[b].rearrange("(j p) e -> p j e", p=128)).then_inc(hc_in, 16)
            sp.dma_start(cx[:, :, :], ctxt[b].rearrange("(c p) t -> p c t", p=128)).then_inc(hc_in, 16)
            sp.dma_start(mk8[:, :], mask[b].partition_broadcast(128)).then_inc(hc_in, 16)

        def l_pe(pe, b, h):
            if h == 0:
                pe.wait_ge(L_DVE.sem, L_DVE.count(b, "norm"))
                if later(b):
                    pe.wait_ge(V_DVE.sem, V_DVE.count(b - 1, "v0"))
            for c in (2 * h, 2 * h + 1):
                for j in range(TJ):
                    o = (c % 2) * T + j * 128
                    last = pe.transpose(LB[h][:, o:o + 128], h_in[:, j, c * 128:(c + 1) * 128], idn[:, :])
            last.then_inc(L_PE.sem, 1)

        def l_pe_qk(pe, b, slot, c):
            if c == 0:
                pe.wait_ge(L_ACT.sem, L_ACT.count(b, "hnh3"))
                pe.wait_ge(L_DVE.sem, L_DVE.count(b, ("hnl", "cxl")[slot]))
            elif c == 2:
                pe.wait_ge(L_ACT.sem, L_ACT.count(b, f"{'qk'[slot]}1"))
            for i in cs:
                wc = slice(c * 128, (c + 1) * 128)
                last = thirds(pe, LB[slot][:, (c % 2) * T:(c % 2 + 1) * T], WQH[:, slot, i, wc], WQL[:, slot, i, wc],
                              (hnh, cxh)[slot][:, i, :], (hnl, cxl)[slot][:, i, :], i == 0, i == EC - 1)
            if c % 2:
                last.then_inc(L_PE.sem, 1)

        def l_pe_v(pe, b, j, half):
            if half == 0:
                pe.wait_ge(L_ACT.sem, L_ACT.count(b, f"{'qk'[j]}3"))
            for c in (2 * half, 2 * half + 1):
                tok = slice(j * 128, (j + 1) * 128)
                last = thirds(pe, LB[j][:, :], cxh[:, c, tok], cxl[:, c, tok], WQH[:, 2, c, :], WQL[:, 2, c, :],
                              c == 0, c == EC - 1)
            if half:
                last.then_inc(V_PE.sem, 1)

        def l_act(act, b):
            act.wait_ge(hc_in, 48 * b + 48)
            if later(b):
                act.wait_ge(V_PE.sem, V_PE.count(b - 1, "v0"))
            act.activation(cxh[:, :, :], cx[:, :, :], ACT.Copy).then_inc(L_ACT.sem, 1)

        def l_act_turn(act, b, h):
            if h == 0:
                if later(b):
                    act.wait_ge(L_DVE.sem, L_DVE.count(b - 1, "hnl"))
                if later(b):
                    act.wait_ge(L_PE.sem, L_PE.count(b - 1, "q_b"))
            act.wait_ge(L_PE.sem, L_PE.count(b, f"turn_{halves[h]}"))
            for c in (2 * h, 2 * h + 1):
                for dst in (hn[:, c, :], hnh[:, c, :]):
                    act.activation(dst, LB[c // 2][:, (c % 2) * T:(c % 2 + 1) * T], ACT.Identity,
                                   bias=bcol("ln1_b", c), scale=bcol("ln1_w", c)).then_inc(L_ACT.sem, 1)

        def l_act_qk(act, b, slot, h):
            if later(b):
                act.wait_ge(A_PE.sem, A_PE.count(b - 1, f"s{8 * h + 7}"))
            act.wait_ge(L_PE.sem, L_PE.count(b, f"{'qk'[slot]}_{halves[h]}"))
            for n in (2 * h, 2 * h + 1):
                act.activation((qt, kt)[slot][:, n, :], LB[slot][:, (n % 2) * T:(n % 2 + 1) * T], ACT.Identity,
                               bias=bcol(("q_b", "k_b")[slot], n)).then_inc(L_ACT.sem, 1)

        def l_dve(dve, b):
            dve.wait_ge(hc_in, 48 * b + 48)
            if later(b):
                dve.wait_ge(L_DVE.sem, L_DVE.count(b - 1, "mean"))
            for j in range(TJ):
                last = dve.bn_stats(bstat[:, j, :], h_in[:, j, :])
            last.then_inc(L_DVE.sem, 1)
            dve.wait_ge(L_DVE.sem, L_DVE.count(b, "stat"))
            if later(b):
                dve.wait_ge(L_POOL.sem, L_POOL.count(b - 1, "eps"))
            alone(dve, passed)
            for j in range(TJ):
                last = dve.bn_aggr(bmv[:, j, :], bstat[:, j, :])
            last.then_inc(L_DVE.sem, 1)

        def l_dve_norm(dve, b):
            dve.wait_ge(L_DVE.sem, L_DVE.count(b, "mean"))
            dve.wait_ge(L_POOL.sem, L_POOL.count(b, "rstd"))
            for j in range(TJ):
                last = dve.tensor_scalar(h_in[:, j, :], h_in[:, j, :], bmv[:, j, 0:1], brstd[:, j:j + 1],
                                         ALU.subtract, ALU.mult)
            last.then_inc(L_DVE.sem, 1)

        def l_dve_low_cx(dve, b):
            if later(b):
                dve.wait_ge(V_PE.sem, V_PE.count(b - 1, "v0"))
            dve.wait_ge(L_ACT.sem, L_ACT.count(b, "cxh"))
            dve.tensor_tensor(cxl[:, :, :], cx[:, :, :], cxh[:, :, :].bitcast(F32), ALU.subtract)\
               .then_inc(L_DVE.sem, 1)

        def l_dve_low(dve, b):
            if later(b):
                dve.wait_ge(L_PE.sem, L_PE.count(b - 1, "q_b"))
            dve.wait_ge(L_ACT.sem, L_ACT.count(b, "hnh3"))
            dve.tensor_tensor(hnl[:, :, :], hn[:, :, :], hnh[:, :, :].bitcast(F32), ALU.subtract)\
               .then_inc(L_DVE.sem, 1)

        def l_dve_mask(dve, b):
            if later(b):
                dve.wait_ge(A_DVE.sem, A_DVE.count(b - 1, f"m{AH - 1}"))
            dve.tensor_scalar(mneg[:, :], mk8[:, :], 0.0, MASKED, ALU.is_equal, ALU.mult).then_inc(L_DVE.sem, 1)

        def l_dve_v(dve, b, j, half):
            if half == 0:
                return
            if j == 1:
                if later(b):
                    dve.wait_ge(A_PE.sem, A_PE.count(b - 1, f"o{AH - 1}"))
            dve.wait_ge(V_PE.sem, V_PE.count(b, f"v{j}"))
            dve.tensor_tensor(vt[:, j, :], LB[j][:, :], rows[:, 0, :], ALU.add).then_inc(V_DVE.sem, 1)

        def l_pool(pool, b):
            if later(b):
                pool.wait_ge(L_DVE.sem, L_DVE.count(b - 1, "norm"))
            pool.wait_ge(L_DVE.sem, L_DVE.count(b, "mean"))
            alone(pool, passed)
            pool.tensor_scalar(bve[:, :], bmv[:, :, 1], 1.0, EPS, ALU.mult, ALU.add).then_inc(L_POOL.sem, 1)
            pool.wait_ge(L_POOL.sem, L_POOL.count(b, "eps"))
            pool.tensor_tensor(brstd[:, :], bve[:, :], mhalf_b[:, :], ALU.pow).then_inc(L_POOL.sem, 1)

        def head(h):
            return h // 4, 32 * (h % 4)

        def a_pe(pe, b, h):
            if h == 0:
                pe.wait_ge(L_ACT.sem, L_ACT.count(b, "q1"))
            if h == AH // 2:
                pe.wait_ge(L_ACT.sem, L_ACT.count(b, "q1"))
            if h == AH // 2:
                pe.wait_ge(L_ACT.sem, L_ACT.count(b, f"q{EC - 1}"))
            if h < AH:
                c, p = head(h)
                if h >= 2:
                    pe.wait_ge(A_DVE.sem, A_DVE.count(b, f"m{h - 2}"))
                else:
                    if later(b):
                        pe.wait_ge(A_DVE.sem, A_DVE.count(b - 1, f"m{AH - 2 + h}"))
                for j in range(TJ):
                    last = pe.matmul(SB[h % 2][:, j * T:(j + 1) * T], qt[p:p + HD, c, j * 128:(j + 1) * 128],
                                     kt[p:p + HD, c, :], start=True, stop=True)
                last.then_inc(A_PE.sem, 1)
            if 0 <= h - TURN < AH:
                n = h - TURN
                pe.wait_ge(A_DVE.sem, A_DVE.count(b, f"w{n}"))
                if n:
                    pe.wait_ge(A_ACT.sem, A_ACT.count(b, f"p{n - 1}"))
                else:
                    if later(b):
                        pe.wait_ge(A_ACT.sem, A_ACT.count(b - 1, f"p{AH - 1}"))
                for i in range(2):
                    for j in range(TJ):
                        o = i * T + j * 128
                        last = pe.transpose(TBK[:, o:o + 128], sc[:, n % NSC, j, i * 128:(i + 1) * 128], idn[:, :])
                last.then_inc(A_PE.sem, 1)
            if h >= OUT:
                n = h - OUT
                c, p = head(n)
                pe.wait_ge(A_ACT.sem, A_ACT.count(b, f"p{n}"))
                if n == 0:
                    pe.wait_ge(V_DVE.sem, V_DVE.count(b, "v0"))
                if n % (AH // 2) == 0:
                    if later(b):
                        pe.wait_ge(C_ACT.sem, C_ACT.count(b - 1, f"aoh_{halves[c // 2]}"))
                for i in range(2):
                    last = pe.matmul(OB[c // 2][p:p + HD, (c % 2) * T:(c % 2 + 1) * T], vt[:, i, n * HD:(n + 1) * HD],
                                     pt[:, n % 2, i, :], start=(i == 0), stop=(i == 1))
                last.then_inc(A_PE.sem, 1)

        def a_dve(dve, b, h):
            if h < AH:
                dve.wait_ge(A_PE.sem, A_PE.count(b, f"s{h}"))
                if h >= NSC:
                    dve.wait_ge(A_ACT.sem, A_ACT.count(b, f"e{h - NSC}"))
                else:
                    if later(b):
                        dve.wait_ge(A_ACT.sem, A_ACT.count(b - 1, f"e{AH - 1}"))
                if h == 0:
                    dve.wait_ge(L_DVE.sem, L_DVE.count(b, "mask"))
                alone(dve, passed)
                for j in range(TJ):
                    last = dve.tensor_tensor_reduce(out=sc[:, h % NSC, j, :], in0=SB[h % 2][:, j * T:(j + 1) * T],
                                                    in1=mneg[:, :], scale=1.0, scalar=MASKED, op0=ALU.add, op1=ALU.max,
                                                    accum_out=mx[:, h % 2, j:j + 1])
                last.then_inc(A_DVE.sem, 1)
                dve.wait_ge(A_DVE.sem, A_DVE.count(b, f"m{h}"))
                if h >= 2:
                    dve.wait_ge(A_ACT.sem, A_ACT.count(b, f"e{h - 2}"))
                dve.tensor_scalar(nmx[:, h % 2, :], mx[:, h % 2, :], -SCALE, None, ALU.mult).then_inc(A_DVE.sem, 1)
            if 1 <= h <= AH:
                n = h - 1
                dve.wait_ge(A_ACT.sem, A_ACT.count(b, f"e{n}"))
                dve.reciprocal(rden[:, n % 2, :], den[:, n % 2, :]).then_inc(A_DVE.sem, 1)
                dve.wait_ge(A_DVE.sem, A_DVE.count(b, f"r{n}"))
                for j in range(TJ):
                    last = dve.tensor_scalar(sc[:, n % NSC, j, :], sc[:, n % NSC, j, :], rden[:, n % 2, j:j + 1], None,
                                             ALU.mult)
                last.then_inc(A_DVE.sem, 1)

        def a_act(act, b, h):
            if 0 <= h - TURN < AH:
                n = h - TURN
                act.wait_ge(A_PE.sem, A_PE.count(b, f"t{n}"))
                act.activation(pt[:, n % 2], TBK[:, :].rearrange("p (i t) -> p i t", i=2), ACT.Copy).then_inc(A_ACT.sem, 1)
            if h < AH:
                act.wait_ge(A_DVE.sem, A_DVE.count(b, f"n{h}"))
                for j in range(TJ):
                    last = act.activation(sc[:, h % NSC, j, :], sc[:, h % NSC, j, :], ACT.Exp, bias=nmx[:, h % 2, j:j + 1],
                                          scale=SCALE, accum_out=den[:, h % 2, j:j + 1])
                last.then_inc(A_ACT.sem, 1)

        def sp_hb(sp, b):
            if later(b):
                sp.wait_ge(hid_out, 16 * b)
            sp.dma_start(hb[:, :, :], scratch[b].rearrange("(j p) e -> p j e", p=128)).then_inc(hb_in, 16)

        def sp_hid(sp, b):
            sp.wait_ge(C_DVE.sem, C_DVE.count(b, "hid1"))
            sp.dma_start(scratch2[b].rearrange("(j p) e -> p j e", p=128), hb[:, :, :]).then_inc(hid_out, 16)

        def c_pe_out(pe, b, j, half):
            if half == 0:
                if j:
                    pe.wait_ge(C_DVE.sem, C_DVE.count(b, "hid0"))
                else:
                    pe.wait_ge(C_DVE.sem, C_DVE.count(b, "aol_b"))
            for c in (2 * half, 2 * half + 1):
                tok = slice(j * 128, (j + 1) * 128)
                last = thirds(pe, CB[:, :], aoh[:, c, tok], aol[:, c, tok], WQH[:, 3, c, :], WQL[:, 3, c, :],
                              c == 0, c == EC - 1)
            if half:
                last.then_inc(C_PE.sem, 1)

        def c_dve_low(dve, b, h):
            if later(b):
                dve.wait_ge(C_PE.sem, C_PE.count(b - 1, "c1"))
            dve.wait_ge(C_ACT.sem, C_ACT.count(b, f"aoh_{halves[h]}"))
            half = slice(2 * h, 2 * h + 2)
            dve.tensor_tensor(aol[:, half, :], aot[:, half, :], aoh[:, half, :].bitcast(F32), ALU.subtract)\
               .then_inc(C_DVE.sem, 1)

        def c_dve_hid(dve, b, j, half):
            if half == 0:
                return
            if j == 0:
                dve.wait_ge(C_POOL.sem, C_POOL.count(b, "hb"))
            dve.wait_ge(C_PE.sem, C_PE.count(b, f"c{j}"))
            dve.tensor_tensor(hb[:, j, :], CB[:, :], hb[:, j, :], ALU.add).then_inc(C_DVE.sem, 1)

        def c_act(act, b, h):
            if later(b):
                act.wait_ge(C_DVE.sem, C_DVE.count(b - 1, "aol_b"))
            if later(b):
                act.wait_ge(C_PE.sem, C_PE.count(b - 1, "c1"))
            act.wait_ge(A_PE.sem, A_PE.count(b, f"o{AH // 2 * (h + 1) - 1}"))
            for dst in (aot[:, 2 * h:2 * h + 2, :], aoh[:, 2 * h:2 * h + 2, :]):
                act.activation(dst, OB[h][:, :].rearrange("p (c t) -> p c t", c=2), ACT.Copy).then_inc(C_ACT.sem, 1)

        def c_pool(pool, b):
            pool.wait_ge(hb_in, 16 * b + 16)
            pool.tensor_tensor(hb[:, :, :], hb[:, :, :], rows[:, 1, :].unsqueeze(1).broadcast_to([128, TJ, E]), ALU.add)\
                .then_inc(C_POOL.sem, 1)

        B_SLOTS = {
            0: [("L_v", 0, 1, 0), ("L_v", 0, 1, 1), ("C_low", -1, 1), ("C_hb", -1)], 1: [("L_v", 0, 0, 0)],
            2: [("L_v", 0, 0, 1)], 3: [("L_stat", 1)], 4: [("C_out", -1, 0, 0), ("L_norm", 1)],
            5: [("C_out", -1, 0, 1), ("L_cx", 1)], 6: [("L_turn", 1, 0)], 7: [("L_turn", 1, 1), ("C_out", -1, 1, 0)],
            8: [("C_out", -1, 1, 1), ("hid", -1)], 9: [("L_qk", 1, 1, 0), ("L_low", 1)],
            10: [("L_qk", 1, 1, 1), ("E_qk", 1, 1, 0)], 11: [("L_qk", 1, 0, 0)], 12: [("L_qk", 1, 0, 1), ("E_qk", 1, 0, 0)],
            13: [("L_qk", 1, 1, 2), ("C_ao", 0, 0)], 14: [("L_qk", 1, 1, 3), ("C_low", 0, 0)], 15: [("L_qk", 1, 0, 2)],
            16: [("E_qk", 1, 1, 1), ("L_mask", 1)], 17: [("L_qk", 1, 0, 3)], 18: [("E_qk", 1, 0, 1)],
            19: [("C_ao", 0, 1)],
        }

        def round_b(eng, p, i, lag):
            def do(name, ahead, *more):
                b = i + ahead
                if name in p and (not isinstance(b, int) or 0 <= b < B):
                    p[name](eng, b, *more)

            do("hc", 1)
            do("hb", -1)
            for slot in range(AH + OUT + lag):
                if slot < AH + OUT:
                    do("A", 0, slot)
                for name, ahead, *more in B_SLOTS.get(slot - lag, ()):
                    do(name, ahead, *more)

        def phase_b(eng, p, lag=0):
            def do(name, b, *more):
                if name in p:
                    p[name](eng, b, *more)

            if "split" in p:
                p["split"](eng, 0)
            for name, *more in (("L_stat",), ("L_norm",), ("L_cx",), ("L_turn", 0), ("L_turn", 1), ("L_low",), ("need",),
                                ("L_qk", 1, 0), ("L_qk", 1, 1),
                                ("E_qk", 1, 0), ("L_qk", 0, 0), ("L_qk", 0, 1), ("E_qk", 0, 0), ("L_qk", 1, 2),
                                ("L_qk", 1, 3), ("E_qk", 1, 1), ("L_qk", 0, 2), ("L_qk", 0, 3), ("E_qk", 0, 1), ("L_mask",)):
                do(name, 0, *more)
            for name in ("split", "need"):
                do(name, 1)
            round_b(eng, p, 0, lag)
            round_b(eng, p, 1, lag)
            with eng.Fori(2, B - 1) as i:
                round_b(eng, p, i, lag)
            round_b(eng, p, B - 1, lag)
            for name, *more in (("hb",), ("C_low", 1), ("C_hb",), ("C_out", 0, 0), ("C_out", 0, 1),
                                ("C_out", 1, 0), ("C_out", 1, 1), ("hid",)):
                do(name, B - 1, *more)

        b_done = [V_PE, V_DVE, L_PE, L_ACT, L_DVE, L_POOL, A_PE, A_ACT, A_DVE, C_PE, C_DVE, C_ACT, C_POOL]

        def end_b(eng):
            for s in b_done:
                eng.wait_ge(s.sem, B * s.per)
            eng.wait_ge(hid_out, 16 * B)

        cb.close()
        cc = ctx.enter_context(ExitStack())
        WMH = sb(cc, "WMH", [128, 8, EC, E], F32R)
        WML = sb(cc, "WML", [128, 8, EC, E], F32R)
        vm = sb(cc, "vm", [128, len(VM), EC])
        fcb = sb(cc, "fcb", [128, FC])
        pbias = sb(cc, "pbias", [128, E])
        mhalf_m = sb(cc, "mhalf_m", [128, TJ])
        hm = sb(cc, "hm", [128, TJ, E])
        mstat = sb(cc, "mstat", [128, TJ, 6])
        mmv = sb(cc, "mmv", [128, TJ, 2])
        mve = sb(cc, "mve", [128, TJ])
        mrstd = sb(cc, "mrstd", [128, TJ])
        y = sb(cc, "y", [128, EC, T])
        yh = sb(cc, "yh", [128, EC, T], F32R)
        yl = sb(cc, "yl", [128, EC, T], F32R)
        RING = 3
        gl = sb(cc, "gl", [128, 2, T])
        glh = sb(cc, "glh", [128, RING, T], F32R)
        gll = sb(cc, "gll", [128, RING, T], F32R)
        hp = sb(cc, "hp", [128, TJ, E])
        RAW_AT = (4, 5, 0, 1, 2, 3, 4, 5)
        c_in = sem("c_in")
        quarter6_in = sem("quarter6_in")
        quarter7_in = sem("quarter7_in")
        m_const = sem("m_const")
        hm_in = sem("hm_in")
        hp_in = sem("hp_in")
        stored = sem("stored")
        msplit_hi = sem("msplit_hi")
        msplit_lo = sem("msplit_lo")
        fs = range(FC)
        M_PE = steps("M_PE", ["turn_a", "turn_b"])
        M_ACT = steps("M_ACT", [f"y{c}" for c in cs])
        M_DVE = steps("M_DVE", ["stat", "mean", "norm"])
        M_POOL = steps("M_POOL", ["eps", "rstd"])
        Y_ACT = steps("Y_ACT", ["high"])
        Y_DVE = steps("Y_DVE", ["low"])
        F_PE = steps("F_PE", [f"f{c}" for c in fs])
        F_ACT = steps("F_ACT", [f"g{c}" for c in fs])
        F_DVE = steps("F_DVE", [f"{n}{c}" for c in fs for n in ("high", "low")])
        O_PE = steps("O_PE", [f"o{c}" for c in fs])
        O_DVE = steps("O_DVE", ["out0", "out1"])
        O_POOL = steps("O_POOL", ["hp"])
        MB, FB, PRB = banks[0:2], banks[2:5], banks[5:7]
        OLAG = 2
        NB = len(FB)

        def sp_hm(sp, b):
            if later(b):
                sp.wait_ge(M_PE.sem, M_PE.count(b - 1, "turn_b"))
            sp.dma_start(hm[:, :, :], scratch2[b].rearrange("(j p) e -> p j e", p=128)).then_inc(hm_in, 16)

        def m_dve_stat(dve, b):
            dve.wait_ge(hm_in, 16 * b + 16)
            if later(b):
                dve.wait_ge(M_DVE.sem, M_DVE.count(b - 1, "mean"))
            for j in range(TJ):
                last = dve.bn_stats(mstat[:, j, :], hm[:, j, :])
            last.then_inc(M_DVE.sem, 1)
            dve.wait_ge(M_DVE.sem, M_DVE.count(b, "stat"))
            if later(b):
                dve.wait_ge(M_POOL.sem, M_POOL.count(b - 1, "eps"))
            alone(dve, passed)
            for j in range(TJ):
                last = dve.bn_aggr(mmv[:, j, :], mstat[:, j, :])
            last.then_inc(M_DVE.sem, 1)

        def m_pool(pool, b):
            if later(b):
                pool.wait_ge(M_DVE.sem, M_DVE.count(b - 1, "norm"))
            pool.wait_ge(M_DVE.sem, M_DVE.count(b, "mean"))
            alone(pool, passed)
            pool.tensor_scalar(mve[:, :], mmv[:, :, 1], 1.0, EPS, ALU.mult, ALU.add).then_inc(M_POOL.sem, 1)
            pool.wait_ge(M_POOL.sem, M_POOL.count(b, "eps"))
            pool.tensor_tensor(mrstd[:, :], mve[:, :], mhalf_m[:, :], ALU.pow).then_inc(M_POOL.sem, 1)

        def m_dve_norm(dve, b):
            dve.wait_ge(M_DVE.sem, M_DVE.count(b, "mean"))
            dve.wait_ge(M_POOL.sem, M_POOL.count(b, "rstd"))
            for j in range(TJ):
                last = dve.tensor_scalar(hm[:, j, :], hm[:, j, :], mmv[:, j, 0:1], mrstd[:, j:j + 1],
                                         ALU.subtract, ALU.mult)
            last.then_inc(M_DVE.sem, 1)

        def m_pe(pe, b):
            pe.wait_ge(M_DVE.sem, M_DVE.count(b, "norm"))
            if later(b):
                pe.wait_ge(M_ACT.sem, M_ACT.count(b - 1, "y3"))
            for h in range(2):
                for c in (2 * h, 2 * h + 1):
                    for j in range(TJ):
                        o = (c % 2) * T + j * 128
                        last = pe.transpose(MB[h][:, o:o + 128], hm[:, j, c * 128:(c + 1) * 128], idn[:, :])
                last.then_inc(M_PE.sem, 1)

        def m_act(act, b):
            if later(b):
                act.wait_ge(Y_DVE.sem, Y_DVE.count(b - 1, "low"))
            for c in cs:
                act.wait_ge(M_PE.sem, M_PE.count(b, f"turn_{halves[c // 2]}"))
                act.activation(y[:, c, :], MB[c // 2][:, (c % 2) * T:(c % 2 + 1) * T], ACT.Identity,
                               bias=vm[:, 1, c:c + 1], scale=vm[:, 0, c:c + 1]).then_inc(M_ACT.sem, 1)

        def y_act(act, b):
            act.wait_ge(M_ACT.sem, M_ACT.count(b, "y3"))
            if later(b):
                act.wait_ge(F_PE.sem, F_PE.count(b - 1, f"f{FC - 1}"))
            act.activation(yh[:, :, :], y[:, :, :], ACT.Copy).then_inc(Y_ACT.sem, 1)

        def y_dve(dve, b):
            dve.wait_ge(Y_ACT.sem, Y_ACT.count(b, "high"))
            dve.tensor_tensor(yl[:, :, :], y[:, :, :], yh[:, :, :].bitcast(F32), ALU.subtract).then_inc(Y_DVE.sem, 1)

        def f_pe(pe, b, c):
            if c == 0:
                pe.wait_ge(Y_DVE.sem, Y_DVE.count(b, "low"))
            if c >= NB:
                pe.wait_ge(F_ACT.sem, F_ACT.count(b, f"g{c - NB}"))
            else:
                if later(b):
                    pe.wait_ge(F_ACT.sem, F_ACT.count(b - 1, f"g{FC - 1}"))
            q, wc = c // 4, slice((c % 4) * 128, (c % 4 + 1) * 128)
            for i in cs:
                last = thirds(pe, FB[c % NB][:, 0:T], WMH[:, q, i, wc], WML[:, q, i, wc], yh[:, i, :], yl[:, i, :],
                              i == 0, i == EC - 1)
            last.then_inc(F_PE.sem, 1)

        def f_act(act, b, c):
            if c >= 2:
                act.wait_ge(F_DVE.sem, F_DVE.count(b, f"low{c - 2}"))
            else:
                if later(b):
                    act.wait_ge(F_DVE.sem, F_DVE.count(b - 1, f"low{FC - 2 + c}"))
            act.wait_ge(F_PE.sem, F_PE.count(b, f"f{c}"))
            act.activation(gl[:, c % 2, :], FB[c % NB][:, 0:T], ACT.Gelu_apprx_tanh, bias=fcb[:, c:c + 1])\
               .then_inc(F_ACT.sem, 1)

        def f_dve(dve, b, c):
            dve.wait_ge(F_ACT.sem, F_ACT.count(b, f"g{c}"))
            if c >= RING:
                dve.wait_ge(O_PE.sem, O_PE.count(b, f"o{c - RING}"))
            else:
                if later(b):
                    dve.wait_ge(O_PE.sem, O_PE.count(b - 1, f"o{FC - 1}"))
            dve.tensor_copy(glh[:, c % RING, :], gl[:, c % 2, :]).then_inc(F_DVE.sem, 1)
            dve.wait_ge(F_DVE.sem, F_DVE.count(b, f"high{c}"))
            dve.tensor_tensor(gll[:, c % RING, :], gl[:, c % 2, :], glh[:, c % RING, :].bitcast(F32), ALU.subtract)\
               .then_inc(F_DVE.sem, 1)

        def o_pe(pe, b, c):
            if c == 0:
                if later(b):
                    pe.wait_ge(O_DVE.sem, O_DVE.count(b - 1, "out1"))
            pe.wait_ge(F_DVE.sem, F_DVE.count(b, f"low{c}"))
            for j in range(TJ):
                tok = slice(j * 128, (j + 1) * 128)
                last = thirds(pe, PRB[j][:, :], glh[:, c % RING, tok], gll[:, c % RING, tok], WMH[:, 4 + c // 4, c % 4, :],
                              WML[:, 4 + c // 4, c % 4, :], c == 0, c == FC - 1)
            last.then_inc(O_PE.sem, 1)

        def o_pool(pool, b):
            pool.wait_ge(hp_in, 16 * b + 16)
            pool.tensor_tensor(hp[:, :, :], hp[:, :, :], pbias[:, :].unsqueeze(1).broadcast_to([128, TJ, E]), ALU.add)\
                .then_inc(O_POOL.sem, 1)

        def o_dve(dve, b):
            dve.wait_ge(O_PE.sem, O_PE.count(b, f"o{FC - 1}"))
            dve.wait_ge(O_POOL.sem, O_POOL.count(b, "hp"))
            for j in range(TJ):
                dve.tensor_tensor(hp[:, j, :], PRB[j][:, :], hp[:, j, :], ALU.add).then_inc(O_DVE.sem, 1)

        def sp_hp(sp, b):
            if later(b):
                sp.wait_ge(stored, 16 * b)
            sp.dma_start(hp[:, :, :], scratch2[b].rearrange("(j p) e -> p j e", p=128)).then_inc(hp_in, 16)

        def sp_out(sp, b):
            sp.wait_ge(O_DVE.sem, O_DVE.count(b, "out1"))
            sp.dma_start(out[b].rearrange("(j p) e -> p j e", p=128), hp[:, :, :]).then_inc(stored, 16)

        C_SLOTS = {0: [("hp", 0)], 1: [("hm", 1)], 5: [("M_stat", 1)], 7: [("M_norm", 1)], 9: [("M_turn", 1)]}

        PARTS = (0, 4, 1, 5, 2, 6, 3, 7)

        def sp_part(sp, k):
            if k == 2:
                sp.wait_ge(msplit_lo, 1)
                sp.dma_start(*loads_m[6]).then_inc(quarter6_in, 16)
            elif k == 3:
                sp.wait_ge(msplit_lo, 3)
                sp.dma_start(*loads_m[7]).then_inc(quarter7_in, 16)

        def act_part(act, k):
            if PARTS[k] == 6:
                act.wait_ge(quarter6_in, 16)
            elif PARTS[k] == 7:
                act.wait_ge(quarter7_in, 16)
            act.activation(WMH[:, PARTS[k]], W[:, RAW_AT[PARTS[k]]], ACT.Copy).then_inc(msplit_hi, 1)

        def dve_part(dve, k):
            n = PARTS[k]
            dve.wait_ge(msplit_hi, k + 1)
            dve.tensor_tensor(WML[:, n], W[:, RAW_AT[n]], WMH[:, n].bitcast(F32), ALU.subtract).then_inc(msplit_lo, 1)

        def pe_need(pe, k):
            pe.wait_ge(msplit_lo, k + 1)

        def round_c(eng, p, i):
            def do(name, ahead, *more):
                b = i + ahead
                if name in p and (not isinstance(b, int) or 0 <= b < B):
                    p[name](eng, b, *more)

            for c in fs:
                if isinstance(i, int) and i == 0:
                    if c % 2 and c < 12 and "part" in p:
                        p["part"](eng, (c + 3) // 2)
                    if c % 2 == 0 and c >= 4 and "need" in p:
                        p["need"](eng, c // 2)
                do("F", 0, c)
                if c >= OLAG:
                    do("O", 0, c - OLAG)
                for name, ahead in C_SLOTS.get(c, ()):
                    do(name, ahead)
            do("Y", 1)
            for c in range(FC - OLAG, FC):
                do("O", 0, c)
            do("out", 0)

        def phase_c(eng, p):
            for name, n in (("hm", 0), ("part", 0), ("M_stat", 0), ("M_norm", 0), ("part", 1), ("M_turn", 0), ("Y", 0),
                            ("need", 1)):
                if name in p:
                    p[name](eng, n)
            round_c(eng, p, 0)
            with eng.Fori(1, B - 1) as i:
                round_c(eng, p, i)
            round_c(eng, p, B - 1)

        block = ctx.enter_context(nc.Block())
        loads_mix = [(seli32, sel_in), (va[:, :, :], vec_a), (idn[:, :], ident),
                     (m1[:, :, :], maa1.rearrange("(c p) n -> p c n", p=128)), (m2[:, :], maa2), (m2b[:, :], maa2b)]
        loads_proj = [(W[:, n, :, :], w_a[n].rearrange("(c p) e -> p c e", p=128)) for n in (WK, WV, WR)]
        loads_proj += [(d1[:, :, :], dec1.rearrange("(c p) n -> p c n", p=128)), (d2[:, :], dec2)]
        loads_a = [(blk[:, :, :], blocks), (selo[:, :, :], sel_out)]
        loads_a += [(W[:, n, :, :] if n < FWR else Wf[:, n - FWR, :, :], w_a[n].rearrange("(c p) e -> p c e", p=128))
                    for n in (WG, WO, FWK, FWR, FWV)] + [(vb[:, :, :], vec_b)]
        loads_q = [(W[:, n, :, :], w_b[n].rearrange("(c p) e -> p c e", p=128)) for n in range(4)]
        loads_b = [(rows[:, n, :], rows_b[n].partition_broadcast(128)) for n in range(2)]
        loads_m = [(W[:, RAW_AT[n], :, :], w_b[4 + n].rearrange("(c p) e -> p c e", p=128)) for n in range(8)]
        loads_c = [(vm[:, :, :], vec_m), (fcb[:, :], fc_b), (pbias[:, :], rows_b[2].partition_broadcast(128))]

        def sp_first_b(sp, b):
            sp.wait_ge(G_PE.sem, G_PE.count(b, "gb"))
            for dst, src in loads_q:
                sp.dma_start(dst, src).then_inc(q_in, 16)

        def sp_loads(sp, b):
            if b == 0:
                for dst, src in loads_proj:
                    sp.dma_start(dst, src).then_inc(proj_in, 16)
                for dst, src in loads_a:
                    sp.dma_start(dst, src).then_inc(weights_in, 16)

        def act_split(act, half):
            for w in QKVO[2 * half:2 * half + 2]:
                act.activation(WQH[:, w], W[:, w], ACT.Copy).then_inc(split_hi, 1)

        def dve_split(dve, half):
            for n in (2 * half, 2 * half + 1):
                dve.wait_ge(split_hi, n + 1)
                dve.tensor_tensor(WQL[:, QKVO[n]], W[:, QKVO[n]], WQH[:, QKVO[n]].bitcast(F32), ALU.subtract)\
                   .then_inc(split_lo, 1)
            if half:
                dve.wait_ge(b_in1, 16 * len(loads_b))

        def pe_split(pe, half):
            pe.wait_ge(split_lo, 2 * half + 2)

        def wait_proj(eng, b):
            eng.wait_ge(proj_in, 16 * len(loads_proj))

        def wait_weights(eng, b):
            eng.wait_ge(weights_in, 16 * len(loads_a))

        @block.sync
        def _(sp):
            for dst, src in loads_mix:
                sp.dma_start(dst, src).then_inc(mix_in, 16)
            phase_a(sp, {"x": sp_x, "loads": sp_loads, "s0": sp_s0, "x1": sp_x1, "save": sp_save, "first_b": sp_first_b})
            end_a(sp)
            sp_hc(sp, 0)
            for dst, src in loads_b:
                sp.dma_start(dst, src).then_inc(b_in1, 16)
            for n, (dst, src) in enumerate(loads_m[:6]):
                if n == 2:
                    sp.wait_ge(split_lo, len(QKVO))
                sp.dma_start(dst, src).then_inc(m_in, 16)
            phase_b(sp, {"hc": sp_hc, "hb": sp_hb, "hid": sp_hid})
            end_b(sp)
            for dst, src in loads_c:
                sp.dma_start(dst, src).then_inc(c_in, 16)
            phase_c(sp, {"part": sp_part, "hm": sp_hm, "hp": sp_hp, "out": sp_out})
            sp.wait_ge(stored, 16 * B)

        @block.scalar
        def _(act):
            act.wait_ge(mix_in, 16 * len(loads_mix))
            act.wait_ge(const_ready, 4)
            phase_a(act, {"weights_in": wait_weights, "X_turn": x_act1, "X_hid": x_act_hid, "P_zk": p_act, "P_vr": p_act_vr, "G": g_act,
                          "S": s_act, "N": n_act, "k_turn": k_act1, "fk": k_act_fk, "fr": k_act_fr})
            end_a(act)
            act.wait_ge(q_in, 16 * len(loads_q))
            phase_b(act, {"split": act_split, "L_cx": l_act, "L_turn": l_act_turn, "E_qk": l_act_qk, "A": a_act, "C_ao": c_act})
            end_b(act)
            act.wait_ge(m_in, 16 * 6)
            act.wait_ge(c_in, 16 * len(loads_c))
            phase_c(act, {"part": act_part, "M_turn": m_act, "Y": y_act, "F": f_act})

        @block.vector
        def _(dve):
            dve.wait_ge(mix_in, 16 * len(loads_mix))
            dve.tensor_scalar(half_gn[:, 0:1, :], va[:, VA.index("gn_w"):VA.index("gn_w") + 1, :], 0.5, None, ALU.mult)\
               .then_inc(const_ready, 1)
            dve.tensor_scalar(half_gn[:, 1:2, :], va[:, VA.index("gn_b"):VA.index("gn_b") + 1, :], 0.5, None, ALU.mult)\
               .then_inc(const_ready, 1)
            dve.tensor_copy(seli[:, :, :], seli32).then_inc(const_ready, 1)
            dve.memset(small[:, 0:1], EPS).then_inc(const_ready, 1)
            dve.wait_ge(const_ready, 4)
            phase_a(dve, {"weights_in": wait_weights, "X_stat": x_dve1, "X_norm": x_dve_norm, "X_shift": x_dve_shift, "X_xx": x_dve_xx,
                          "X_mix": x_dve2, "P_vr": p_dve, "G_out": g_dve, "S": s_dve, "N_out": n_dve,
                          "wo": k_dve_wo, "k_stat": k_dve_stat, "k_norm": k_dve_norm, "k_shift": k_dve2, "k_xk": k_dve_xk, "k_xr": k_dve_xr,
                          "fv": k_dve_fv}, LAG)
            end_a(dve)
            phase_b(dve, {"split": dve_split, "L_stat": l_dve, "L_norm": l_dve_norm, "L_cx": l_dve_low_cx, "L_low": l_dve_low, "L_mask": l_dve_mask, "L_v": l_dve_v,
                          "A": a_dve, "C_low": c_dve_low, "C_out": c_dve_hid}, 1)
            end_b(dve)
            phase_c(dve, {"part": dve_part, "M_stat": m_dve_stat, "M_norm": m_dve_norm, "Y": y_dve, "F": f_dve, "out": o_dve})

        @block.gpsimd
        def _(pool):
            pool.memset(mhalf[:, :], -0.5).then_inc(b_const, 1)
            pool.wait_ge(b_const, 1)
            phase_a(pool, {"X_stat": x_pool1, "X_mix": x_pool2, "S": s_pool, "k_stat": k_pool}, LAG)
            end_a(pool)
            pool.memset(mhalf_b[:, :], -0.5).then_inc(b_const, 1)
            pool.wait_ge(b_const, 2)
            pool.wait_ge(b_in1, 16 * len(loads_b))
            phase_b(pool, {"L_stat": l_pool, "C_hb": c_pool})
            end_b(pool)
            pool.memset(mhalf_m[:, :], -0.5).then_inc(b_const, 1)
            pool.wait_ge(b_const, 3)
            pool.wait_ge(c_in, 16 * len(loads_c))
            phase_c(pool, {"M_stat": m_pool, "hp": o_pool})

        @block.tensor
        def _(pe):
            pe.wait_ge(mix_in, 16 * len(loads_mix))
            pe.wait_ge(const_ready, 4)
            phase_a(pe, {"proj_in": wait_proj, "weights_in": wait_weights, "X_turn": x_pe1, "X_hid": x_pe_hid, "X_mix": x_pe2, "P_zk": p_pe, "P_vr": p_pe_vr,
                         "G": g_pe, "S": s_pe, "S_begin": s_pe_begin, "N": n_pe, "wo": k_pe_wo, "k_turn": k_pe2,
                         "fk": k_pe_fk, "fr": k_pe_fr, "fv": k_pe_fv})
            end_a(pe)
            phase_b(pe, {"need": pe_split, "L_turn": l_pe, "L_qk": l_pe_qk, "L_v": l_pe_v, "A": a_pe, 
                         "C_out": c_pe_out})
            end_b(pe)
            phase_c(pe, {"need": pe_need, "M_turn": m_pe, "F": f_pe, "O": o_pe})


def kernel(**inputs):
    import numpy as np
    import concourse.bacc as bacc
    from concourse.bass_utils import run_bass_kernel_spmd

    a = {k: np.asarray(v) for k, v in inputs.items()}

    def l0(n):
        return a["L0_xattn_" + n]

    def l1(n):
        return a["L1_xattn_" + n]

    def cols(vectors):
        return np.ascontiguousarray(np.stack([v.reshape(EC, 128).T for v in vectors], axis=1))

    ctx_ = a["ctx_2048"]
    heads = np.arange(128) // S
    same = (heads[:, None] == heads[None, :]).astype(np.float32)
    index = np.arange(128) % S
    sel_in = same[:, None, :] * (index[:, None, None] == np.arange(S)[None, :, None]).astype(np.float32)
    sel_out = same[:, None, :] * ((index[None, None, :] == np.arange(S)[None, :, None]) - np.float32(1 / S)).astype(np.float32)
    arrays = {
        "x": a["x"],
        "prev1": np.ascontiguousarray(ctx_[:, 1, :].reshape(B, EC, 128).transpose(0, 2, 1)),
        "prev2": np.ascontiguousarray(ctx_[:, 0, :].reshape(B, EC, 128).transpose(0, 2, 1)),
        "s0": np.ascontiguousarray(ctx_[:, 2:2 + S, :].reshape(B, EC, 128, S).transpose(0, 2, 1, 3).reshape(B, 128, EC * S)),
        "ctxt": np.ascontiguousarray(ctx_.transpose(0, 2, 1)),
        "mask": a["mask_BxS2_bf1"].view(np.uint8),
        "vec_a": cols([l0("ln1_w"), l0("ln1_b"), l0("maa_x"), *l0("maa_stack"), l0("time_decay"),
                       l0("faaaa").reshape(E), l0("gn_w"), l0("gn_b"), l0("ln2_w"), l0("ln2_b"),
                       l0("ffn_maa_k"), l0("ffn_maa_r")]),
        "w_a": np.stack([np.ascontiguousarray(l0(n).T) for n in ("Wr", "Wk", "Wv", "Wg", "Wo", "ffn_Wk", "ffn_Wr", "ffn_Wv")]),
        "maa1": l0("maa_w1"),
        "maa2": np.ascontiguousarray(l0("maa_w2")[:4].reshape(4 * MAA, E)),
        "maa2b": np.ascontiguousarray(l0("maa_w2")[4]),
        "dec1": l0("decay_w1"),
        "dec2": l0("decay_w2"),
        "vec_b": cols([l1("ln1_w"), l1("ln1_b"), l1("q_b"), l1("k_b")]),
        "vec_m": cols([l1("ln2_w"), l1("ln2_b")]),
        "w_b": np.stack([l1("q_w"), l1("k_w"), l1("v_w"), l1("cproj_w")]
                        + [np.ascontiguousarray(l1("fc_w")[:, n * E:(n + 1) * E]) for n in range(4)]
                        + [l1("proj_w")[n * E:(n + 1) * E] for n in range(4)]),
        "fc_b": np.ascontiguousarray(l1("fc_b").reshape(FC, 128).T),
        "rows_b": np.stack([l1("v_b"), l1("cproj_b"), l1("proj_b")]),
        "ident": np.eye(128, dtype=np.float32),
        "blocks": np.ascontiguousarray(np.stack([same, np.eye(128, dtype=np.float32) - same / np.float32(S),
                                                 same / np.float32(S)], axis=1)),
        "sel_in": sel_in,
        "sel_out": sel_out,
    }
    nc = bacc.Bacc("TRN2", target_bir_lowering=False, num_devices=1)
    args = [nc.dram_tensor(f"in_{k}", v.shape, mybir.dt.from_np(v.dtype), kind="ExternalInput").ap()
            for k, v in arrays.items()]
    scratch = nc.dram_tensor("scratch", (B, T, E), F32, kind="Internal").ap()
    scratch2 = nc.dram_tensor("scratch2", (B, T, E), F32, kind="Internal").ap()
    out = nc.dram_tensor("out_0", (B, T, E), F32, kind="ExternalOutput").ap()
    build(nc, *args, scratch, scratch2, out)
    r = run_bass_kernel_spmd(nc, [{f"in_{k}": v for k, v in arrays.items()}], core_ids=[0])
    return r.results[0]["out_0"]
```
